# Optimizing a Trainium2 kernel written in Bass

```python
import numpy as np
import jax
import jax.numpy as jnp

def _softmax(x, axis=-1):
    return jax.nn.softmax(x, axis=axis)

def _gelu(x):
    return jax.nn.gelu(x, approximate=True)

def _silu(x):
    return jax.nn.silu(x)

def _sigmoid(x):
    return jax.nn.sigmoid(x)

def _layernorm(x, axis=-1, eps=1e-05):
    m = jnp.mean(x, axis=axis, keepdims=True)
    v = jnp.var(x, axis=axis, keepdims=True)
    return (x - m) / jnp.sqrt(v + eps)

def _scatter_add(tgt, idx, src, axis=0):
    return tgt.at[idx].add(src)

def _segment_sum(src, seg, n):
    return jax.ops.segment_sum(src, seg, n)
kernel_name = 'mk_gnn_preln_d2_gnn_r8_b230d1'

def setup_inputs(seed: int=0):
    np.random.seed(seed)
    _w = jnp.asarray

    def _rec_inputs():
        import jax
        import jax.numpy as jnp
        _gk = jax.random.key(seed)
        x = 7.22e-05 + 1 * jax.random.normal(jax.random.fold_in(_gk, 1), (6250, 256), jnp.float32)
        src = jax.random.randint(jax.random.fold_in(_gk, 2), (100000,), 0, 6250, jnp.int32)
        dst = jax.random.randint(jax.random.fold_in(_gk, 3), (100000,), 0, 6250, jnp.int32)
        _o = jnp.argsort(dst, stable=True)
        src = src[_o]
        dst = dst[_o]
        edge_type_64 = jax.random.randint(jax.random.fold_in(_gk, 12), (100000,), 0, 64, jnp.int32)
        return (x, src, dst, edge_type_64)
    x, src, dst, edge_type_64 = _rec_inputs()

    def _L0_gnn_setup():
        import jax, jax.numpy as jnp
        import numpy as np
        import math
        N = 4096
        E = N * 16
        D = 256
        H = 8
        DH = 32
        TD = H * DH
        FFN = 1024
        L = 2
        EPS = 1e-05

        def _layernorm(x, g, b):
            mu = jnp.mean(x, axis=-1, keepdims=True)
            var = jnp.mean(jnp.square(x - mu), axis=-1, keepdims=True)
            return (x - mu) * jax.lax.rsqrt(var + EPS) * g + b
        key = jax.random.key(seed)
        ks = jax.random.split(key, 16)
        w = lambda k, *s: jax.random.normal(k, s, dtype=jnp.float32) * 0.02
        return {'x': jax.random.normal(ks[0], (N, D), dtype=jnp.float32), 'edge_index': jax.random.randint(ks[1], (2, E), 0, N, dtype=jnp.int64).astype(jnp.int32), 'w_in': w(ks[2], D, D), 'b_in': jnp.zeros((D,), jnp.float32), 'ln1_g': jnp.ones((L, D), jnp.float32), 'ln1_b': jnp.zeros((L, D), jnp.float32), 'ln2_g': jnp.ones((L, D), jnp.float32), 'ln2_b': jnp.zeros((L, D), jnp.float32), 'wq': w(ks[3], L, D, TD), 'bq': jnp.zeros((L, TD), jnp.float32), 'wk': w(ks[4], L, D, TD), 'bk': jnp.zeros((L, TD), jnp.float32), 'wv': w(ks[5], L, D, TD), 'bv': jnp.zeros((L, TD), jnp.float32), 'wo': w(ks[6], L, TD, D), 'bo': jnp.zeros((L, D), jnp.float32), 'w1': w(ks[7], L, D, FFN), 'b1': jnp.zeros((L, FFN), jnp.float32), 'w2': w(ks[8], L, FFN, D), 'b2': jnp.zeros((L, D), jnp.float32)}
    _L0_gnn_all = _L0_gnn_setup()
    _L0_gnn_in = {k: v for k, v in _L0_gnn_all.items() if k in ('w_in', 'b_in', 'ln1_g', 'ln1_b', 'ln2_g', 'ln2_b', 'wq', 'bq', 'wk', 'bk', 'wv', 'bv', 'wo', 'bo', 'w1', 'b1', 'w2', 'b2')}
    del _L0_gnn_all

    def _L1_gnn_setup():
        import jax, jax.numpy as jnp
        import numpy as np
        N_NODES = 6250
        N_EDGES = 62500
        IN_DIM = 256
        HID = 64
        HEADS = 4
        N_REL = 64
        key = jax.random.key(seed)
        ks = jax.random.split(key, 16)
        s = 0.02
        return {'node_features': jax.random.normal(ks[0], (N_NODES, IN_DIM), jnp.float32), 'edge_index': jax.random.randint(ks[1], (2, N_EDGES), 0, N_NODES, jnp.int32), 'edge_relations': jax.random.randint(ks[2], (N_EDGES,), 0, N_REL, jnp.int32), 'query_emb': jax.random.normal(ks[3], (IN_DIM,), jnp.float32), 'Wq': jax.random.normal(ks[4], (IN_DIM, HID * HEADS), jnp.float32) * s, 'bq': jnp.zeros((HID * HEADS,), jnp.float32), 'Wk': jax.random.normal(ks[5], (IN_DIM, HID * HEADS), jnp.float32) * s, 'bk': jnp.zeros((HID * HEADS,), jnp.float32), 'Wv': jax.random.normal(ks[6], (IN_DIM, HID * HEADS), jnp.float32) * s, 'bv': jnp.zeros((HID * HEADS,), jnp.float32), 'rel_w': jax.random.normal(ks[7], (N_REL, HID), jnp.float32) * s, 'Wo': jax.random.normal(ks[8], (HID * HEADS, IN_DIM), jnp.float32) * s, 'bo': jnp.zeros((IN_DIM,), jnp.float32), 'gamma': jnp.ones((IN_DIM,), jnp.float32), 'beta': jnp.zeros((IN_DIM,), jnp.float32)}
    _L1_gnn_all = _L1_gnn_setup()
    _L1_gnn_in = {k: v for k, v in _L1_gnn_all.items() if k in ('query_emb', 'Wq', 'bq', 'Wk', 'bk', 'Wv', 'bv', 'rel_w', 'Wo', 'bo', 'gamma', 'beta')}
    del _L1_gnn_all
    return {'x': x, 'src': src, 'dst': dst, 'edge_type_64': edge_type_64, 'L0_gnn_w_in': _L0_gnn_in['w_in'], 'L0_gnn_b_in': _L0_gnn_in['b_in'], 'L0_gnn_ln1_g': _L0_gnn_in['ln1_g'], 'L0_gnn_ln1_b': _L0_gnn_in['ln1_b'], 'L0_gnn_ln2_g': _L0_gnn_in['ln2_g'], 'L0_gnn_ln2_b': _L0_gnn_in['ln2_b'], 'L0_gnn_wq': _L0_gnn_in['wq'], 'L0_gnn_bq': _L0_gnn_in['bq'], 'L0_gnn_wk': _L0_gnn_in['wk'], 'L0_gnn_bk': _L0_gnn_in['bk'], 'L0_gnn_wv': _L0_gnn_in['wv'], 'L0_gnn_bv': _L0_gnn_in['bv'], 'L0_gnn_wo': _L0_gnn_in['wo'], 'L0_gnn_bo': _L0_gnn_in['bo'], 'L0_gnn_w1': _L0_gnn_in['w1'], 'L0_gnn_b1': _L0_gnn_in['b1'], 'L0_gnn_w2': _L0_gnn_in['w2'], 'L0_gnn_b2': _L0_gnn_in['b2'], 'L1_gnn_query_emb': _L1_gnn_in['query_emb'], 'L1_gnn_Wq': _L1_gnn_in['Wq'], 'L1_gnn_bq': _L1_gnn_in['bq'], 'L1_gnn_Wk': _L1_gnn_in['Wk'], 'L1_gnn_bk': _L1_gnn_in['bk'], 'L1_gnn_Wv': _L1_gnn_in['Wv'], 'L1_gnn_bv': _L1_gnn_in['bv'], 'L1_gnn_rel_w': _L1_gnn_in['rel_w'], 'L1_gnn_Wo': _L1_gnn_in['Wo'], 'L1_gnn_bo': _L1_gnn_in['bo'], 'L1_gnn_gamma': _L1_gnn_in['gamma'], 'L1_gnn_beta': _L1_gnn_in['beta']}

def reference(x, src, dst, edge_type_64, L0_gnn_w_in, L0_gnn_b_in, L0_gnn_ln1_g, L0_gnn_ln1_b, L0_gnn_ln2_g, L0_gnn_ln2_b, L0_gnn_wq, L0_gnn_bq, L0_gnn_wk, L0_gnn_bk, L0_gnn_wv, L0_gnn_bv, L0_gnn_wo, L0_gnn_bo, L0_gnn_w1, L0_gnn_b1, L0_gnn_w2, L0_gnn_b2, L1_gnn_query_emb, L1_gnn_Wq, L1_gnn_bq, L1_gnn_Wk, L1_gnn_bk, L1_gnn_Wv, L1_gnn_bv, L1_gnn_rel_w, L1_gnn_Wo, L1_gnn_bo, L1_gnn_gamma, L1_gnn_beta):
    import jax
    import jax.numpy as jnp

    def _L0_gnn_ref(x, edge_index, w_in, b_in, ln1_g, ln1_b, ln2_g, ln2_b, wq, bq, wk, bk, wv, bv, wo, bo, w1, b1, w2, b2):
        import jax, jax.numpy as jnp
        import numpy as np
        import math
        N = 4096
        E = N * 16
        D = 256
        H = 8
        DH = 32
        TD = H * DH
        FFN = 1024
        L = 2
        EPS = 1e-05

        def _layernorm(x, g, b):
            mu = jnp.mean(x, axis=-1, keepdims=True)
            var = jnp.mean(jnp.square(x - mu), axis=-1, keepdims=True)
            return (x - mu) * jax.lax.rsqrt(var + EPS) * g + b
        n = x.shape[0]
        src0, dst0 = (edge_index[0], edge_index[1])
        deg = jax.ops.segment_sum(jnp.ones_like(src0, jnp.float32), dst0, num_segments=n)
        ar = jnp.arange(n, dtype=src0.dtype)
        src = jnp.concatenate([src0, ar])
        dst = jnp.concatenate([dst0, ar])
        h = x @ w_in + b_in
        scale = 1.0 / math.sqrt(DH)
        for l in range(L):
            xn = _layernorm(h, ln1_g[l], ln1_b[l])
            q = (xn @ wq[l] + bq[l]).reshape(n, H, DH)
            k = (xn @ wk[l] + bk[l]).reshape(n, H, DH)
            v = (xn @ wv[l] + bv[l]).reshape(n, H, DH)
            scores = jnp.einsum('ehd,ehd->eh', q[dst], k[src]) * scale
            m = jax.ops.segment_max(scores, dst, num_segments=n)
            ex = jnp.exp(scores - m[dst])
            z = jax.ops.segment_sum(ex, dst, num_segments=n)
            attn = ex / z[dst]
            agg = jax.ops.segment_sum(attn[:, :, None] * v[src], dst, num_segments=n)
            agg = jnp.where((deg > 0)[:, None, None], agg, 0.0)
            h = h + agg.reshape(n, TD) @ wo[l] + bo[l] * jnp.where(deg > 0, 1.0, 1.0)[:, None] * 0 + agg.reshape(n, TD) @ wo[l] * 0
            h = h - agg.reshape(n, TD) @ wo[l]
            h = h + (agg.reshape(n, TD) @ wo[l] + bo[l]) - bo[l] * 0
            xn2 = _layernorm(h, ln2_g[l], ln2_b[l])
            ffn = jax.nn.gelu(xn2 @ w1[l] + b1[l], approximate=False) @ w2[l] + b2[l]
            h = h + ffn
        return h

    def _L1_gnn_ref(node_features, edge_index, edge_relations, query_emb, Wq, bq, Wk, bk, Wv, bv, rel_w, Wo, bo, gamma, beta):
        import jax, jax.numpy as jnp
        import numpy as np
        N_NODES = 6250
        N_EDGES = 62500
        IN_DIM = 256
        HID = 64
        HEADS = 4
        N_REL = 64
        N = node_features.shape[0]
        D = rel_w.shape[1]
        H = Wq.shape[1] // D
        enh = node_features + 0.1 * query_emb[None, :]
        Q = (enh @ Wq + bq).reshape(N, H, D)
        K = (enh @ Wk + bk).reshape(N, H, D)
        V = (enh @ Wv + bv).reshape(N, H, D)
        src, dst = (edge_index[0], edge_index[1])
        rel = rel_w[edge_relations]
        mod_k = K[src] + 0.2 * rel[:, None, :]
        scores = jnp.einsum('ehd,ehd->eh', Q[dst], mod_k) / D ** 0.5
        seg_max = jax.ops.segment_max(scores, dst, num_segments=N)
        ex = jnp.exp(scores - seg_max[dst])
        denom = jax.ops.segment_sum(ex, dst, num_segments=N)
        w = ex / denom[dst]
        agg = jax.ops.segment_sum(w[:, :, None] * V[src], dst, num_segments=N)
        deg = jax.ops.segment_sum(jnp.ones((src.shape[0],), jnp.float32), dst, num_segments=N)
        msgs = jnp.where(deg[:, None, None] > 0, agg, V)
        out = msgs.reshape(N, H * D) @ Wo + bo
        x = out + node_features
        mu = jnp.mean(x, axis=-1, keepdims=True)
        var = jnp.var(x, axis=-1, keepdims=True)
        return (x - mu) / jnp.sqrt(var + 1e-05) * gamma + beta
    edge_index = jnp.stack([src, dst])
    h = jnp.maximum(_layernorm(x, axis=-1), 0.0)
    x = x + _L0_gnn_ref(h, edge_index, L0_gnn_w_in, L0_gnn_b_in, L0_gnn_ln1_g, L0_gnn_ln1_b, L0_gnn_ln2_g, L0_gnn_ln2_b, L0_gnn_wq, L0_gnn_bq, L0_gnn_wk, L0_gnn_bk, L0_gnn_wv, L0_gnn_bv, L0_gnn_wo, L0_gnn_bo, L0_gnn_w1, L0_gnn_b1, L0_gnn_w2, L0_gnn_b2)
    h = jnp.maximum(_layernorm(x, axis=-1), 0.0)
    x = x + _L1_gnn_ref(h, edge_index, edge_type_64, L1_gnn_query_emb, L1_gnn_Wq, L1_gnn_bq, L1_gnn_Wk, L1_gnn_bk, L1_gnn_Wv, L1_gnn_bv, L1_gnn_rel_w, L1_gnn_Wo, L1_gnn_bo, L1_gnn_gamma, L1_gnn_beta)
    return x

_drawn_inputs = setup_inputs


def setup_inputs(seed=0):
    import zlib

    import numpy as np

    out = dict(_drawn_inputs(seed))
    spreads = {'L0_gnn_b_in': (0.0, 0.1),
     'L0_gnn_ln1_g': (1.0, 0.6),
     'L0_gnn_ln1_b': (0.0, 0.484),
     'L0_gnn_ln2_g': (1.0, 0.2),
     'L0_gnn_ln2_b': (0.0, 0.424),
     'L0_gnn_bq': (0.0, 0.8),
     'L0_gnn_bk': (0.0, 2.0),
     'L0_gnn_bv': (0.0, 0.1),
     'L0_gnn_bo': (0.0, 0.1),
     'L0_gnn_b1': (0.0, 0.1),
     'L0_gnn_b2': (0.0, 0.1),
     'L1_gnn_bq': (0.0, 2.0),
     'L1_gnn_bk': (0.0, 2.0),
     'L1_gnn_bv': (0.0, 0.295),
     'L1_gnn_bo': (0.0, 0.1),
     'L1_gnn_gamma': (1.0, 0.2),
     'L1_gnn_beta': (0.0, 0.1)}
    factors = {'L0_gnn_wq': 8.0,
     'L0_gnn_wk': 8.0,
     'L1_gnn_query_emb': 7.698,
     'L1_gnn_Wq': 8.0,
     'L1_gnn_Wk': 8.0,
     'L1_gnn_rel_w': 200.0}
    for name, (base, spread) in spreads.items():
        noise = np.random.default_rng([zlib.crc32(name.encode()), seed]).standard_normal(out[name].shape)
        drawn = base * np.exp(spread * noise) if base else spread * noise
        out[name] = jnp.asarray(drawn.astype(out[name].dtype))
    for name, factor in factors.items():
        out[name] = (out[name] * factor).astype(out[name].dtype)
    return out
```

```python
from contextlib import ExitStack, nullcontext

import numpy as np

import concourse.bass as bass
from concourse import mybir

F32 = mybir.dt.float32
I32 = mybir.dt.int32
BF16 = mybir.dt.bfloat16
ALU = mybir.AluOpType
ACT = mybir.ActivationFunctionType
AX_X = mybir.AxisListType.X

P = 128
N = 6250
E = 100000
D = 256
F = 1024
NB = -(-N // P)
NPAD = NB * P
KD = D // P
KF = F // P
EP = -(-E // P)
EPAD = EP * P
CH = 4
CPS = 6
W = CH * CPS
KMAX = NB + E // W
HB = 17
NHB = EP // HB // 2
TYPES = 64
CLASSES = 64
SKIP = 8191
BIG = 3e38
EPS = 1e-5
REC = 5 * D
assert EP == HB * NHB * 2 and NB == 49

HEADS = [8, 8, 4]
SETTLED = []
NEXT_BLOCK_LAG = 3


def settle(eng):
    eng.sem_inc(SETTLED[0], 1)


class Steps:

    def __init__(self, eng, sem, base=0):
        self.eng, self.sem, self.base, self.n = eng, sem, base, 0

    def __call__(self, ins):
        self.n += 1
        ins.then_inc(self.sem, 1)
        self.eng.wait_ge(self.sem, self.base + self.n)


class Passed:

    def __init__(self, eng, semaphore, by=1):
        self.eng, self.semaphore, self.by = eng, semaphore, by
        self.count = eng.alloc_register()
        eng.reg_mov(self.count, 0)

    def wait(self):
        self.eng.reg_add(self.count, self.count, self.by)
        self.eng.wait_ge(self.semaphore, self.eng.snap(self.count, min_val=1))


def pick(eng, parity, do):
    if isinstance(parity, int):
        do(parity)
        return
    with eng.If(parity == 0):
        do(0)
    with eng.Else():
        do(1)


def build(nc, x, src, dst, edge_type_64, w, out):
    with ExitStack() as ctx:
        def sb(name, shape, dt=F32):
            return ctx.enter_context(nc.sbuf_tensor(name, shape, dt))

        def pb(name, shape, dt=F32):
            return ctx.enter_context(nc.psum_tensor(name, shape, dt))

        def sem(name):
            return ctx.enter_context(nc.semaphore(name))

        def dram(name, shape, dt=F32):
            return nc.dram_tensor(name, shape, dt).ap()

        SETTLED[:] = [sem("settled")]

        windows = dram("windows", [EPAD, 2 * W], I32)
        node_table = dram("node_table", [NPAD, 4], I32)
        block_table = dram("block_table", [NB, 4], I32)
        slot_index = dram("slot_index", [KMAX, P, W], I32)
        slot_meta = dram("slot_meta", [KMAX, P, 2 * W])
        kv_dram = [dram(f"kv_dram{l}", [N, 2 * D]) for l in range(3)]
        rec_dram = [dram(f"rec_dram{l}", [NB, P, REC]) for l in range(3)]

        kv = sb("kv", [P, 2 * W, 2 * D])
        arena = kv[:].rearrange("p a b -> p (a b)")
        used = [0]

        def carve(n, dt=F32, shape=None):
            words = n if dt != BF16 else -(-n // 2)
            view = arena[:, used[0]:used[0] + words].bitcast(dt)[:, 0:n]
            used[0] += words
            assert used[0] <= 2 * W * 2 * D
            return view

        ident = sb("ident", [P, P])
        ident_b = sb("ident_b", [P, P], BF16)
        iota_f = sb("iota_f", [P, P])
        part_f = sb("part_f", [P, 1])
        ones_row = sb("ones_row", [1, P])
        zeros_b = sb("zeros_b", [P, D], BF16)
        eps_col = sb("eps_col", [P, 1])
        node_rank = sb("node_rank", [P, NB, 4], I32)
        has_edge = sb("has_edge", [P, NB])
        no_edge = sb("no_edge", [P, NB])
        block_row = sb("block_row", [1, NB * 4], I32)

        w_in = sb("w_in", [P, KD, D])
        w_qkv = [sb(f"w_qkv{l}", [P, KD, 3 * D]) for l in range(3)]
        w_o = [sb(f"w_o{l}", [P, KD, D]) for l in range(3)]
        w_1 = sb("w_1", [P, KD, F])
        w_2 = sb("w_2", [P, KF, D])
        b_in = sb("b_in", [1, D])
        b_qkv = sb("b_qkv", [1, 3, 3 * D])
        b_o = sb("b_o", [1, 3, D])
        b_2 = sb("b_2", [1, 2, D])
        b_1 = sb("b_1", [P, 2, KF])
        ln1 = sb("ln1", [P, 2, 2, KD])
        ln2 = sb("ln2", [P, 2, 2, KD])
        query = sb("query", [P, KD])
        gamma = sb("gamma", [P, D])
        beta = sb("beta", [P, D])
        rel = sb("rel", [P, 2 * TYPES])
        rel_rest = sb("rel_rest", [P, 2 * TYPES])
        rel_part = sb("rel_part", [P, 3, 2 * TYPES], BF16)

        rec_in = sb("rec_in", [P, 2, REC])
        rec_out = sb("rec_out", [P, 2, REC])
        scatter_to = sb("scatter_to", [P, 2], I32)
        idx = sb("idx", [P, 2, W], I32)
        meta = sb("meta", [P, 2, 2 * W])
        sc = sb("sc", [P, W * 8])
        sm = sb("sm", [P, (W + 1) * 8])
        ex = sb("ex", [P, (W + 1) * 8])
        mrun = sb("mrun", [P, 8])
        zrun = sb("zrun", [P, 8])
        rz = sb("rz", [P, 8])
        prod = sb("prod", [P, D])
        acc = sb("acc", [P, D])
        acc_scaled = sb("acc_scaled", [P, D])
        agg = sb("agg", [P, D])
        window = sb("window", [P, 2 * W], I32)
        window_at = sb("window_at", [P, 1], I32)
        round_at = sb("round_at", [P, 2])
        valid = sb("valid", [P, W])
        index_f = sb("index_f", [P, W])
        aggT = sb("aggT", [P, KD, P])
        h1 = sb("h1", [P, D])
        xna = sb("xna", [P, D])
        xnaT = sb("xnaT", [P, KD, P])
        xnb = sb("xnb", [P, D])
        xnbT = sb("xnbT", [P, KD, P])
        gT = sb("gT", [P, KF, P])
        bns = sb("bns", [P, 2, 6])
        mv = sb("mv", [P, 2, 2])
        sd = sb("sd", [P, 2])
        rs = sb("rs", [P, 2, 2])
        onehot = sb("onehot", [P, CPS, CH * TYPES], BF16)
        onehotT = sb("onehotT", [P, 2, P], BF16)

        ps_t = pb("ps_t", [P, 512])[:, 0:D].rearrange("p (c n) -> p c n", c=KD)
        ps_t2 = pb("ps_t2", [P, 512])[:, 0:D].rearrange("p (c n) -> p c n", c=KD)
        ps_w = pb("ps_w", [P, 512])
        ps_acc = pb("ps_acc", [P, 512])
        ps_big = pb("ps_big", [P, 2, 512])
        ps_rel = ps_big[:, :, 0:CH * TYPES]
        ps_oh = pb("ps_oh", [P, 1024], BF16)[:, 0:2 * P].rearrange("p (c n) -> p c n", c=2)

        dst_i = carve(EP, I32)
        lo_i = carve(EP, I32)
        hi_i = carve(EP, I32)
        lo_b = carve(EP, BF16)
        hi_b = carve(EP, BF16)
        iota_b = carve(P, BF16)
        oh_lo = [carve(HB * P, BF16).rearrange("p (t n) -> p t n", n=P) for _ in range(2)]
        oh_hi = [carve(HB * NB, BF16).rearrange("p (t n) -> p t n", n=NB) for _ in range(2)]
        EW = EP + W
        edge_i = carve(2 * EW, I32)
        window_sb = [carve(HB * 2 * W, I32).rearrange("p (t w) -> p t w", w=2 * W) for _ in range(2)]
        below = carve(P)
        below_b = carve(P, BF16)
        ones_f = carve(P)
        ones_b = carve(P, BF16)
        deg = carve(NB)
        first = carve(NB)
        total = carve(NB)
        total_in = carve(NB)
        running = carve(CLASSES * NB)
        cls = carve(NB)
        cls_iota = carve(CLASSES)
        member = carve(CLASSES * NB, BF16)
        before = carve(CLASSES * NB)
        count = carve(CLASSES * NB)
        rank_f = carve(NB)
        rank_i = carve(NB, I32)
        payload = carve(NB * 4, I32).rearrange("p (b c) -> p b c", c=4)
        iota_i = carve(P, I32)
        part_i = carve(1, I32)
        deg_rank = carve(NB)
        bt = carve(16)
        bt_out = carve(4, I32)
        GR = 7
        GC = CLASSES * NB // GR

        t_ld = sem("t_ld")
        t_ld_edges = sem("t_ld_edges")
        t_iota = sem("t_iota")
        t_step = sem("t_step")
        t_oh = sem("t_oh")
        t_hist = sem("t_hist")
        t_histdone = sem("t_histdone")
        t_deg = sem("t_deg")
        t_pre = sem("t_pre")
        t_member = sem("t_member")
        t_grp = sem("t_grp")
        t_grpcopied = sem("t_grpcopied")
        t_rank = sem("t_rank")
        t_scat = sem("t_scat")
        t_nodes = sem("t_nodes")
        t_degr = sem("t_degr")
        t_degT = sem("t_degT")
        t_cn = sem("t_cn")
        t_cs = sem("t_cs")
        t_bt = sem("t_bt")
        t_btst = sem("t_btst")
        t_win = sem("t_win")
        t_winst = [sem(f"t_winst{u}") for u in range(2)]
        t_row = sem("t_row")
        t_w = sem("t_w")

        windows_v = windows.rearrange("(p c t) w -> p c (t w)", p=P, t=HB)

        loads = [
            (w_in[:], w["L0_gnn_w_in"].rearrange("(c p) n -> p c n", p=P)),
            (w_1[:], w["L0_gnn_w1"][0].rearrange("(c p) n -> p c n", p=P)),
            (w_2[:], w["L0_gnn_w2"][0].rearrange("(c p) n -> p c n", p=P)),
            (b_in[:], w["L0_gnn_b_in"].rearrange("(a n) -> a n", a=1)),
            (query[:], w["L1_gnn_query_emb"].rearrange("(c p) -> p c", p=P)),
            (gamma[:], w["L1_gnn_gamma"].rearrange("(a n) -> a n", a=1).broadcast_to([P, D])),
            (beta[:], w["L1_gnn_beta"].rearrange("(a n) -> a n", a=1).broadcast_to([P, D])),
            (rel[0:TYPES, 0:TYPES], w["L1_gnn_rel_w"]),
            (rel[TYPES:2 * TYPES, TYPES:2 * TYPES], w["L1_gnn_rel_w"]),
        ]
        for l in range(2):
            for c, k in enumerate("qkv"):
                loads.append((w_qkv[l][:, :, c * D:(c + 1) * D],
                              w[f"L0_gnn_w{k}"][l].rearrange("(c p) n -> p c n", p=P)))
                loads.append((b_qkv[:, l, c * D:(c + 1) * D], w[f"L0_gnn_b{k}"][l:l + 1, :]))
            loads.append((w_o[l][:], w["L0_gnn_wo"][l].rearrange("(c p) n -> p c n", p=P)))
            loads.append((b_o[:, l, :], w["L0_gnn_bo"][l:l + 1, :]))
            loads.append((b_2[:, l, :], w["L0_gnn_b2"][l:l + 1, :]))
            loads.append((b_1[:, l, :], w["L0_gnn_b1"][l].rearrange("(c p) -> p c", p=P)))
            for n, s in enumerate("gb"):
                loads.append((ln1[:, l, n, :], w[f"L0_gnn_ln1_{s}"][l].rearrange("(c p) -> p c", p=P)))
                loads.append((ln2[:, l, n, :], w[f"L0_gnn_ln2_{s}"][l].rearrange("(c p) -> p c", p=P)))
        for c, k in enumerate("qkv"):
            loads.append((w_qkv[2][:, :, c * D:(c + 1) * D],
                          w[f"L1_gnn_W{k}"].rearrange("(c p) n -> p c n", p=P)))
            loads.append((b_qkv[:, 2, c * D:(c + 1) * D],
                          w[f"L1_gnn_b{k}"].rearrange("(a n) -> a n", a=1)))
        loads.append((w_o[2][:], w["L1_gnn_Wo"].rearrange("(c p) n -> p c n", p=P)))
        loads.append((b_o[:, 2, :], w["L1_gnn_bo"].rearrange("(a n) -> a n", a=1)))

        with nc.Block() as block:
            @block.sync
            def _(sp):
                sp.dma_start(dst_i, dst.rearrange("(p t) -> p t", p=P)).then_inc(t_ld, 16)
                for n, a in enumerate((src, edge_type_64)):
                    sp.dma_start(edge_i[:, n * EW:(n + 1) * EW],
                                 bass.AP(tensor=a.tensor, offset=0, ap=[[EP, P], [1, EW]])).then_inc(t_ld_edges, 16)
                sp.wait_ge(t_step, 1)
                for to, of in loads:
                    sp.dma_start(to, of, allow_slow_non_contiguous=True).then_inc(t_w, 16)
                with sp.Fori(0, NHB) as i:
                    for u in range(2):
                        sp.wait_ge(t_win, i * 2 + u + 1)
                        sp.dma_start(windows_v[:, bass.ds(i * 2 + u, 1), :].rearrange("p a b -> p (a b)"),
                                     window_sb[u].rearrange("p t w -> p (t w)")).then_inc(t_winst[u], 16)
                sp.wait_ge(t_scat, 16 * NB)
                sp.dma_start(node_rank[:], node_table.rearrange("(b p) c -> p b c", p=P)).then_inc(t_nodes, 16)
                sp.wait_ge(t_bt, 1)
                sp.dma_start(block_table, bt_out[0:NB, :]).then_inc(t_btst, 16)
                sp.wait_ge(t_btst, 16)
                sp.dma_start(block_row[:], block_table.rearrange("(a b) c -> a (b c)", a=1)).then_inc(t_row, 16)
                sp.wait_ge(t_row, 16)
                sp.wait_ge(t_w, 16 * len(loads))
                for u in range(2):
                    sp.wait_ge(t_winst[u], 16 * NHB)
                    settle(sp)

            @block.gpsimd
            def _(pool):
                nc.gpsimd.iota(iota_i, pattern=[[1, P]], base=0, channel_multiplier=0).then_inc(t_iota, 1)
                nc.gpsimd.iota(part_i, pattern=[[1, 1]], base=0, channel_multiplier=1).then_inc(t_iota, 1)
                nc.gpsimd.iota(payload[:, :, 0:1], pattern=[[P, NB], [1, 1]], base=0,
                               channel_multiplier=1).then_inc(t_iota, 1)
                pool.wait_ge(t_rank, 1)
                for b in range(NB):
                    pool.indirect_dma_start(node_table, bass.IndirectOffsetOnAxis(ap=rank_i[:, b:b + 1], axis=0),
                                            payload[:, b, :], None).then_inc(t_scat, 16)

            @block.scalar
            def _(act):
                act.wait_ge(t_ld_edges, 32)
                settle(act)
                with act.Fori(0, NHB) as i:
                    for u in range(2):
                        with act.If(i >= 1):
                            act.wait_ge(t_winst[u], 16 * i)
                            settle(act)
                        for n in range(2):
                            at = edge_i[:, bass.ds(n * EW + (i * 2 + u) * HB, 1)]
                            at = bass.AP(tensor=at.tensor, offset=at.offset, ap=[at.ap[0], [1, HB], [1, W]])
                            ins = nc.scalar.copy(window_sb[u][:, :, n * W:(n + 1) * W], at)
                        ins.then_inc(t_win, 1)

            @block.tensor
            def _(pe):
                pe.wait_ge(t_oh, 1)
                nc.tensor.matmul(ps_w[:, 0:NB], ident_b[:], zeros_b[:, 0:NB], start=True, stop=False,
                                 skip_group_check=True)
                with pe.Fori(0, NHB) as i:
                    for u in range(2):
                        pe.wait_ge(t_oh, i * 2 + u + 2)
                        for t in range(HB):
                            mm = nc.tensor.matmul(ps_w[:, 0:NB], oh_lo[u][:, t, :], oh_hi[u][:, t, :], start=False,
                                                  stop=False, skip_group_check=True)
                        mm.then_inc(t_hist, 1)
                pe.wait_ge(t_deg, 1)
                nc.tensor.matmul(ps_big[:, 0, 0:NB], below, deg, start=True, stop=True).then_inc(t_pre, 1)
                nc.tensor.matmul(ps_big[:, 1, 0:NB], ones_f, deg, start=True, stop=True).then_inc(t_pre, 1)
                pe.wait_ge(t_member, 1)
                for g in range(GR):
                    if g >= 1:
                        pe.wait_ge(t_grpcopied, g)
                        settle(pe)
                    pe.matmul(ps_big[:, 0, 0:GC], below_b, member[:, g * GC:(g + 1) * GC], start=True, stop=True)
                    pe.matmul(ps_big[:, 1, 0:GC], ones_b, member[:, g * GC:(g + 1) * GC], start=True,
                              stop=True).then_inc(t_grp, 1)
                pe.wait_ge(t_degr, 1)
                nc.tensor.transpose(ps_t[0:NB, 0, :], deg_rank, ident[:]).then_inc(t_degT, 1)
                pe.wait_ge(t_cn, 1)
                nc.tensor.matmul(ps_w[0:NB, 64:66], below[0:NB, 0:NB], bt[0:NB, 2:4], start=True,
                                 stop=True).then_inc(t_cs, 1)

            @block.vector
            def _(dve):
                step = Steps(dve, t_step)
                step(nc.vector.memset(rel[:], 0.0))
                dve.wait_ge(t_iota, 3)
                step(nc.vector.tensor_copy(iota_f[:], iota_i))
                step(nc.vector.tensor_copy(part_f[:], part_i))
                nc.vector.tensor_copy(iota_b, iota_f[:])
                nc.vector.memset(zeros_b[:], 0.0)
                nc.vector.memset(eps_col[:], EPS)
                nc.vector.memset(rec_in[:], 0.0)
                nc.vector.memset(window[:], 0)
                nc.vector.memset(ones_row[:], 1.0)
                nc.vector.memset(ones_f, 1.0)
                nc.vector.memset(ones_b, 1.0)
                nc.vector.memset(running, 0.0)
                nc.vector.tensor_scalar(ident[:], iota_f[:], part_f[:], None, ALU.is_equal)
                nc.vector.tensor_scalar(ident_b[:], iota_f[:], part_f[:], None, ALU.is_equal)
                nc.vector.tensor_scalar(below, iota_f[:], part_f[:], None, ALU.is_gt)
                nc.vector.tensor_scalar(below_b, iota_f[:], part_f[:], None, ALU.is_gt)
                nc.vector.tensor_scalar(cls_iota, iota_f[:, 0:CLASSES], -float(CLASSES - 1), None,
                                        ALU.add).then_inc(t_oh, 1)
                dve.wait_ge(t_ld, 16)
                nc.vector.tensor_scalar(lo_i, dst_i, P - 1, None, ALU.bitwise_and)
                step(nc.vector.tensor_scalar(hi_i, dst_i, 7, None, ALU.arith_shift_right))
                nc.vector.tensor_copy(lo_b, lo_i)
                step(nc.vector.tensor_copy(hi_b, hi_i))
                counted = Passed(dve, t_hist)
                with dve.Fori(0, NHB) as i:
                    for u in range(2):
                        with dve.If(i >= 1):
                            counted.wait()
                            settle(dve)
                        at = bass.ds((i * 2 + u) * HB, HB)
                        nc.vector.tensor_tensor(
                            oh_lo[u], iota_b.unsqueeze(1).broadcast_to([P, HB, P]),
                            lo_b[:, at].unsqueeze(2).broadcast_to([P, HB, P]), ALU.is_equal)
                        nc.vector.tensor_tensor(
                            oh_hi[u], iota_b[:, 0:NB].unsqueeze(1).broadcast_to([P, HB, NB]),
                            hi_b[:, at].unsqueeze(2).broadcast_to([P, HB, NB]), ALU.is_equal).then_inc(t_oh, 1)
                dve.wait_ge(t_hist, NHB * 2)
                nc.vector.tensor_copy(deg, ps_w[:, 0:NB]).then_inc(t_deg, 1)
                dve.wait_ge(t_deg, 1)
                dve.wait_ge(t_pre, 2)
                step(nc.vector.tensor_copy(total, ps_big[:, 1, 0:NB]))
                step(nc.vector.tensor_tensor_scan(total_in, total, running[:, 0:NB], 0.0, ALU.add, ALU.add))
                step(nc.vector.tensor_tensor(first, total_in, total, ALU.subtract))
                step(nc.vector.tensor_tensor(first, first, ps_big[:, 0, 0:NB], ALU.add))
                step(nc.vector.tensor_scalar(cls, deg, float(CLASSES - 1), -1.0, ALU.min, ALU.mult))
                member_v = member.rearrange("p (c b) -> p c b", b=NB)
                nc.vector.tensor_tensor(member_v, cls.unsqueeze(1).broadcast_to([P, CLASSES, NB]),
                                        cls_iota.unsqueeze(2).broadcast_to([P, CLASSES, NB]),
                                        ALU.is_equal).then_inc(t_member, 1)
                dve.wait_ge(t_member, 1)
                for g in range(GR):
                    dve.wait_ge(t_grp, g + 1)
                    nc.vector.tensor_copy(before[:, g * GC:(g + 1) * GC], ps_big[:, 0, 0:GC])
                    nc.vector.tensor_copy(count[:, g * GC:(g + 1) * GC], ps_big[:, 1, 0:GC]).then_inc(t_grpcopied, 1)
                dve.wait_ge(t_grpcopied, GR)
                step(nc.vector.tensor_tensor(before, before, count, ALU.subtract))
                step(nc.vector.tensor_tensor_scan(running, count, running, 0.0, ALU.add, ALU.add))
                step(nc.vector.tensor_tensor(before, before, running, ALU.add))
                step(nc.vector.tensor_tensor(before, before, member, ALU.mult))
                step(nc.vector.tensor_reduce(rank_f, before.rearrange("p (c b) -> p b c", b=NB), AX_X, ALU.add))
                nc.vector.tensor_copy(payload[:, :, 1], first)
                nc.vector.tensor_copy(payload[:, :, 2], deg)
                nc.vector.tensor_copy(payload[:, :, 3], deg)
                nc.vector.tensor_copy(rank_i, rank_f).then_inc(t_rank, 1)
                dve.wait_ge(t_nodes, 16)
                step(nc.vector.tensor_copy(deg_rank, node_rank[:, :, 2]))
                nc.vector.tensor_scalar(has_edge[:], deg_rank, 1.0, None, ALU.min)
                nc.vector.tensor_scalar(no_edge[:], deg_rank, 0.0, None, ALU.is_equal).then_inc(t_degr, 1)
                dve.wait_ge(t_degT, 1)
                b0 = bt[0:NB]
                step(nc.vector.tensor_reduce(b0[:, 0:1], ps_t[0:NB, 0, :], AX_X, ALU.max))

                def ceil_div(to, of, by):
                    step(nc.vector.tensor_scalar(b0[:, 1:2], of, (by - 1) / 2, 1.0 / by, ALU.add, ALU.mult))
                    step(nc.vector.tensor_scalar(b0[:, 1:2], b0[:, 1:2], 8388608.0, None, ALU.add))
                    step(nc.vector.tensor_scalar(b0[:, 1:2], b0[:, 1:2], 8388608.0, None, ALU.subtract))
                    step(nc.vector.tensor_scalar(to, b0[:, 1:2], 1.0, None, ALU.max))

                ceil_div(b0[:, 2:3], b0[:, 0:1], CH)
                ceil_div(b0[:, 3:4], b0[:, 2:3], CPS)
                step(nc.vector.tensor_scalar(b0[:, 4:5], b0[:, 3:4], -1.0, -float(CPS), ALU.add, ALU.mult))
                step(nc.vector.tensor_tensor(b0[:, 4:5], b0[:, 4:5], b0[:, 2:3], ALU.add))
                nc.vector.nop().then_inc(t_cn, 1)
                dve.wait_ge(t_cs, 1)
                nc.vector.tensor_copy(bt_out[0:NB, 0:1], b0[:, 4:5])
                nc.vector.tensor_copy(bt_out[0:NB, 1:2], ps_w[0:NB, 64:65])
                nc.vector.tensor_scalar(bt_out[0:NB, 2:3], b0[:, 3:4], 1.0, None, ALU.subtract)
                nc.vector.tensor_copy(bt_out[0:NB, 3:4], ps_w[0:NB, 65:66]).then_inc(t_bt, 1)
                dve.wait_ge(t_w, 16 * len(loads))
                step(nc.vector.tensor_scalar(rel_rest[:], rel[:], 0.2, None, ALU.mult))
                for n in range(3):
                    step(nc.vector.tensor_copy(rel_part[:, n, :], rel_rest[:]))
                    step(nc.vector.tensor_tensor(rel_rest[:], rel_rest[:], rel_part[:, n, :], ALU.subtract))
                nc.vector.tensor_scalar(query[:], query[:], 0.1, None, ALU.mult)
                nc.vector.memset(sc[:], 0.0)


        def block_counts(eng, b):
            def word(c, lo, hi):
                at = 4 * b + c
                sl = slice(at, at + 1) if isinstance(b, int) else bass.ds(at, 1)
                return eng.value_load(block_row[0:1, sl], min_val=lo, max_val=hi)
            return word(0, 1, CPS), word(1, 0, KMAX * CPS), word(2, 0, KMAX), word(3, 0, KMAX)

        def round_number(k):
            return nc.s_assert_within(k, 0, KMAX - 1, skip_runtime_bounds_check_because="a block has a round per W edges of its fullest node at most")

        def one(parity):
            return slice(parity, parity + 1) if isinstance(parity, int) else bass.ds(parity, 1)

        def flat(ap):
            return ap.rearrange("p a n -> p (a n)")

        def stats(step, n, of, done):
            settle(nc.vector)
            step(nc.vector.bn_stats(bns[:, n, :], of))
            settle(nc.vector)
            nc.vector.bn_aggr(mv[:, n, :], bns[:, n, :]).then_inc(done, 1)

        def deviation(n, done):
            nc.scalar.activation(sd[:, n:n + 1], mv[:, n, 1:2], ACT.Sqrt, bias=eps_col[:]).then_inc(done, 1)

        def scales(step, n, done):
            step(nc.vector.reciprocal(rs[:, n, 0:1], sd[:, n:n + 1]))
            nc.vector.tensor_scalar(rs[:, n, 1:2], mv[:, n, 0:1], rs[:, n, 0:1], -1.0, ALU.mult,
                                    ALU.mult).then_inc(done, 1)

        def transposes(to, of, done):
            for c in range(KD):
                mm = nc.tensor.transpose(to[:, c, :], of[:, c * P:(c + 1) * P], ident[:])
            mm.then_inc(done, 1)

        def project(to, ofT, wt, row, cols=(0, D)):
            a, z = cols
            nc.tensor.matmul(to, ones_row[:], row[:, a:z], start=True, stop=False)
            for c in range(KD):
                mm = nc.tensor.matmul(to, ofT[:, c, :], wt[:, c, a:z], start=False, stop=(c == KD - 1))
            return mm

        def project_qkv(l, ofT, done):
            project(ps_big[:, 0, :], ofT, w_qkv[l], b_qkv[:, l, :], (0, 2 * D))
            project(ps_big[:, 1, 0:D], ofT, w_qkv[l], b_qkv[:, l, :], (2 * D, 3 * D)).then_inc(done, 1)

        p_xat = sem("p_xat")
        p_x = [sem(f"p_x{u}") for u in range(2)]
        p_xfree = sem("p_xfree")
        p_wat = sem("p_wat")
        p_win = sem("p_win")
        p_slot = sem("p_slot")
        p_slotst = sem("p_slotst")
        p_round = sem("p_round")
        p_stepa = sem("p_stepa")
        p_stepb = sem("p_stepb")
        p_cur = sem("p_cur")
        p_vara, p_sda, p_rsa, p_xna, p_ta, p_taT = (sem("p_a" + s) for s in ("var", "sd", "rs", "xn", "tp", "ts"))
        p_h = sem("p_h")
        p_varb, p_sdb, p_rsb, p_xnb, p_tb, p_tbT = (sem("p_b" + s) for s in ("var", "sd", "rs", "xn", "tp", "ts"))
        p_qkv = sem("p_qkv")
        p_rec = sem("p_rec")
        p_recst = sem("p_recst")
        p_kvst = sem("p_kvst")

        with nc.Block() as block:
            @block.sync
            def _(sp):
                with sp.Fori(0, NB) as b:
                    _, _, earlier, before_b = block_counts(sp, b)
                    with sp.Fori(0, earlier + 1) as j:
                        k = round_number(before_b + j)
                        sp.wait_ge(p_slot, k + 1)
                        sp.dma_start(slot_index[bass.ds(k, 1)].rearrange("a p w -> p (a w)"),
                                     flat(idx[:, one(k % 2), :])).then_inc(p_slotst, 16)
                        sp.dma_start(slot_meta[bass.ds(k, 1)].rearrange("a p w -> p (a w)"),
                                     flat(meta[:, one(k % 2), :])).then_inc(p_slotst, 16)
                        sp.wait_ge(p_slotst, 32 * (k + 1))
                        settle(sp)

            @block.gpsimd
            def _(pool):
                def scatter_kv(b):
                    def do(u):
                        pool.indirect_dma_start(
                            kv_dram[0], bass.IndirectOffsetOnAxis(ap=scatter_to[:, u:u + 1], axis=0),
                            rec_out[:, u, D:3 * D], None, bounds_check=N - 1, oob_is_err=False).then_inc(p_kvst, 16)
                    pool.wait_ge(p_rec, b + 1)
                    settle(pool)
                    pick(pool, b % 2, do)
                    pool.wait_ge(p_kvst, 16 * (b + 1))
                    settle(pool)

                def block_of(b):
                    def gather_x(u):
                        pool.indirect_dma_start(
                            rec_in[:, u, 0:D], None, x,
                            bass.IndirectOffsetOnAxis(ap=scatter_to[:, u:u + 1], axis=0),
                            bounds_check=N - 1, oob_is_err=False).then_inc(p_x[u], 16)
                    _, _, earlier, before_b = block_counts(pool, b)
                    pool.wait_ge(p_xat, b + 1)
                    settle(pool)
                    pick(pool, b % 2, gather_x)
                    with pool.Fori(0, earlier + 1) as j:
                        pool.wait_ge(p_wat, before_b + j + 1)
                        settle(pool)
                        pool.indirect_dma_start(
                            window[:], None, windows, bass.IndirectOffsetOnAxis(ap=window_at[:], axis=0),
                            bounds_check=EPAD - 1, oob_is_err=False).then_inc(p_win, 16)

                block_of(0)
                with pool.Fori(1, NB) as b:
                    block_of(b)
                    scatter_kv(b - 1)
                nc.gpsimd.memset(kv[:], 0.0)
                scatter_kv(NB - 1)

            @block.vector
            def _(dve):
                def part_a(b):
                    step = Steps(dve, p_stepa, b * 2)
                    _, _, earlier, before_b = block_counts(dve, b)
                    par = b % 2
                    if not isinstance(b, int):
                        with dve.If(b >= 2):
                            dve.wait_ge(p_kvst, 16 * (b - 1))
                            dve.wait_ge(p_xfree, b - 1)
                            settle(dve)
                    nc.vector.tensor_copy(scatter_to[:, one(par)], node_rank[:, one(b), 0:1].rearrange(
                        "p a c -> p (a c)")).then_inc(p_xat, 1)
                    nc.vector.tensor_copy(round_at[:], node_rank[:, one(b), 1:3].rearrange(
                        "p a c -> p (a c)")).then_inc(p_cur, 1)
                    dve.wait_ge(p_cur, b + 1)
                    nc.vector.tensor_copy(window_at[:], round_at[:, 0:1]).then_inc(p_wat, 1)

                    def stats_x():
                        def wait(u):
                            dve.wait_ge(p_x[u], 16 * (b // 2 + 1))
                            settle(dve)
                        pick(dve, par, wait)
                        stats(step, 0, flat(rec_in[:, one(par), 0:D]), p_vara)

                    def slots():
                        with dve.Fori(0, earlier + 1) as j:
                            k = round_number(before_b + j)
                            dve.wait_ge(p_win, 16 * (k + 1))
                            settle(dve)
                            with dve.If(k >= 2):
                                stored.wait()
                                settle(dve)
                            m = flat(meta[:, one(k % 2), :])
                            chain = Steps(dve, p_round, k * 4)
                            chain(nc.vector.tensor_scalar(valid[:], iota_f[:, 0:W], round_at[:, 1:2], None, ALU.is_lt))
                            nc.vector.tensor_copy(m[:, W:2 * W], window[:, W:2 * W])
                            chain(nc.vector.tensor_scalar(m[:, 0:W], valid[:], 0.5, BIG, ALU.subtract, ALU.mult))
                            chain(nc.vector.scalar_tensor_tensor(out=index_f[:], in0=window[:, 0:W],
                                                                 scalar=-float(SKIP), in1=valid[:], op0=ALU.add,
                                                                 op1=ALU.mult))
                            chain(nc.vector.tensor_scalar(flat(idx[:, one(k % 2), :]), index_f[:], float(SKIP), None,
                                                          ALU.add))
                            nc.vector.tensor_scalar(round_at[:, 0:1], round_at[:, 0:1], float(W), None, ALU.add)
                            nc.vector.tensor_scalar(round_at[:, 1:2], round_at[:, 1:2], -float(W), None,
                                                    ALU.add).then_inc(p_slot, 1)
                            dve.wait_ge(p_slot, k + 1)
                            settle(dve)
                            with dve.If(j < earlier):
                                nc.vector.tensor_copy(window_at[:], round_at[:, 0:1]).then_inc(p_wat, 1)
                        dve.nop()

                    def scale_x():
                        dve.wait_ge(p_sda, b + 1)
                        scales(step, 0, p_rsa)
                    return stats_x, scale_x, slots

                def part_b(b):
                    step = Steps(dve, p_stepb, b * 3)
                    dve.wait_ge(p_h, b + 1)
                    h = flat(rec_out[:, one(b % 2), 3 * D:4 * D])
                    step(nc.vector.tensor_copy(h, ps_w[:, 0:D]))
                    stats(step, 1, h, p_varb)

                    def scale_h():
                        dve.wait_ge(p_sdb, b + 1)
                        scales(step, 1, p_rsb)
                    return scale_h

                stored = Passed(dve, p_slotst, 32)
                stats_x, scale_x, slots = part_a(0)
                stats_x()
                slots()
                scale_x()
                with dve.Fori(1, NB) as b:
                    stats_x, scale_x, slots = part_a(b)
                    scale_h = part_b(b - 1)
                    stats_x()
                    scale_h()
                    scale_x()
                    slots()
                scale_h = part_b(NB - 1)
                scale_h()

            @block.scalar
            def _(act):
                def part_a(b):
                    def normed():
                        par = b % 2
                        xr = flat(rec_in[:, one(par), 0:D])
                        act.wait_ge(p_rsa, b + 1)
                        nc.scalar.activation(xna[:], xr, ACT.Relu, scale=rs[:, 0, 0:1],
                                             bias=rs[:, 0, 1:2]).then_inc(p_xna, 1)
                        if not isinstance(b, int):
                            with act.If(b >= 2):
                                act.wait_ge(p_recst, 16 * (b - 1))
                                settle(act)
                        nc.scalar.copy(flat(rec_out[:, one(par), 4 * D:5 * D]), xr).then_inc(p_xfree, 1)

                    def turned():
                        act.wait_ge(p_ta, b + 1)
                        nc.scalar.copy(xnaT[:], ps_t).then_inc(p_taT, 1)
                    act.wait_ge(p_vara, b + 1)
                    deviation(0, p_sda)
                    return normed, turned

                def part_b(b):
                    act.wait_ge(p_varb, b + 1)
                    deviation(1, p_sdb)

                    def normed():
                        act.wait_ge(p_rsb, b + 1)
                        nc.scalar.activation(xnb[:], flat(rec_out[:, one(b % 2), 3 * D:4 * D]), ACT.Identity,
                                             scale=rs[:, 1, 0:1], bias=rs[:, 1, 1:2]).then_inc(p_xnb, 1)

                    def turned():
                        act.wait_ge(p_tb, b + 1)
                        for c in range(KD):
                            ins = nc.scalar.activation(xnbT[:, c, :], ps_t2[:, c, :], ACT.Identity,
                                                       scale=ln1[:, 0, 0, c:c + 1], bias=ln1[:, 0, 1, c:c + 1])
                        ins.then_inc(p_tbT, 1)

                    def record():
                        par = b % 2
                        act.wait_ge(p_qkv, b + 1)
                        nc.scalar.copy(flat(rec_out[:, one(par), 0:2 * D]), ps_big[:, 0, :])
                        nc.scalar.copy(flat(rec_out[:, one(par), 2 * D:3 * D]), ps_big[:, 1, 0:D]).then_inc(p_rec, 1)
                        act.wait_ge(p_rec, b + 1)
                        if not isinstance(b, int) or b:
                            act.wait_ge(p_recst, 16 * b)
                            settle(act)
                        act.dma_start(rec_dram[0][one(b)].rearrange("a p n -> p (a n)"),
                                      flat(rec_out[:, one(par), :])).then_inc(p_recst, 16)
                    return normed, turned, record

                normed, turned = part_a(0)
                normed()
                turned()
                with act.Fori(1, NB) as b:
                    normed_b, turned_b, record = part_b(b - 1)
                    normed_a, turned_a = part_a(b)
                    normed_b()
                    normed_a()
                    turned_b()
                    turned_a()
                    record()
                normed_b, turned_b, record = part_b(NB - 1)
                normed_b()
                turned_b()
                record()
                act.wait_ge(p_recst, 16 * NB)
                settle(act)

            @block.tensor
            def _(pe):
                def part_a(b):
                    pe.wait_ge(p_xna, b + 1)
                    transposes(ps_t, xna, p_ta)

                    def entry():
                        pe.wait_ge(p_taT, b + 1)
                        project(ps_w[:, 0:D], xnaT, w_in, b_in).then_inc(p_h, 1)
                    return entry

                def part_b(b):
                    pe.wait_ge(p_xnb, b + 1)
                    transposes(ps_t2, xnb, p_tb)

                    def qkv():
                        pe.wait_ge(p_tbT, b + 1)
                        if not isinstance(b, int) or b:
                            pe.wait_ge(p_rec, b)
                            settle(pe)
                        project_qkv(0, xnbT, p_qkv)
                    return qkv

                entry = part_a(0)
                entry()
                with pe.Fori(1, NB) as b:
                    qkv = part_b(b - 1)
                    entry = part_a(b)
                    qkv()
                    entry()
                part_b(NB - 1)()


        moved_by_dma = ("idx", "meta", "kv0", "kv1", "rec", "recst", "scat", "wload")
        between = {name: sem(name) for name in (
            "mul", "score", "relk", "to_exp", "exped", "scaled", "weighted", "summed", "acc", "agg", "round", "block",
            "dense", "aggT", "aggTs", "w", "var1", "sd1", "rs1", "xn1", "xT1", "xTs1", "f1", "g", "f2", "var2", "sd2",
            "rs2", "xn2", "xT2", "xTs2", "qkv", "recq", "oh", "ohT", "ohTs", "relp", "outx", "mixed", "last",
            "arrived")}
        numbers = sorted(handle.num for handle in between.values())
        assert numbers[-1] - numbers[0] == len(numbers) - 1
        for l in range(3):
            H = HEADS[l]
            DH = D // H
            scale = 1.0 / float(np.sqrt(DH))
            typed = l == 2
            S_DENSE = 4 if typed else 6

            s = dict(between, **{name: sem(f"l{l}_{name}") for name in moved_by_dma})
            if l:
                with nc.Block() as block:
                    @block.gpsimd
                    def _(pool):
                        pool.sem_clear(range(numbers[0], numbers[-1] + 1))
            kv_sem = [s["kv0"], s["kv1"]]
            scw = sc[:, 0:W * H]
            smw = sm[:, 0:(W + 1) * H]
            exw = ex[:, 0:(W + 1) * H]
            chunks = kv[:].rearrange("p (r s) d -> p r s d", s=CH)

            def last_round(counts):
                last, chunks_before, earlier, rounds_before = counts
                return (round_number(rounds_before + earlier), chunks_before + earlier * CPS, last)

            def earlier_rounds(eng, counts, do):
                _, chunks_before, earlier, rounds_before = counts
                with eng.If(earlier > 0):
                    with eng.Fori(0, earlier) as j:
                        do(round_number(rounds_before + j), chunks_before + j * CPS, CPS)
                    eng.nop()

            with nc.Block() as block:
                @block.sync
                def _(sp):
                    if l == 1:
                        sp.dma_start(w_1[:], w["L0_gnn_w1"][1].rearrange("(c p) n -> p c n", p=P)).then_inc(s["wload"], 16)
                        sp.dma_start(w_2[:], w["L0_gnn_w2"][1].rearrange("(c p) n -> p c n", p=P)).then_inc(s["wload"], 16)
                    arrived, scored, done = (Passed(sp, s[name]) for name in ("arrived", "scaled", "recq"))
                    with sp.Fori(0, NB) as b:
                        _, _, earlier, rounds_before = block_counts(sp, b)
                        with sp.Fori(0, earlier + 1) as j:
                            k = round_number(rounds_before + j)
                            with sp.If(k >= 2):
                                arrived.wait()
                                settle(sp)
                            with sp.If(k >= 1):
                                sp.wait_ge(s["idx"], 16 * k)
                                settle(sp)
                            sp.dma_start(flat(idx[:, one(k % 2), :]),
                                         slot_index[bass.ds(k, 1)].rearrange("a p w -> p (a w)")).then_inc(s["idx"], 16)
                            with sp.If(k >= 2):
                                scored.wait()
                                settle(sp)
                            with sp.If(k >= 1):
                                sp.wait_ge(s["meta"], 16 * k)
                                settle(sp)
                            sp.dma_start(flat(meta[:, one(k % 2), :]),
                                         slot_meta[bass.ds(k, 1)].rearrange("a p w -> p (a w)")).then_inc(s["meta"], 16)
                        with sp.If(b >= 2):
                            done.wait()
                            settle(sp)
                        with sp.If(b >= 1):
                            sp.wait_ge(s["rec"], 16 * b)
                            settle(sp)
                        sp.dma_start(flat(rec_in[:, one(b % 2), :]),
                                     rec_dram[l][bass.ds(b, 1)].rearrange("a p n -> p (a n)")).then_inc(s["rec"], 16)

                @block.gpsimd
                def _(pool):
                    summed, recorded = Passed(pool, s["summed"]), Passed(pool, s["recq"])
                    scattered = Passed(pool, s["scat"], 16)

                    def scatter(par):
                        def do(u):
                            if typed:
                                to, of = out, rec_out[:, u, 0:D]
                            else:
                                to, of = kv_dram[l + 1], rec_out[:, u, D:3 * D]
                            pool.indirect_dma_start(
                                to, bass.IndirectOffsetOnAxis(ap=scatter_to[:, u:u + 1], axis=0), of, None,
                                bounds_check=N - 1, oob_is_err=False).then_inc(s["scat"], 16)
                        recorded.wait()
                        settle(pool)
                        pick(pool, par, do)
                        scattered.wait()
                        settle(pool)

                    def gather_round(u, k, filled):
                        def gather(c):
                            for slot in range(c * CH, (c + 1) * CH):
                                pool.indirect_dma_start(
                                    kv[:, u * W + slot, :], None, kv_dram[l],
                                    bass.IndirectOffsetOnAxis(ap=idx[:, u, slot:slot + 1], axis=0),
                                    bounds_check=N - 1, oob_is_err=False).then_inc(kv_sem[u], 16)
                        gather(0)
                        for c in range(1, CPS):
                            if isinstance(filled, int):
                                gather(c)
                                continue
                            with pool.If(filled > c):
                                gather(c)
                            pool.nop()

                    with pool.Fori(0, NB) as b:
                        counts = block_counts(pool, b)

                        def gathers(k, _, filled):
                            pool.wait_ge(s["idx"], 16 * (k + 1))
                            settle(pool)
                            with pool.If(k >= 2):
                                summed.wait()
                                settle(pool)
                            pick(pool, k % 2, lambda u: gather_round(u, k, filled))
                        earlier_rounds(pool, counts, gathers)
                        gathers(*last_round(counts))
                        with pool.If(b >= NEXT_BLOCK_LAG):
                            scatter((b + NEXT_BLOCK_LAG) % 2)
                    for b in range(NB - NEXT_BLOCK_LAG, NB):
                        scatter(b % 2)

                @block.vector
                def _(dve):
                    def rel_onehots(k, chunk0, filled):
                        types = flat(meta[:, one(k % 2), W:2 * W])
                        dve.wait_ge(s["meta"], 16 * (k + 1))
                        settle(dve)
                        with dve.Fori(0, filled) as c:
                            at = types_slice(types, c)
                            nc.vector.tensor_tensor(
                                onehot[:, one(c), :].rearrange("p a (s n) -> p (a s) n", n=TYPES),
                                iota_f[:, 0:TYPES].unsqueeze(1).broadcast_to([P, CH, TYPES]),
                                at.unsqueeze(2).broadcast_to([P, CH, TYPES]), ALU.is_equal).then_inc(s["oh"], 1)
                        dve.nop()

                    def types_slice(types, c):
                        return types[:, bass.ds(c * CH, CH)]

                    def chunk_of(k, c, z):
                        return chunks[:, one((k % 2) * CPS + c), :, z * D:(z + 1) * D].rearrange("p a s d -> p (a s) d")

                    def scores(b, k, chunk0, filled):
                        q = flat(rec_in[:, one(b % 2), 0:D]).unsqueeze(1).broadcast_to([P, CH, D])

                        def wait(u):
                            dve.reg_add(sent[u], sent[u], filled * (16 * CH))
                            dve.wait_ge(kv_sem[u], dve.snap(sent[u], min_val=1))
                            settle(dve)
                        pick(dve, k % 2, wait)
                        nc.vector.memset(prod[:, 0:1], 0.0).then_inc(s["arrived"], 1)
                        if not typed:
                            dve.wait_ge(s["meta"], 16 * (k + 1))
                            settle(dve)
                        with dve.Fori(0, filled) as c:
                            at = chunk_of(k, c, 0)
                            if typed:
                                dve.wait_ge(s["relp"], chunk0 + c + 1)
                                nc.vector.tensor_tensor(
                                    at.rearrange("p s (h d) -> p s h d", h=H), at.rearrange("p s (h d) -> p s h d", h=H),
                                    rel_of(chunk0 + c).unsqueeze(2).broadcast_to([P, CH, H, DH]),
                                    ALU.add).then_inc(s["relk"], 1)
                                dve.wait_ge(s["relk"], chunk0 + c + 1)
                                settle(dve)
                            nc.vector.tensor_tensor(at, at, q, ALU.mult).then_inc(s["mul"], 1)
                            dve.wait_ge(s["mul"], chunk0 + c + 1)
                            nc.vector.tensor_reduce(
                                scw[:, bass.ds(c * (CH * H), CH * H)].rearrange("p (s h) -> p s h", h=H),
                                at.rearrange("p s (h d) -> p s h d", h=H), AX_X, ALU.add).then_inc(s["score"], 1)
                        dve.nop()

                    def rel_of(chunk):
                        return ps_rel[:, one(chunk % 2), :].rearrange("p a (s d) -> p (a s) d", d=TYPES)

                    def maxima(step, k, chunk0, filled):
                        dve.wait_ge(s["score"], chunk0 + filled)
                        cap = flat(meta[:, one(k % 2), 0:W]).unsqueeze(2).broadcast_to([P, W, H])
                        nc.vector.tensor_copy(smw[:, W * H:], mrun[:, 0:H])
                        step(nc.vector.tensor_tensor(smw[:, 0:W * H].rearrange("p (s h) -> p s h", h=H),
                                                     scw.rearrange("p (s h) -> p s h", h=H), cap, ALU.min))
                        step(nc.vector.tensor_reduce(mrun[:, 0:H], smw.rearrange("p (s h) -> p h s", h=H), AX_X,
                                                     ALU.max))
                        view = smw.rearrange("p (s h) -> p s h", h=H)
                        nc.vector.tensor_tensor(view, view, mrun[:, 0:H].unsqueeze(1).broadcast_to([P, W + 1, H]),
                                                ALU.subtract).then_inc(s["to_exp"], 1)

                    def rescale(step, b, k):
                        dve.wait_ge(s["exped"], k + 1)
                        dve.wait_ge(s["acc"], k + b + 1)
                        alpha = exw[:, W * H:]
                        step(nc.vector.tensor_tensor(
                            acc_scaled[:].rearrange("p (h d) -> p h d", h=H), acc[:].rearrange("p (h d) -> p h d", h=H),
                            alpha.unsqueeze(2).broadcast_to([P, H, DH]), ALU.mult))
                        step(nc.vector.tensor_tensor(alpha, alpha, zrun[:, 0:H], ALU.mult))
                        nc.vector.tensor_reduce(zrun[:, 0:H], exw.rearrange("p (s h) -> p h s", h=H), AX_X,
                                                ALU.add).then_inc(s["scaled"], 1)

                    def weigh(k, chunk0, filled):
                        with dve.Fori(0, filled) as c:
                            at = chunk_of(k, c, 1).rearrange("p s (h d) -> p s h d", h=H)
                            wt = exw[:, bass.ds(c * (CH * H), CH * H)].rearrange("p (s h) -> p s h", h=H)
                            nc.vector.tensor_tensor(at, at, wt.unsqueeze(3).broadcast_to([P, CH, H, DH]),
                                                    ALU.mult).then_inc(s["weighted"], 1)
                        dve.nop()

                    def iteration(b, dense):
                        step = Steps(dve, s["block"], b * (3 if typed else 4))
                        counts = block_counts(dve, b)
                        k, chunk0, filled = last_round(counts)
                        dve.wait_ge(s["rec"], 16 * (b + 1))
                        r = rec_in[:, one(b % 2), :]
                        q, own_k = flat(r[:, :, 0:D]), flat(r[:, :, D:2 * D])
                        if typed:
                            nc.vector.memset(mrun[:], -1e37)
                            step(nc.vector.memset(zrun[:], 0.0))
                        else:
                            nc.vector.memset(zrun[:], 1.0)
                            step(nc.vector.tensor_tensor(prod[:], q, own_k, ALU.mult))
                            step(nc.vector.tensor_reduce(mrun[:, 0:H], prod[:].rearrange("p (h d) -> p h d", h=H),
                                                         AX_X, ALU.add))

                        def whole(k, chunk0, filled):
                            extra = Steps(dve, s["round"], dve.snap(extras, min_val=0))
                            if typed:
                                rel_onehots(k, chunk0, filled)
                            scores(b, k, chunk0, filled)
                            maxima(extra, k, chunk0, filled)
                            rescale(extra, b, k)
                            weigh(k, chunk0, filled)
                            dve.reg_add(extras, extras, 4)
                        settle(dve)
                        earlier_rounds(dve, counts, whole)
                        last = Steps(dve, s["last"], b * 4)
                        if typed:
                            rel_onehots(k, chunk0, filled)
                        scores(b, k, chunk0, filled)
                        if dense:
                            dense.residual()
                        maxima(last, k, chunk0, filled)
                        if dense:
                            dense.scales1()
                        rescale(last, b, k)
                        weigh(k, chunk0, filled)
                        if dense:
                            dense.second()
                        dve.wait_ge(s["scaled"], k + 1)
                        if typed:
                            step(nc.vector.tensor_scalar(rz[:, 0:H], zrun[:, 0:H], 1e-30, None, ALU.max))
                            step(nc.vector.reciprocal(rz[:, 0:H], rz[:, 0:H]))
                        else:
                            step(nc.vector.reciprocal(rz[:, 0:H], zrun[:, 0:H]))
                            step(nc.vector.tensor_scalar(rz[:, 0:H], rz[:, 0:H], has_edge[:, one(b)], None, ALU.mult))
                        dve.wait_ge(s["acc"], k + b + 2)
                        ins = nc.vector.tensor_tensor(
                            agg[:].rearrange("p (h d) -> p h d", h=H), acc[:].rearrange("p (h d) -> p h d", h=H),
                            rz[:, 0:H].unsqueeze(2).broadcast_to([P, H, DH]), ALU.mult)
                        if typed:
                            ins.then_inc(s["mixed"], 1)
                            dve.wait_ge(s["mixed"], b + 1)
                            ins = nc.vector.scalar_tensor_tensor(
                                out=agg[:], in0=flat(r[:, :, 2 * D:3 * D]), scalar=no_edge[:, one(b)], in1=agg[:],
                                op0=ALU.mult, op1=ALU.add)
                        ins.then_inc(s["agg"], 1)
                        if dense:
                            dense.scales2()

                    class Dense:

                        def __init__(self, b):
                            self.b, self.step = b, Steps(dve, s["dense"], b * S_DENSE)
                            self.res = flat(rec_in[:, one(b % 2), 3 * D:4 * D])
                            self.x = flat(rec_in[:, one(b % 2), 4 * D:5 * D])
                            self.out = rec_out[:, one(b % 2), :]

                        def residual(self):
                            dve.wait_ge(s["w"], self.b + 1)
                            self.step(nc.vector.tensor_tensor(h1[:], self.res, ps_w[:, 0:D], ALU.add))
                            stats(self.step, 0, h1[:], s["var1"])

                        def scales1(self):
                            dve.wait_ge(s["sd1"], self.b + 1)
                            scales(self.step, 0, s["rs1"])

                        def slot_free(self):
                            with dve.If(self.b >= 2) if not isinstance(self.b, int) else nullcontext():
                                scattered.wait()
                                if not typed:
                                    stored.wait()
                                settle(dve)
                            nc.vector.tensor_copy(scatter_to[:, one(self.b % 2)], flat(node_rank[:, one(self.b), 0:1]))

                        def second(self):
                            self.slot_free()
                            if typed:
                                dve.wait_ge(s["xn1"], self.b + 1)
                                o = flat(self.out[:, :, 0:D])
                                self.step(nc.vector.tensor_tensor(xna[:], xna[:], gamma[:], ALU.mult))
                                nc.vector.tensor_tensor(h1[:], beta[:], self.x, ALU.add).then_inc(s["outx"], 1)
                                dve.wait_ge(s["outx"], self.b + 1)
                                nc.vector.tensor_tensor(o, xna[:], h1[:], ALU.add).then_inc(s["recq"], 1)
                                return
                            dve.wait_ge(s["f2"], self.b + 1)
                            if l == 0:
                                h = flat(self.out[:, :, 3 * D:4 * D])
                                self.step(nc.vector.tensor_tensor(h, h1[:], ps_w[:, 256:256 + D], ALU.add))
                                stats(self.step, 1, h, s["var2"])
                            else:
                                self.step(nc.vector.tensor_tensor(h1[:], h1[:], ps_w[:, 256:256 + D], ALU.add))
                                x1 = flat(self.out[:, :, 4 * D:5 * D])
                                nc.vector.tensor_tensor(x1, h1[:], self.x, ALU.add).then_inc(s["outx"], 1)
                                dve.wait_ge(s["outx"], self.b + 1)
                                stats(self.step, 1, x1, s["var2"])

                        def scales2(self):
                            if not typed:
                                dve.wait_ge(s["sd2"], self.b + 1)
                                scales(self.step, 1, s["rs2"])

                        def alone(self):
                            self.residual()
                            self.scales1()
                            self.second()
                            self.scales2()

                    sent = [dve.alloc_register(f"l{l}_sent{u}") for u in range(2)]
                    extras = dve.alloc_register(f"l{l}_extras")
                    for reg in (*sent, extras):
                        dve.reg_mov(reg, 0)
                    scattered, stored = Passed(dve, s["scat"], 16), Passed(dve, s["recst"], 16)
                    iteration(0, None)
                    with dve.Fori(1, NB) as b:
                        iteration(b, Dense(b - 1))
                    Dense(NB - 1).alone()

                @block.scalar
                def _(act):
                    def sum_out(k):
                        act.wait_ge(s["summed"], k + 1)
                        nc.scalar.copy(acc[:], ps_acc[:, 0:D]).then_inc(s["acc"], 1)

                    def exp_round(k):
                        act.wait_ge(s["to_exp"], k + 1)
                        nc.scalar.activation(exw, smw, ACT.Exp, scale=scale).then_inc(s["exped"], 1)

                    def onehots(chunk0, filled):
                        with act.Fori(0, filled) as c:
                            act.wait_ge(s["ohT"], chunk0 + c + 1)
                            nc.scalar.copy(onehotT[:], ps_oh).then_inc(s["ohTs"], 1)
                        act.nop()

                    def iteration(b, dense):
                        counts = block_counts(act, b)
                        k, chunk0, filled = last_round(counts)
                        act.wait_ge(s["rec"], 16 * (b + 1))
                        if not isinstance(b, int) or b:
                            act.wait_ge(s["agg"], b)
                            settle(act)
                        if typed:
                            nc.scalar.copy(acc[:], zeros_b[:]).then_inc(s["acc"], 1)
                        else:
                            nc.scalar.copy(acc[:], flat(rec_in[:, one(b % 2), 2 * D:3 * D])).then_inc(s["acc"], 1)

                        def whole(k, chunk0, filled):
                            if typed:
                                onehots(chunk0, filled)
                            exp_round(k)
                            sum_out(k)
                        earlier_rounds(act, counts, whole)
                        if typed:
                            onehots(chunk0, filled)
                        if dense:
                            dense.turn_sums()
                            dense.deviation1()
                        exp_round(k)
                        if dense:
                            dense.middle()
                        sum_out(k)
                        if dense:
                            dense.tail()

                    class Dense:
                        def __init__(self, b):
                            self.b = b
                            self.out = rec_out[:, one(b % 2), :]

                        def turn_sums(self):
                            act.wait_ge(s["aggT"], self.b + 1)
                            nc.scalar.copy(aggT[:], ps_t).then_inc(s["aggTs"], 1)

                        def deviation1(self):
                            act.wait_ge(s["var1"], self.b + 1)
                            deviation(0, s["sd1"])

                        def middle(self):
                            act.wait_ge(s["rs1"], self.b + 1)
                            nc.scalar.activation(xna[:], h1[:], ACT.Identity, scale=rs[:, 0, 0:1],
                                                 bias=rs[:, 0, 1:2]).then_inc(s["xn1"], 1)
                            if typed:
                                return
                            act.wait_ge(s["xT1"], self.b + 1)
                            for c in range(KD):
                                ins = nc.scalar.activation(xnaT[:, c, :], ps_t[:, c, :], ACT.Identity,
                                                           scale=ln2[:, l, 0, c:c + 1], bias=ln2[:, l, 1, c:c + 1])
                            ins.then_inc(s["xTs1"], 1)
                            for f in range(KF):
                                act.wait_ge(s["f1"], self.b * 2 + f // 4 + 1)
                                nc.scalar.activation(gT[:, f, :], ps_big[:, f // 4, (f % 4) * P:(f % 4 + 1) * P], ACT.Gelu,
                                                     bias=b_1[:, l, f:f + 1]).then_inc(s["g"], 1)
                            act.wait_ge(s["var2"], self.b + 1)
                            deviation(1, s["sd2"])

                        def tail(self):
                            if typed:
                                return
                            act.wait_ge(s["rs2"], self.b + 1)
                            if l == 0:
                                nc.scalar.activation(xnb[:], flat(self.out[:, :, 3 * D:4 * D]), ACT.Identity,
                                                     scale=rs[:, 1, 0:1], bias=rs[:, 1, 1:2]).then_inc(s["xn2"], 1)
                                nc.scalar.copy(flat(self.out[:, :, 4 * D:5 * D]),
                                               flat(rec_in[:, one(self.b % 2), 4 * D:5 * D]))
                            else:
                                nc.scalar.activation(xnb[:], flat(self.out[:, :, 4 * D:5 * D]), ACT.Relu,
                                                     scale=rs[:, 1, 0:1], bias=rs[:, 1, 1:2]).then_inc(s["xn2"], 1)
                                act.wait_ge(s["xn2"], self.b + 1)
                                nc.scalar.copy(flat(self.out[:, :, 3 * D:4 * D]), xnb[:])
                            act.wait_ge(s["xT2"], self.b + 1)
                            for c in range(KD):
                                if l == 0:
                                    ins = nc.scalar.activation(xnbT[:, c, :], ps_t2[:, c, :], ACT.Identity,
                                                               scale=ln1[:, 1, 0, c:c + 1], bias=ln1[:, 1, 1, c:c + 1])
                                else:
                                    ins = nc.scalar.activation(xnbT[:, c, :], ps_t2[:, c, :], ACT.Identity,
                                                               bias=query[:, c:c + 1])
                            ins.then_inc(s["xTs2"], 1)
                            act.wait_ge(s["qkv"], self.b + 1)
                            nc.scalar.copy(flat(self.out[:, :, 0:2 * D]), ps_big[:, 0, :])
                            nc.scalar.copy(flat(self.out[:, :, 2 * D:3 * D]), ps_big[:, 1, 0:D]).then_inc(s["recq"], 1)
                            act.wait_ge(s["recq"], self.b + 1)
                            if not isinstance(self.b, int) or self.b:
                                act.wait_ge(s["recst"], 16 * self.b)
                                settle(act)
                            act.dma_start(rec_dram[l + 1][one(self.b)].rearrange("a p n -> p (a n)"),
                                          flat(self.out)).then_inc(s["recst"], 16)

                        def alone(self):
                            self.turn_sums()
                            self.deviation1()
                            self.middle()
                            self.tail()

                    iteration(0, None)
                    with act.Fori(1, NB) as b:
                        iteration(b, Dense(b - 1))
                    Dense(NB - 1).alone()
                    if not typed:
                        act.wait_ge(s["recst"], 16 * NB)
                        settle(act)

                @block.tensor
                def _(pe):
                    def sums(k, chunk0, filled):
                        pe.wait_ge(s["scaled"], k + 1)
                        nc.tensor.matmul(ps_acc[:, 0:D], ident[:], acc_scaled[:], start=True, stop=False,
                                         skip_group_check=True)
                        with pe.Fori(0, filled) as c:
                            pe.wait_ge(s["weighted"], chunk0 + c + 1)
                            at = chunks[:, one((k % 2) * CPS + c), :, D:2 * D]
                            for slot in range(CH):
                                nc.tensor.matmul(ps_acc[:, 0:D], ident[:], at[:, :, slot, :].rearrange(
                                    "p a d -> p (a d)"), start=False, stop=False, skip_group_check=True)
                        nc.tensor.matmul(ps_acc[:, 0:32], ident_b[:], zeros_b[:, 0:32], start=False, stop=True,
                                         skip_group_check=True).then_inc(s["summed"], 1)

                    def relations(chunk0, filled):
                        with pe.Fori(0, filled) as c:
                            n = chunk0 + c
                            pe.wait_ge(s["oh"], n + 1)
                            for pair in range(2):
                                mm = nc.tensor.transpose(ps_oh[:, pair, :],
                                                         flat(onehot[:, one(c), pair * P:(pair + 1) * P]), ident_b[:])
                            mm.then_inc(s["ohT"], 1)
                            pe.wait_ge(s["ohTs"], n + 1)
                            settle(pe)
                            with pe.If(n >= 2):
                                read.wait()
                                settle(pe)
                            for pair in range(2):
                                for part in range(3):
                                    mm = nc.tensor.matmul(
                                        flat(ps_rel[:, one(n % 2), pair * P:(pair + 1) * P]), onehotT[:, pair, :],
                                        rel_part[:, part, :], start=(part == 0), stop=(part == 2))
                            mm.then_inc(s["relp"], 1)
                        pe.nop()

                    def iteration(b, dense):
                        counts = block_counts(pe, b)
                        k, chunk0, filled = last_round(counts)

                        def whole(k, chunk0, filled):
                            if typed:
                                relations(chunk0, filled)
                            sums(k, chunk0, filled)
                        earlier_rounds(pe, counts, whole)
                        if typed:
                            relations(chunk0, filled)
                        if dense:
                            dense.first()
                        sums(k, chunk0, filled)
                        if dense:
                            dense.tail()

                    class Dense:
                        def __init__(self, b):
                            self.b = b

                        def first(self):
                            pe.wait_ge(s["agg"], self.b + 1)
                            transposes(ps_t, agg, s["aggT"])
                            pe.wait_ge(s["aggTs"], self.b + 1)
                            project(ps_w[:, 0:D], aggT, w_o[l], b_o[:, l, :]).then_inc(s["w"], 1)
                            if typed:
                                return
                            pe.wait_ge(s["xn1"], self.b + 1)
                            transposes(ps_t, xna, s["xT1"])
                            pe.wait_ge(s["xTs1"], self.b + 1)
                            if l == 1:
                                pe.wait_ge(s["wload"], 32)
                                settle(pe)
                            if not isinstance(self.b, int) or self.b:
                                pe.wait_ge(s["recq"], self.b)
                                settle(pe)
                            for f in range(KF):
                                to = ps_big[:, f // 4, (f % 4) * P:(f % 4 + 1) * P]
                                for c in range(KD):
                                    mm = nc.tensor.matmul(to, w_1[:, c, f * P:(f + 1) * P], xnaT[:, c, :],
                                                          start=(c == 0), stop=(c == KD - 1))
                                if f % 4 == 3:
                                    mm.then_inc(s["f1"], 1)
                            to = ps_w[:, D:2 * D]
                            nc.tensor.matmul(to, ones_row[:], b_2[:, l, :], start=True, stop=False)
                            for f in range(KF):
                                pe.wait_ge(s["g"], self.b * KF + f + 1)
                                mm = nc.tensor.matmul(to, gT[:, f, :], w_2[:, f, :], start=False, stop=(f == KF - 1))
                            mm.then_inc(s["f2"], 1)

                        def tail(self):
                            if typed:
                                return
                            pe.wait_ge(s["xn2"], self.b + 1)
                            transposes(ps_t2, xnb, s["xT2"])
                            pe.wait_ge(s["xTs2"], self.b + 1)
                            project_qkv(l + 1, xnbT, s["qkv"])

                    if typed:
                        read = Passed(pe, s["relk"])
                    iteration(0, None)
                    with pe.Fori(1, NB) as b:
                        iteration(b, Dense(b - 1))
                    last = Dense(NB - 1)
                    last.first()
                    last.tail()

        return locals()


_WEIGHTS = [
    "L0_gnn_w_in", "L0_gnn_b_in", "L0_gnn_ln1_g", "L0_gnn_ln1_b", "L0_gnn_ln2_g", "L0_gnn_ln2_b", "L0_gnn_wq",
    "L0_gnn_bq", "L0_gnn_wk", "L0_gnn_bk", "L0_gnn_wv", "L0_gnn_bv", "L0_gnn_wo", "L0_gnn_bo", "L0_gnn_w1",
    "L0_gnn_b1", "L0_gnn_w2", "L0_gnn_b2", "L1_gnn_query_emb", "L1_gnn_Wq", "L1_gnn_bq", "L1_gnn_Wk", "L1_gnn_bk",
    "L1_gnn_Wv", "L1_gnn_bv", "L1_gnn_rel_w", "L1_gnn_Wo", "L1_gnn_bo", "L1_gnn_gamma", "L1_gnn_beta",
]


def kernel(**inputs):
    import concourse.bacc as bacc
    from concourse.bass_utils import run_bass_kernel_spmd

    nc = bacc.Bacc("TRN2", target_bir_lowering=False, num_devices=1)
    arrays, aps = {}, {}

    def give(name, a):
        arrays[f"in_{name}"] = a
        aps[name] = nc.dram_tensor(f"in_{name}", a.shape, mybir.dt.from_np(a.dtype), kind="ExternalInput").ap()

    def padded(a, size, fill):
        out = np.full((size,), fill, a.dtype)
        out[:a.shape[0]] = a
        return out

    give("x", np.ascontiguousarray(inputs["x"]))
    give("src", padded(np.asarray(inputs["src"]), EPAD + W, 0))
    give("dst", padded(np.asarray(inputs["dst"]), EPAD, NPAD))
    give("edge_type_64", padded(np.asarray(inputs["edge_type_64"]), EPAD + W, 0))
    for name in _WEIGHTS:
        give(name, np.ascontiguousarray(inputs[name]))
    out = nc.dram_tensor("out", (N, D), F32, kind="ExternalOutput").ap()
    build(nc, aps["x"], aps["src"], aps["dst"], aps["edge_type_64"], aps, out)
    r = run_bass_kernel_spmd(nc, [arrays], core_ids=[0])
    return r.results[0]["out"]
```

```python
from contextlib import ExitStack, nullcontext

import numpy as np

import concourse.bass as bass
from concourse import mybir

F32 = mybir.dt.float32
I32 = mybir.dt.int32
BF16 = mybir.dt.bfloat16
ALU = mybir.AluOpType
ACT = mybir.ActivationFunctionType
AX_X = mybir.AxisListType.X

P = 128
N = 6250
E = 100000
D = 256
F = 1024
NB = -(-N // P)
NPAD = NB * P
KD = D // P
KF = F // P
EP = -(-E // P)
EPAD = EP * P
CH = 4
CPS = 6
W = CH * CPS
KMAX = NB + E // W
HB = 17
NHB = EP // HB // 2
TYPES = 64
CLASSES = 64
SKIP = 8191
BIG = 3e38
EPS = 1e-5
REC = 5 * D
assert EP == HB * NHB * 2 and NB == 49

HEADS = [8, 8, 4]
RING = 4
SETTLED = []
DEPTH = 3
SCATTER_LAG = 4


def settle(eng):
    eng.sem_inc(SETTLED[0], 1)


class Steps:

    def __init__(self, eng, sem, base=0):
        self.eng, self.sem, self.base, self.n = eng, sem, base, 0

    def __call__(self, ins):
        self.n += 1
        ins.then_inc(self.sem, 1)
        self.eng.wait_ge(self.sem, self.base + self.n)


class Passed:

    def __init__(self, eng, semaphore, by=1):
        self.eng, self.semaphore, self.by = eng, semaphore, by
        self.count = eng.alloc_register()
        eng.reg_mov(self.count, 0)

    def wait(self):
        self.eng.reg_add(self.count, self.count, self.by)
        self.eng.wait_ge(self.semaphore, self.eng.snap(self.count, min_val=1))


def pick(eng, parity, do):
    if isinstance(parity, int):
        do(parity)
        return
    with eng.If(parity == 0):
        do(0)
    with eng.Else():
        do(1)


def build(nc, x, src, dst, edge_type_64, w, out):
    with ExitStack() as ctx:
        def sb(name, shape, dt=F32):
            return ctx.enter_context(nc.sbuf_tensor(name, shape, dt))

        def pb(name, shape, dt=F32):
            return ctx.enter_context(nc.psum_tensor(name, shape, dt))

        def sem(name):
            return ctx.enter_context(nc.semaphore(name))

        def dram(name, shape, dt=F32):
            return nc.dram_tensor(name, shape, dt).ap()

        SETTLED[:] = [sem("settled")]

        windows = dram("windows", [EPAD, 2 * W], I32)
        node_table = dram("node_table", [NPAD, 4], I32)
        block_table = dram("block_table", [NB, 2], I32)
        slot_index = dram("slot_index", [KMAX, P, W], I32)
        slot_meta = dram("slot_meta", [KMAX, P, 2 * W])
        kv_dram = [dram(f"kv_dram{l}", [N, 2 * D]) for l in range(3)]
        rec_dram = [dram(f"rec_dram{l}", [NB, P, REC]) for l in range(3)]

        kv = sb("kv", [P, 2 * W, 2 * D])
        arena = kv[:].rearrange("p a b -> p (a b)")
        used = [0]

        def carve(n, dt=F32, shape=None):
            words = n if dt != BF16 else -(-n // 2)
            view = arena[:, used[0]:used[0] + words].bitcast(dt)[:, 0:n]
            used[0] += words
            assert used[0] <= 2 * W * 2 * D
            return view

        ident = sb("ident", [P, P])
        ident_b = sb("ident_b", [P, P], BF16)
        iota_f = sb("iota_f", [P, P])
        part_f = sb("part_f", [P, 1])
        ones_row = sb("ones_row", [1, P])
        zeros_b = sb("zeros_b", [P, D], BF16)
        node_rank = sb("node_rank", [P, NB, 4], I32)
        has_edge = sb("has_edge", [P, NB])
        no_edge = sb("no_edge", [P, NB])
        block_row = sb("block_row", [1, NB * 2], I32)

        shared = sb("shared", [P, KF * P])
        w_in = shared[:, 0:KD * D].rearrange("p (c n) -> p c n", c=KD)
        gT = shared[:].rearrange("p (f n) -> p f n", f=KF)
        onehot = shared[:, 0:CPS * CH * TYPES // 2].bitcast(BF16).rearrange("p (c n) -> p c n", c=CPS)
        onehotT = shared[:, CPS * CH * TYPES // 2:CPS * CH * TYPES // 2 + P].bitcast(BF16).rearrange(
            "p (c n) -> p c n", c=2)
        w_qkv = [sb(f"w_qkv{l}", [P, KD, 3 * D]) for l in range(3)]
        w_o = [sb(f"w_o{l}", [P, KD, D]) for l in range(3)]
        w_1 = sb("w_1", [P, KD, F])
        w_2 = sb("w_2", [P, KF, D])
        b_in = sb("b_in", [1, D])
        b_qkv = sb("b_qkv", [1, 3, 3 * D])
        b_o = sb("b_o", [1, 3, D])
        b_2 = sb("b_2", [1, 2, D])
        b_1 = sb("b_1", [P, 2, KF])
        ln1 = sb("ln1", [P, 2, 2, KD])
        ln2 = sb("ln2", [P, 2, 2, KD])
        query = sb("query", [P, KD])
        gamma = sb("gamma", [P, D])
        beta = sb("beta", [P, D])
        rel = sb("rel", [P, 2 * TYPES])
        rel_rest = sb("rel_rest", [P, 2 * TYPES])
        rel_part = sb("rel_part", [P, 3, 2 * TYPES], BF16)

        rec_in = sb("rec_in", [P, RING, REC])
        rec_out = sb("rec_out", [P, 2, REC])
        scatter_to = sb("scatter_to", [P, 2], I32)
        idx = sb("idx", [P, 2, W], I32)
        meta = sb("meta", [P, 2, 2 * W])
        sc = sb("sc", [P, W * 8])
        sm = sb("sm", [P, (W + 1) * 8])
        ex = sb("ex", [P, (W + 1) * 8])
        mrun = sb("mrun", [P, 8])
        zrun = sb("zrun", [P, 8])
        rz = sb("rz", [P, 8])
        prod = sb("prod", [P, D])
        acc = sb("acc", [P, D])
        acc_scaled = sb("acc_scaled", [P, D])
        agg = sb("agg", [P, D])
        window = sb("window", [P, 2 * W], I32)
        window_at = sb("window_at", [P, 1], I32)
        round_at = sb("round_at", [P, 2])
        valid = sb("valid", [P, W])
        index_f = sb("index_f", [P, W])
        aggT = sb("aggT", [P, KD, P])
        h1 = sb("h1", [P, D])
        xna = sb("xna", [P, D])
        xnaT = sb("xnaT", [P, KD, P])
        xnb = sb("xnb", [P, D])
        xnbT = sb("xnbT", [P, KD, P])
        bns = sb("bns", [P, 2, 6])
        mv = sb("mv", [P, 2, 2])
        sd = sb("sd", [P, 2])
        rs = sb("rs", [P, 2, 2])
        eps_col = sb("eps_col", [P, 1])

        ps_t = pb("ps_t", [P, 512])[:, 0:D].rearrange("p (c n) -> p c n", c=KD)
        ps_t2_w = pb("ps_t2_w", [P, 512])
        ps_t2 = ps_t2_w[:, 0:D].rearrange("p (c n) -> p c n", c=KD)
        ps_w = pb("ps_w", [P, 512])
        ps_acc = pb("ps_acc", [P, 512])
        ps_big = pb("ps_big", [P, 2, 512])
        ps_rel = ps_big[:, :, 0:CH * TYPES]
        ps_qk = pb("ps_qk", [P, 512])[:]
        ps_v = pb("ps_v", [P, 512])
        ps_oh = ps_v[:, 0:P].bitcast(BF16).rearrange("p (c n) -> p c n", c=2)

        dst_i = carve(EP, I32)
        lo_i = carve(EP, I32)
        hi_i = carve(EP, I32)
        lo_b = carve(EP, BF16)
        hi_b = carve(EP, BF16)
        iota_b = carve(P, BF16)
        oh_lo = [carve(HB * P, BF16).rearrange("p (t n) -> p t n", n=P) for _ in range(2)]
        oh_hi = [carve(HB * NB, BF16).rearrange("p (t n) -> p t n", n=NB) for _ in range(2)]
        EW = EP + W
        edge_i = carve(2 * EW, I32)
        window_sb = [carve(HB * 2 * W, I32).rearrange("p (t w) -> p t w", w=2 * W) for _ in range(2)]
        below = carve(P)
        below_b = carve(P, BF16)
        ones_f = carve(P)
        ones_b = carve(P, BF16)
        deg = carve(NB)
        first = carve(NB)
        total = carve(NB)
        total_in = carve(NB)
        running = carve(CLASSES * NB)
        cls = carve(NB)
        cls_iota = carve(CLASSES)
        member = carve(CLASSES * NB, BF16)
        before = carve(CLASSES * NB)
        count = carve(CLASSES * NB)
        rank_f = carve(NB)
        rank_i = carve(NB, I32)
        payload = carve(NB * 4, I32).rearrange("p (b c) -> p b c", c=4)
        iota_i = carve(P, I32)
        part_i = carve(1, I32)
        deg_rank = carve(NB)
        bt = carve(16)
        bt_out = carve(2, I32)
        GR = 7
        GC = CLASSES * NB // GR

        t_ld = sem("t_ld")
        t_ld_edges = sem("t_ld_edges")
        t_iota = sem("t_iota")
        t_step = sem("t_step")
        t_oh = sem("t_oh")
        t_hist = sem("t_hist")
        t_histdone = sem("t_histdone")
        t_deg = sem("t_deg")
        t_pre = sem("t_pre")
        t_member = sem("t_member")
        t_grp = sem("t_grp")
        t_grpcopied = sem("t_grpcopied")
        t_rank = sem("t_rank")
        t_scat = sem("t_scat")
        t_nodes = sem("t_nodes")
        t_degr = sem("t_degr")
        t_degT = sem("t_degT")
        t_bt = sem("t_bt")
        t_btst = sem("t_btst")
        t_win = sem("t_win")
        t_winst = [sem(f"t_winst{u}") for u in range(2)]
        t_row = sem("t_row")
        t_w = sem("t_w")

        windows_v = windows.rearrange("(p c t) w -> p c (t w)", p=P, t=HB)

        loads = [
            (w_in, w["L0_gnn_w_in"].rearrange("(c p) n -> p c n", p=P)),
            (w_1[:], w["L0_gnn_w1"][0].rearrange("(c p) n -> p c n", p=P)),
            (w_2[:], w["L0_gnn_w2"][0].rearrange("(c p) n -> p c n", p=P)),
            (b_in[:], w["L0_gnn_b_in"].rearrange("(a n) -> a n", a=1)),
            (query[:], w["L1_gnn_query_emb"].rearrange("(c p) -> p c", p=P)),
            (gamma[:], w["L1_gnn_gamma"].rearrange("(a n) -> a n", a=1).broadcast_to([P, D])),
            (beta[:], w["L1_gnn_beta"].rearrange("(a n) -> a n", a=1).broadcast_to([P, D])),
            (rel[0:TYPES, 0:TYPES], w["L1_gnn_rel_w"]),
            (rel[TYPES:2 * TYPES, TYPES:2 * TYPES], w["L1_gnn_rel_w"]),
        ]
        for l in range(2):
            for c, k in enumerate("qkv"):
                loads.append((w_qkv[l][:, :, c * D:(c + 1) * D],
                              w[f"L0_gnn_w{k}"][l].rearrange("(c p) n -> p c n", p=P)))
                loads.append((b_qkv[:, l, c * D:(c + 1) * D], w[f"L0_gnn_b{k}"][l:l + 1, :]))
            loads.append((w_o[l][:], w["L0_gnn_wo"][l].rearrange("(c p) n -> p c n", p=P)))
            loads.append((b_o[:, l, :], w["L0_gnn_bo"][l:l + 1, :]))
            loads.append((b_2[:, l, :], w["L0_gnn_b2"][l:l + 1, :]))
            loads.append((b_1[:, l, :], w["L0_gnn_b1"][l].rearrange("(c p) -> p c", p=P)))
            for n, s in enumerate("gb"):
                loads.append((ln1[:, l, n, :], w[f"L0_gnn_ln1_{s}"][l].rearrange("(c p) -> p c", p=P)))
                loads.append((ln2[:, l, n, :], w[f"L0_gnn_ln2_{s}"][l].rearrange("(c p) -> p c", p=P)))
        for c, k in enumerate("qkv"):
            loads.append((w_qkv[2][:, :, c * D:(c + 1) * D],
                          w[f"L1_gnn_W{k}"].rearrange("(c p) n -> p c n", p=P)))
            loads.append((b_qkv[:, 2, c * D:(c + 1) * D],
                          w[f"L1_gnn_b{k}"].rearrange("(a n) -> a n", a=1)))
        loads.append((w_o[2][:], w["L1_gnn_Wo"].rearrange("(c p) n -> p c n", p=P)))
        loads.append((b_o[:, 2, :], w["L1_gnn_bo"].rearrange("(a n) -> a n", a=1)))

        with nc.Block() as block:
            @block.sync
            def _(sp):
                sp.dma_start(dst_i, dst.rearrange("(p t) -> p t", p=P)).then_inc(t_ld, 16)
                for n, a in enumerate((src, edge_type_64)):
                    sp.dma_start(edge_i[:, n * EW:(n + 1) * EW],
                                 bass.AP(tensor=a.tensor, offset=0, ap=[[EP, P], [1, EW]])).then_inc(t_ld_edges, 16)
                sp.wait_ge(t_step, 1)
                for to, of in loads:
                    sp.dma_start(to, of, allow_slow_non_contiguous=True).then_inc(t_w, 16)
                with sp.Fori(0, NHB) as i:
                    for u in range(2):
                        sp.wait_ge(t_win, i * 2 + u + 1)
                        sp.dma_start(windows_v[:, bass.ds(i * 2 + u, 1), :].rearrange("p a b -> p (a b)"),
                                     window_sb[u].rearrange("p t w -> p (t w)")).then_inc(t_winst[u], 16)
                sp.wait_ge(t_scat, 16 * NB)
                sp.dma_start(node_rank[:], node_table.rearrange("(b p) c -> p b c", p=P)).then_inc(t_nodes, 16)
                sp.wait_ge(t_bt, 1)
                sp.dma_start(block_table, bt_out[0:NB, :]).then_inc(t_btst, 16)
                sp.wait_ge(t_btst, 16)
                sp.dma_start(block_row[:], block_table.rearrange("(a b) c -> a (b c)", a=1)).then_inc(t_row, 16)
                sp.wait_ge(t_row, 16)
                sp.wait_ge(t_w, 16 * len(loads))
                for u in range(2):
                    sp.wait_ge(t_winst[u], 16 * NHB)
                    settle(sp)

            @block.gpsimd
            def _(pool):
                nc.gpsimd.iota(iota_i, pattern=[[1, P]], base=0, channel_multiplier=0).then_inc(t_iota, 1)
                nc.gpsimd.iota(part_i, pattern=[[1, 1]], base=0, channel_multiplier=1).then_inc(t_iota, 1)
                nc.gpsimd.iota(payload[:, :, 0:1], pattern=[[P, NB], [1, 1]], base=0,
                               channel_multiplier=1).then_inc(t_iota, 1)
                pool.wait_ge(t_rank, 1)
                for b in range(NB):
                    pool.indirect_dma_start(node_table, bass.IndirectOffsetOnAxis(ap=rank_i[:, b:b + 1], axis=0),
                                            payload[:, b, :], None).then_inc(t_scat, 16)

            @block.scalar
            def _(act):
                act.wait_ge(t_ld_edges, 32)
                settle(act)
                with act.Fori(0, NHB) as i:
                    for u in range(2):
                        with act.If(i >= 1):
                            act.wait_ge(t_winst[u], 16 * i)
                            settle(act)
                        for n in range(2):
                            at = edge_i[:, bass.ds(n * EW + (i * 2 + u) * HB, 1)]
                            at = bass.AP(tensor=at.tensor, offset=at.offset, ap=[at.ap[0], [1, HB], [1, W]])
                            ins = nc.scalar.copy(window_sb[u][:, :, n * W:(n + 1) * W], at)
                        ins.then_inc(t_win, 1)

            @block.tensor
            def _(pe):
                pe.wait_ge(t_oh, 1)
                nc.tensor.matmul(ps_w[:, 0:NB], ident_b[:], zeros_b[:, 0:NB], start=True, stop=False,
                                 skip_group_check=True)
                with pe.Fori(0, NHB) as i:
                    for u in range(2):
                        pe.wait_ge(t_oh, i * 2 + u + 2)
                        for t in range(HB):
                            mm = nc.tensor.matmul(ps_w[:, 0:NB], oh_lo[u][:, t, :], oh_hi[u][:, t, :], start=False,
                                                  stop=False, skip_group_check=True)
                        mm.then_inc(t_hist, 1)
                pe.wait_ge(t_deg, 1)
                nc.tensor.matmul(ps_big[:, 0, 0:NB], below, deg, start=True, stop=True).then_inc(t_pre, 1)
                nc.tensor.matmul(ps_big[:, 1, 0:NB], ones_f, deg, start=True, stop=True).then_inc(t_pre, 1)
                pe.wait_ge(t_member, 1)
                for g in range(GR):
                    if g >= 1:
                        pe.wait_ge(t_grpcopied, g)
                        settle(pe)
                    pe.matmul(ps_big[:, 0, 0:GC], below_b, member[:, g * GC:(g + 1) * GC], start=True, stop=True)
                    pe.matmul(ps_big[:, 1, 0:GC], ones_b, member[:, g * GC:(g + 1) * GC], start=True,
                              stop=True).then_inc(t_grp, 1)
                pe.wait_ge(t_degr, 1)
                nc.tensor.transpose(ps_t[0:NB, 0, :], deg_rank, ident[:]).then_inc(t_degT, 1)

            @block.vector
            def _(dve):
                step = Steps(dve, t_step)
                step(nc.vector.memset(rel[:], 0.0))
                dve.wait_ge(t_iota, 3)
                step(nc.vector.tensor_copy(iota_f[:], iota_i))
                step(nc.vector.tensor_copy(part_f[:], part_i))
                nc.vector.tensor_copy(iota_b, iota_f[:])
                nc.vector.memset(zeros_b[:], 0.0)
                nc.vector.memset(eps_col[:], EPS)
                nc.vector.memset(rec_in[:], 0.0)
                nc.vector.memset(window[:], 0)
                nc.vector.memset(ones_row[:], 1.0)
                nc.vector.memset(ones_f, 1.0)
                nc.vector.memset(ones_b, 1.0)
                nc.vector.memset(running, 0.0)
                nc.vector.tensor_scalar(ident[:], iota_f[:], part_f[:], None, ALU.is_equal)
                nc.vector.tensor_scalar(ident_b[:], iota_f[:], part_f[:], None, ALU.is_equal)
                nc.vector.tensor_scalar(below, iota_f[:], part_f[:], None, ALU.is_gt)
                nc.vector.tensor_scalar(below_b, iota_f[:], part_f[:], None, ALU.is_gt)
                nc.vector.tensor_scalar(cls_iota, iota_f[:, 0:CLASSES], -float(CLASSES - 1), None,
                                        ALU.add).then_inc(t_oh, 1)
                dve.wait_ge(t_ld, 16)
                nc.vector.tensor_scalar(lo_i, dst_i, P - 1, None, ALU.bitwise_and)
                step(nc.vector.tensor_scalar(hi_i, dst_i, 7, None, ALU.arith_shift_right))
                nc.vector.tensor_copy(lo_b, lo_i)
                step(nc.vector.tensor_copy(hi_b, hi_i))
                counted = Passed(dve, t_hist)
                with dve.Fori(0, NHB) as i:
                    for u in range(2):
                        with dve.If(i >= 1):
                            counted.wait()
                            settle(dve)
                        at = bass.ds((i * 2 + u) * HB, HB)
                        nc.vector.tensor_tensor(
                            oh_lo[u], iota_b.unsqueeze(1).broadcast_to([P, HB, P]),
                            lo_b[:, at].unsqueeze(2).broadcast_to([P, HB, P]), ALU.is_equal)
                        nc.vector.tensor_tensor(
                            oh_hi[u], iota_b[:, 0:NB].unsqueeze(1).broadcast_to([P, HB, NB]),
                            hi_b[:, at].unsqueeze(2).broadcast_to([P, HB, NB]), ALU.is_equal).then_inc(t_oh, 1)
                dve.wait_ge(t_hist, NHB * 2)
                nc.vector.tensor_copy(deg, ps_w[:, 0:NB]).then_inc(t_deg, 1)
                dve.wait_ge(t_deg, 1)
                dve.wait_ge(t_pre, 2)
                step(nc.vector.tensor_copy(total, ps_big[:, 1, 0:NB]))
                step(nc.vector.tensor_tensor_scan(total_in, total, running[:, 0:NB], 0.0, ALU.add, ALU.add))
                step(nc.vector.tensor_tensor(first, total_in, total, ALU.subtract))
                step(nc.vector.tensor_tensor(first, first, ps_big[:, 0, 0:NB], ALU.add))
                step(nc.vector.tensor_scalar(cls, deg, float(CLASSES - 1), -1.0, ALU.min, ALU.mult))
                member_v = member.rearrange("p (c b) -> p c b", b=NB)
                nc.vector.tensor_tensor(member_v, cls.unsqueeze(1).broadcast_to([P, CLASSES, NB]),
                                        cls_iota.unsqueeze(2).broadcast_to([P, CLASSES, NB]),
                                        ALU.is_equal).then_inc(t_member, 1)
                dve.wait_ge(t_member, 1)
                for g in range(GR):
                    dve.wait_ge(t_grp, g + 1)
                    nc.vector.tensor_copy(before[:, g * GC:(g + 1) * GC], ps_big[:, 0, 0:GC])
                    nc.vector.tensor_copy(count[:, g * GC:(g + 1) * GC], ps_big[:, 1, 0:GC]).then_inc(t_grpcopied, 1)
                dve.wait_ge(t_grpcopied, GR)
                step(nc.vector.tensor_tensor(before, before, count, ALU.subtract))
                step(nc.vector.tensor_tensor_scan(running, count, running, 0.0, ALU.add, ALU.add))
                step(nc.vector.tensor_tensor(before, before, running, ALU.add))
                step(nc.vector.tensor_tensor(before, before, member, ALU.mult))
                step(nc.vector.tensor_reduce(rank_f, before.rearrange("p (c b) -> p b c", b=NB), AX_X, ALU.add))
                nc.vector.tensor_copy(payload[:, :, 1], first)
                nc.vector.tensor_copy(payload[:, :, 2], deg)
                nc.vector.tensor_copy(payload[:, :, 3], deg)
                nc.vector.tensor_copy(rank_i, rank_f).then_inc(t_rank, 1)
                dve.wait_ge(t_nodes, 16)
                step(nc.vector.tensor_copy(deg_rank, node_rank[:, :, 2]))
                nc.vector.tensor_scalar(has_edge[:], deg_rank, 1.0, None, ALU.min)
                nc.vector.tensor_scalar(no_edge[:], deg_rank, 0.0, None, ALU.is_equal).then_inc(t_degr, 1)
                dve.wait_ge(t_degT, 1)
                b0 = bt[0:NB]
                step(nc.vector.tensor_reduce(b0[:, 0:1], ps_t[0:NB, 0, :], AX_X, ALU.max))

                def ceil_div(to, of, by):
                    step(nc.vector.tensor_scalar(b0[:, 1:2], of, (by - 1) / 2, 1.0 / by, ALU.add, ALU.mult))
                    step(nc.vector.tensor_scalar(b0[:, 1:2], b0[:, 1:2], 8388608.0, None, ALU.add))
                    step(nc.vector.tensor_scalar(b0[:, 1:2], b0[:, 1:2], 8388608.0, None, ALU.subtract))
                    step(nc.vector.tensor_scalar(to, b0[:, 1:2], 1.0, None, ALU.max))

                ceil_div(b0[:, 2:3], b0[:, 0:1], CH)
                ceil_div(b0[:, 3:4], b0[:, 2:3], CPS)
                step(nc.vector.tensor_scalar(b0[:, 4:5], b0[:, 3:4], -1.0, -float(CPS), ALU.add, ALU.mult))
                step(nc.vector.tensor_tensor(b0[:, 4:5], b0[:, 4:5], b0[:, 2:3], ALU.add))
                nc.vector.tensor_copy(bt_out[0:NB, 0:1], b0[:, 4:5])
                nc.vector.tensor_scalar(bt_out[0:NB, 1:2], b0[:, 3:4], 1.0, None, ALU.subtract).then_inc(t_bt, 1)
                dve.wait_ge(t_w, 16 * len(loads))
                step(nc.vector.tensor_scalar(rel_rest[:], rel[:], 0.2, None, ALU.mult))
                for n in range(3):
                    step(nc.vector.tensor_copy(rel_part[:, n, :], rel_rest[:]))
                    step(nc.vector.tensor_tensor(rel_rest[:], rel_rest[:], rel_part[:, n, :], ALU.subtract))
                nc.vector.tensor_scalar(query[:], query[:], 0.1, None, ALU.mult)
                nc.vector.memset(sc[:], 0.0)


        class Blocks:

            def __init__(self, eng):
                self.eng = eng
                self.chunks = eng.alloc_register()
                self.rounds = eng.alloc_register()
                eng.reg_mov(self.chunks, 0)
                eng.reg_mov(self.rounds, 0)

            def next(self, b):
                def word(c, lo, hi):
                    sl = slice(2 * b + c, 2 * b + c + 1) if isinstance(b, int) else bass.ds(2 * b + c, 1)
                    return self.eng.value_load(block_row[0:1, sl], min_val=lo, max_val=hi)
                last, earlier = word(0, 1, CPS), word(1, 0, KMAX)
                before = [self.eng.snap(reg, min_val=0, max_val=most)
                          for reg, most in ((self.chunks, KMAX * CPS), (self.rounds, KMAX))]
                self.eng.reg_add(self.chunks, self.chunks, earlier * CPS + last)
                self.eng.reg_add(self.rounds, self.rounds, earlier + 1)
                return last, before[0], earlier, before[1]

        def round_number(k):
            return nc.s_assert_within(k, 0, KMAX - 1, skip_runtime_bounds_check_because="a block has a round per W edges of its fullest node at most")

        def one(parity):
            return slice(parity, parity + 1) if isinstance(parity, int) else bass.ds(parity, 1)

        def flat(ap):
            return ap.rearrange("p a n -> p (a n)")

        def stats(step, n, of, done):
            settle(nc.vector)
            step(nc.vector.bn_stats(bns[:, n, :], of))
            settle(nc.vector)
            nc.vector.bn_aggr(mv[:, n, :], bns[:, n, :]).then_inc(done, 1)

        def deviation(n, done):
            nc.scalar.activation(sd[:, n:n + 1], mv[:, n, 1:2], ACT.Sqrt, bias=eps_col[:]).then_inc(done, 1)

        def scales(step, n, done):
            step(nc.vector.reciprocal(rs[:, n, 0:1], sd[:, n:n + 1]))
            nc.vector.tensor_scalar(rs[:, n, 1:2], mv[:, n, 0:1], rs[:, n, 0:1], -1.0, ALU.mult,
                                    ALU.mult).then_inc(done, 1)

        def transposes(to, of, done):
            for c in range(KD):
                mm = nc.tensor.transpose(to[:, c, :], of[:, c * P:(c + 1) * P], ident[:])
            mm.then_inc(done, 1)

        def project(to, ofT, wt, row, cols=(0, D)):
            a, z = cols
            nc.tensor.matmul(to, ones_row[:], row[:, a:z], start=True, stop=False)
            for c in range(KD):
                mm = nc.tensor.matmul(to, ofT[:, c, :], wt[:, c, a:z], start=False, stop=(c == KD - 1))
            return mm

        def project_qkv(l, ofT, done):
            project(ps_qk, ofT, w_qkv[l], b_qkv[:, l, :], (0, 2 * D))
            project(ps_v[:, 0:D], ofT, w_qkv[l], b_qkv[:, l, :], (2 * D, 3 * D)).then_inc(done, 1)

        p_xat = sem("p_xat")
        p_x = [sem(f"p_x{u}") for u in range(2)]
        p_xfree = sem("p_xfree")
        p_wat = sem("p_wat")
        p_win = sem("p_win")
        p_slot = sem("p_slot")
        p_slotst = sem("p_slotst")
        p_round = sem("p_round")
        p_stepa = sem("p_stepa")
        p_stepb = sem("p_stepb")
        p_cur = sem("p_cur")
        p_vara, p_sda, p_rsa, p_xna, p_ta, p_taT = (sem("p_a" + s) for s in ("var", "sd", "rs", "xn", "tp", "ts"))
        p_h = sem("p_h")
        p_varb, p_sdb, p_rsb, p_xnb, p_tb, p_tbT = (sem("p_b" + s) for s in ("var", "sd", "rs", "xn", "tp", "ts"))
        p_qkv = sem("p_qkv")
        p_rec = sem("p_rec")
        p_recst = sem("p_recst")
        p_kvst = sem("p_kvst")

        with nc.Block() as block:
            @block.sync
            def _(sp):
                blocks = Blocks(sp)
                with sp.Fori(0, NB) as b:
                    _, _, earlier, before_b = blocks.next(b)
                    with sp.Fori(0, earlier + 1) as j:
                        k = round_number(before_b + j)
                        sp.wait_ge(p_slot, k + 1)
                        sp.dma_start(slot_index[bass.ds(k, 1)].rearrange("a p w -> p (a w)"),
                                     flat(idx[:, one(k % 2), :])).then_inc(p_slotst, 16)
                        sp.dma_start(slot_meta[bass.ds(k, 1)].rearrange("a p w -> p (a w)"),
                                     flat(meta[:, one(k % 2), :])).then_inc(p_slotst, 16)
                        sp.wait_ge(p_slotst, 32 * (k + 1))
                        settle(sp)

            @block.gpsimd
            def _(pool):
                def scatter_kv(b):
                    def do(u):
                        pool.indirect_dma_start(
                            kv_dram[0], bass.IndirectOffsetOnAxis(ap=scatter_to[:, u:u + 1], axis=0),
                            rec_out[:, u, D:3 * D], None, bounds_check=N - 1, oob_is_err=False).then_inc(p_kvst, 16)
                    pool.wait_ge(p_rec, b + 1)
                    settle(pool)
                    pick(pool, b % 2, do)
                    pool.wait_ge(p_kvst, 16 * (b + 1))
                    settle(pool)

                def block_of(b):
                    def gather_x(u):
                        pool.indirect_dma_start(
                            rec_in[:, u, 0:D], None, x,
                            bass.IndirectOffsetOnAxis(ap=scatter_to[:, u:u + 1], axis=0),
                            bounds_check=N - 1, oob_is_err=False).then_inc(p_x[u], 16)
                    _, _, earlier, before_b = blocks.next(b)
                    pool.wait_ge(p_xat, b + 1)
                    settle(pool)
                    pick(pool, b % 2, gather_x)
                    with pool.Fori(0, earlier + 1) as j:
                        pool.wait_ge(p_wat, before_b + j + 1)
                        settle(pool)
                        pool.indirect_dma_start(
                            window[:], None, windows, bass.IndirectOffsetOnAxis(ap=window_at[:], axis=0),
                            bounds_check=EPAD - 1, oob_is_err=False).then_inc(p_win, 16)

                blocks = Blocks(pool)
                block_of(0)
                with pool.Fori(1, NB) as b:
                    block_of(b)
                    scatter_kv(b - 1)
                nc.gpsimd.memset(kv[:], 0.0)
                scatter_kv(NB - 1)

            @block.vector
            def _(dve):
                def part_a(b):
                    step = Steps(dve, p_stepa, b * 2)
                    _, _, earlier, before_b = blocks.next(b)
                    par = b % 2
                    if not isinstance(b, int):
                        with dve.If(b >= 2):
                            dve.wait_ge(p_kvst, 16 * (b - 1))
                            dve.wait_ge(p_xfree, b - 1)
                            settle(dve)
                    nc.vector.tensor_copy(scatter_to[:, one(par)], node_rank[:, one(b), 0:1].rearrange(
                        "p a c -> p (a c)")).then_inc(p_xat, 1)
                    nc.vector.tensor_copy(round_at[:], node_rank[:, one(b), 1:3].rearrange(
                        "p a c -> p (a c)")).then_inc(p_cur, 1)
                    dve.wait_ge(p_cur, b + 1)
                    nc.vector.tensor_copy(window_at[:], round_at[:, 0:1]).then_inc(p_wat, 1)

                    def stats_x():
                        def wait(u):
                            dve.wait_ge(p_x[u], 16 * (b // 2 + 1))
                            settle(dve)
                        pick(dve, par, wait)
                        stats(step, 0, flat(rec_in[:, one(par), 0:D]), p_vara)

                    def slots():
                        with dve.Fori(0, earlier + 1) as j:
                            k = round_number(before_b + j)
                            dve.wait_ge(p_win, 16 * (k + 1))
                            settle(dve)
                            with dve.If(k >= 2):
                                stored.wait()
                                settle(dve)
                            m = flat(meta[:, one(k % 2), :])
                            chain = Steps(dve, p_round, k * 4)
                            chain(nc.vector.tensor_scalar(valid[:], iota_f[:, 0:W], round_at[:, 1:2], None, ALU.is_lt))
                            nc.vector.tensor_copy(m[:, W:2 * W], window[:, W:2 * W])
                            chain(nc.vector.tensor_scalar(m[:, 0:W], valid[:], 0.5, BIG, ALU.subtract, ALU.mult))
                            chain(nc.vector.scalar_tensor_tensor(out=index_f[:], in0=window[:, 0:W],
                                                                 scalar=-float(SKIP), in1=valid[:], op0=ALU.add,
                                                                 op1=ALU.mult))
                            chain(nc.vector.tensor_scalar(flat(idx[:, one(k % 2), :]), index_f[:], float(SKIP), None,
                                                          ALU.add))
                            nc.vector.tensor_scalar(round_at[:, 0:1], round_at[:, 0:1], float(W), None, ALU.add)
                            nc.vector.tensor_scalar(round_at[:, 1:2], round_at[:, 1:2], -float(W), None,
                                                    ALU.add).then_inc(p_slot, 1)
                            dve.wait_ge(p_slot, k + 1)
                            settle(dve)
                            with dve.If(j < earlier):
                                nc.vector.tensor_copy(window_at[:], round_at[:, 0:1]).then_inc(p_wat, 1)
                        dve.nop()

                    def scale_x():
                        dve.wait_ge(p_sda, b + 1)
                        scales(step, 0, p_rsa)
                    return stats_x, scale_x, slots

                def part_b(b):
                    step = Steps(dve, p_stepb, b * 3)
                    dve.wait_ge(p_h, b + 1)
                    h = flat(rec_out[:, one(b % 2), 3 * D:4 * D])
                    step(nc.vector.tensor_copy(h, ps_w[:, 0:D]))
                    stats(step, 1, h, p_varb)

                    def scale_h():
                        dve.wait_ge(p_sdb, b + 1)
                        scales(step, 1, p_rsb)
                    return scale_h

                stored = Passed(dve, p_slotst, 32)
                blocks = Blocks(dve)
                stats_x, scale_x, slots = part_a(0)
                stats_x()
                slots()
                scale_x()
                with dve.Fori(1, NB) as b:
                    stats_x, scale_x, slots = part_a(b)
                    scale_h = part_b(b - 1)
                    stats_x()
                    scale_h()
                    scale_x()
                    slots()
                scale_h = part_b(NB - 1)
                scale_h()

            @block.scalar
            def _(act):
                def part_a(b):
                    def normed():
                        par = b % 2
                        xr = flat(rec_in[:, one(par), 0:D])
                        act.wait_ge(p_rsa, b + 1)
                        nc.scalar.activation(xna[:], xr, ACT.Relu, scale=rs[:, 0, 0:1],
                                             bias=rs[:, 0, 1:2]).then_inc(p_xna, 1)
                        if not isinstance(b, int):
                            with act.If(b >= 2):
                                act.wait_ge(p_recst, 16 * (b - 1))
                                settle(act)
                        nc.scalar.copy(flat(rec_out[:, one(par), 4 * D:5 * D]), xr).then_inc(p_xfree, 1)

                    def turned():
                        act.wait_ge(p_ta, b + 1)
                        nc.scalar.copy(xnaT[:], ps_t).then_inc(p_taT, 1)
                    act.wait_ge(p_vara, b + 1)
                    deviation(0, p_sda)
                    return normed, turned

                def part_b(b):
                    act.wait_ge(p_varb, b + 1)
                    deviation(1, p_sdb)

                    def normed():
                        act.wait_ge(p_rsb, b + 1)
                        nc.scalar.activation(xnb[:], flat(rec_out[:, one(b % 2), 3 * D:4 * D]), ACT.Identity,
                                             scale=rs[:, 1, 0:1], bias=rs[:, 1, 1:2]).then_inc(p_xnb, 1)

                    def turned():
                        act.wait_ge(p_tb, b + 1)
                        for c in range(KD):
                            ins = nc.scalar.activation(xnbT[:, c, :], ps_t2[:, c, :], ACT.Identity,
                                                       scale=ln1[:, 0, 0, c:c + 1], bias=ln1[:, 0, 1, c:c + 1])
                        ins.then_inc(p_tbT, 1)

                    def record():
                        par = b % 2
                        act.wait_ge(p_qkv, b + 1)
                        nc.scalar.copy(flat(rec_out[:, one(par), 0:2 * D]), ps_qk)
                        nc.scalar.copy(flat(rec_out[:, one(par), 2 * D:3 * D]), ps_v[:, 0:D]).then_inc(p_rec, 1)
                        act.wait_ge(p_rec, b + 1)
                        if not isinstance(b, int) or b:
                            act.wait_ge(p_recst, 16 * b)
                            settle(act)
                        act.dma_start(rec_dram[0][one(b)].rearrange("a p n -> p (a n)"),
                                      flat(rec_out[:, one(par), :])).then_inc(p_recst, 16)
                    return normed, turned, record

                normed, turned = part_a(0)
                normed()
                turned()
                with act.Fori(1, NB) as b:
                    normed_b, turned_b, record = part_b(b - 1)
                    normed_a, turned_a = part_a(b)
                    normed_b()
                    normed_a()
                    turned_b()
                    turned_a()
                    record()
                normed_b, turned_b, record = part_b(NB - 1)
                normed_b()
                turned_b()
                record()
                act.wait_ge(p_recst, 16 * NB)
                settle(act)

            @block.tensor
            def _(pe):
                def part_a(b):
                    pe.wait_ge(p_xna, b + 1)
                    transposes(ps_t, xna, p_ta)

                    def entry():
                        pe.wait_ge(p_taT, b + 1)
                        project(ps_w[:, 0:D], xnaT, w_in, b_in).then_inc(p_h, 1)
                    return entry

                def part_b(b):
                    pe.wait_ge(p_xnb, b + 1)
                    transposes(ps_t2, xnb, p_tb)

                    def qkv():
                        pe.wait_ge(p_tbT, b + 1)
                        if not isinstance(b, int) or b:
                            pe.wait_ge(p_rec, b)
                            settle(pe)
                        project_qkv(0, xnbT, p_qkv)
                    return qkv

                entry = part_a(0)
                entry()
                with pe.Fori(1, NB) as b:
                    qkv = part_b(b - 1)
                    entry = part_a(b)
                    qkv()
                    entry()
                part_b(NB - 1)()


        moved_by_dma = ("idx", "meta", "kv0", "kv1", "rec", "recst", "scat", "wload")
        between = {name: sem(name) for name in (
            "mul", "score", "relk", "to_exp", "exped", "scaled", "weighted", "summed", "acc", "agg", "round", "start",
            "norm", "residual", "second", "scale1", "scale2", "aggT", "aggTs", "w", "var1", "sd1", "var2", "sd2", "rs1", "xn1", "xT1", "xTs1", "f1", "g", "f2", "rs2", "xn2", "xT2", "xTs2", "qkv", "recq", "oh", "ohT", "ohTs", "relp", "outx", "mixed", "last",
            "arrived")}
        numbers = sorted(handle.num for handle in between.values())
        assert numbers[-1] - numbers[0] == len(numbers) - 1
        for l in range(3):
            H = HEADS[l]
            DH = D // H
            scale = 1.0 / float(np.sqrt(DH))
            typed = l == 2
            s = dict(between, **{name: sem(f"l{l}_{name}") for name in moved_by_dma})
            if l:
                with nc.Block() as block:
                    @block.gpsimd
                    def _(pool):
                        pool.sem_clear(range(numbers[0], numbers[-1] + 1))
            kv_sem = [s["kv0"], s["kv1"]]
            scw = sc[:, 0:W * H]
            smw = sm[:, 0:(W + 1) * H]
            exw = ex[:, 0:(W + 1) * H]
            chunks = kv[:].rearrange("p (r s) d -> p r s d", s=CH)

            def last_round(counts):
                last, chunks_before, earlier, rounds_before = counts
                return (round_number(rounds_before + earlier), chunks_before + earlier * CPS, last)

            def exists(b):
                return not isinstance(b, int) or 0 <= b < NB

            def iterate(eng, iteration, peeled=DEPTH):
                for b in range(peeled):
                    iteration(b)
                with eng.Fori(peeled, NB) as b:
                    iteration(b)
                for b in range(NB, NB + DEPTH):
                    iteration(b)

            def earlier_rounds(eng, counts, do):
                _, chunks_before, earlier, rounds_before = counts
                with eng.If(earlier > 0):
                    with eng.Fori(0, earlier) as j:
                        do(round_number(rounds_before + j), chunks_before + j * CPS, CPS)
                    eng.nop()

            with nc.Block() as block:
                @block.sync
                def _(sp):
                    if l == 1:
                        sp.dma_start(w_1[:], w["L0_gnn_w1"][1].rearrange("(c p) n -> p c n", p=P)).then_inc(s["wload"], 16)
                        sp.dma_start(w_2[:], w["L0_gnn_w2"][1].rearrange("(c p) n -> p c n", p=P)).then_inc(s["wload"], 16)
                    arrived, scored, done = (Passed(sp, s[name]) for name in ("arrived", "scaled", "recq"))
                    blocks = Blocks(sp)
                    with sp.Fori(0, NB) as b:
                        _, _, earlier, rounds_before = blocks.next(b)
                        with sp.Fori(0, earlier + 1) as j:
                            k = round_number(rounds_before + j)
                            with sp.If(k >= 2):
                                arrived.wait()
                                settle(sp)
                            with sp.If(k >= 1):
                                sp.wait_ge(s["idx"], 16 * k)
                                settle(sp)
                            sp.dma_start(flat(idx[:, one(k % 2), :]),
                                         slot_index[bass.ds(k, 1)].rearrange("a p w -> p (a w)")).then_inc(s["idx"], 16)
                            with sp.If(k >= 2):
                                scored.wait()
                                settle(sp)
                            with sp.If(k >= 1):
                                sp.wait_ge(s["meta"], 16 * k)
                                settle(sp)
                            sp.dma_start(flat(meta[:, one(k % 2), :]),
                                         slot_meta[bass.ds(k, 1)].rearrange("a p w -> p (a w)")).then_inc(s["meta"], 16)
                        with sp.If(b >= RING):
                            done.wait()
                            settle(sp)
                        with sp.If(b >= 1):
                            sp.wait_ge(s["rec"], 16 * b)
                            settle(sp)
                        sp.dma_start(flat(rec_in[:, one(b % RING), :]),
                                     rec_dram[l][bass.ds(b, 1)].rearrange("a p n -> p (a n)")).then_inc(s["rec"], 16)

                @block.gpsimd
                def _(pool):
                    summed, recorded = Passed(pool, s["summed"]), Passed(pool, s["recq"])
                    scattered = Passed(pool, s["scat"], 16)

                    def scatter(par):
                        def do(u):
                            if typed:
                                to, of = out, rec_out[:, u, 0:D]
                            else:
                                to, of = kv_dram[l + 1], rec_out[:, u, D:3 * D]
                            pool.indirect_dma_start(
                                to, bass.IndirectOffsetOnAxis(ap=scatter_to[:, u:u + 1], axis=0), of, None,
                                bounds_check=N - 1, oob_is_err=False).then_inc(s["scat"], 16)
                        recorded.wait()
                        settle(pool)
                        pick(pool, par, do)
                        scattered.wait()
                        settle(pool)

                    def gather_round(u, k, filled):
                        def gather(c):
                            for slot in range(c * CH, (c + 1) * CH):
                                pool.indirect_dma_start(
                                    kv[:, u * W + slot, :], None, kv_dram[l],
                                    bass.IndirectOffsetOnAxis(ap=idx[:, u, slot:slot + 1], axis=0),
                                    bounds_check=N - 1, oob_is_err=False).then_inc(kv_sem[u], 16)
                        gather(0)
                        for c in range(1, CPS):
                            if isinstance(filled, int):
                                gather(c)
                                continue
                            with pool.If(filled > c):
                                gather(c)
                            pool.nop()

                    blocks = Blocks(pool)
                    with pool.Fori(0, NB) as b:
                        counts = blocks.next(b)

                        def gathers(k, _, filled):
                            pool.wait_ge(s["idx"], 16 * (k + 1))
                            settle(pool)
                            with pool.If(k >= 2):
                                summed.wait()
                                settle(pool)
                            pick(pool, k % 2, lambda u: gather_round(u, k, filled))
                        earlier_rounds(pool, counts, gathers)
                        gathers(*last_round(counts))
                        with pool.If(b >= SCATTER_LAG):
                            scatter(b % 2)
                    for b in range(NB - SCATTER_LAG, NB):
                        scatter(b % 2)

                @block.vector
                def _(dve):
                    def rel_onehots(k, chunk0, filled):
                        types = flat(meta[:, one(k % 2), W:2 * W])
                        dve.wait_ge(s["meta"], 16 * (k + 1))
                        settle(dve)
                        with dve.Fori(0, filled) as c:
                            at = types_slice(types, c)
                            nc.vector.tensor_tensor(
                                onehot[:, one(c), :].rearrange("p a (s n) -> p (a s) n", n=TYPES),
                                iota_f[:, 0:TYPES].unsqueeze(1).broadcast_to([P, CH, TYPES]),
                                at.unsqueeze(2).broadcast_to([P, CH, TYPES]), ALU.is_equal).then_inc(s["oh"], 1)
                        dve.nop()

                    def types_slice(types, c):
                        return types[:, bass.ds(c * CH, CH)]

                    def chunk_of(k, c, z):
                        return chunks[:, one((k % 2) * CPS + c), :, z * D:(z + 1) * D].rearrange("p a s d -> p (a s) d")

                    def scores(b, k, chunk0, filled, meanwhile=lambda: None):
                        q = flat(rec_in[:, one(b % RING), 0:D]).unsqueeze(1).broadcast_to([P, CH, D])

                        for u in range(2):
                            dve.reg_add(sent[u], sent[u], ((k + 1 + u) % 2) * (filled * (16 * CH)))
                        for u in range(2):
                            dve.wait_ge(kv_sem[u], dve.snap(sent[u], min_val=0))
                            settle(dve)
                        nc.vector.memset(prod[:, 0:1], 0.0).then_inc(s["arrived"], 1)
                        if not typed:
                            dve.wait_ge(s["meta"], 16 * (k + 1))

                        def add_relation(c):
                            dve.wait_ge(s["relp"], chunk0 + c + 1)
                            at = chunk_of(k, c, 0).rearrange("p s (h d) -> p s h d", h=H)
                            nc.vector.tensor_tensor(
                                at, at, rel_of(chunk0 + c).unsqueeze(2).broadcast_to([P, CH, H, DH]),
                                ALU.add).then_inc(s["relk"], 1)

                        def products(c):
                            if typed:
                                dve.wait_ge(s["relk"], chunk0 + c + 1)
                            at = chunk_of(k, c, 0)
                            nc.vector.tensor_tensor(at, at, q, ALU.mult).then_inc(s["mul"], 1)

                        def head_sums(c):
                            dve.wait_ge(s["mul"], chunk0 + c + 1)
                            if typed:
                                settle(dve)
                            nc.vector.tensor_reduce(
                                scw[:, slice(c * CH * H, (c + 1) * CH * H) if isinstance(c, int) else
                                    bass.ds(c * (CH * H), CH * H)].rearrange("p (s h) -> p s h", h=H),
                                chunk_of(k, c, 0).rearrange("p s (h d) -> p s h d", h=H), AX_X,
                                ALU.add).then_inc(s["score"], 1)

                        if typed:
                            add_relation(0)
                        else:
                            products(0)
                        meanwhile()
                        settle(dve)
                        with dve.If(filled > 1) if not isinstance(filled, int) else nullcontext():
                            with dve.Fori(1, filled) as c:
                                if typed:
                                    products(c - 1)
                                    add_relation(c)
                                else:
                                    products(c)
                                head_sums(c - 1)
                            dve.nop()
                        if typed:
                            products(filled - 1)
                        head_sums(filled - 1)

                    def rel_of(chunk):
                        return ps_rel[:, one(chunk % 2), :].rearrange("p a (s d) -> p (a s) d", d=TYPES)

                    def maxima(step, k, chunk0, filled):
                        dve.wait_ge(s["score"], chunk0 + filled)
                        cap = flat(meta[:, one(k % 2), 0:W]).unsqueeze(2).broadcast_to([P, W, H])
                        nc.vector.tensor_copy(smw[:, W * H:], mrun[:, 0:H])
                        step(nc.vector.tensor_tensor(smw[:, 0:W * H].rearrange("p (s h) -> p s h", h=H),
                                                     scw.rearrange("p (s h) -> p s h", h=H), cap, ALU.min))
                        step(nc.vector.tensor_reduce(mrun[:, 0:H], smw.rearrange("p (s h) -> p h s", h=H), AX_X,
                                                     ALU.max))
                        view = smw.rearrange("p (s h) -> p s h", h=H)
                        nc.vector.tensor_tensor(view, view, mrun[:, 0:H].unsqueeze(1).broadcast_to([P, W + 1, H]),
                                                ALU.subtract).then_inc(s["to_exp"], 1)

                    def rescale(step, b, k):
                        dve.wait_ge(s["exped"], k + 1)
                        dve.wait_ge(s["acc"], k + b + 1)
                        alpha = exw[:, W * H:]
                        step(nc.vector.tensor_tensor(
                            acc_scaled[:].rearrange("p (h d) -> p h d", h=H), acc[:].rearrange("p (h d) -> p h d", h=H),
                            alpha.unsqueeze(2).broadcast_to([P, H, DH]), ALU.mult))
                        step(nc.vector.tensor_tensor(alpha, alpha, zrun[:, 0:H], ALU.mult))
                        nc.vector.tensor_reduce(zrun[:, 0:H], exw.rearrange("p (s h) -> p h s", h=H), AX_X,
                                                ALU.add).then_inc(s["scaled"], 1)

                    def weigh(k, chunk0, filled):
                        with dve.Fori(0, filled) as c:
                            at = chunk_of(k, c, 1).rearrange("p s (h d) -> p s h d", h=H)
                            wt = exw[:, bass.ds(c * (CH * H), CH * H)].rearrange("p (s h) -> p s h", h=H)
                            nc.vector.tensor_tensor(at, at, wt.unsqueeze(3).broadcast_to([P, CH, H, DH]),
                                                    ALU.mult).then_inc(s["weighted"], 1)
                        dve.nop()

                    def start(b):
                        dve.wait_ge(s["rec"], 16 * (b + 1))
                        r = rec_in[:, one(b % RING), :]
                        step = Steps(dve, s["start"], b * (1 if typed else 2))
                        if typed:
                            nc.vector.memset(mrun[:], -1e37)
                            step(nc.vector.memset(zrun[:], 0.0))
                        else:
                            nc.vector.memset(zrun[:], 1.0)
                            step(nc.vector.tensor_tensor(prod[:], flat(r[:, :, 0:D]), flat(r[:, :, D:2 * D]), ALU.mult))
                            step(nc.vector.tensor_reduce(mrun[:, 0:H], prod[:].rearrange("p (h d) -> p h d", h=H),
                                                         AX_X, ALU.add))

                    def weight_sums(b, k):
                        step = Steps(dve, s["norm"], b * 2)
                        dve.wait_ge(s["scaled"], k + 1)
                        if typed:
                            step(nc.vector.tensor_scalar(rz[:, 0:H], zrun[:, 0:H], 1e-30, None, ALU.max))
                            step(nc.vector.reciprocal(rz[:, 0:H], rz[:, 0:H]))
                        else:
                            step(nc.vector.reciprocal(rz[:, 0:H], zrun[:, 0:H]))
                            step(nc.vector.tensor_scalar(rz[:, 0:H], rz[:, 0:H], has_edge[:, one(b)], None, ALU.mult))

                    def finish(b, rounds):
                        dve.wait_ge(s["acc"], rounds + b + 1)
                        ins = nc.vector.tensor_tensor(
                            agg[:].rearrange("p (h d) -> p h d", h=H), acc[:].rearrange("p (h d) -> p h d", h=H),
                            rz[:, 0:H].unsqueeze(2).broadcast_to([P, H, DH]), ALU.mult)
                        if typed:
                            ins.then_inc(s["mixed"], 1)
                            dve.wait_ge(s["mixed"], b + 1)
                            ins = nc.vector.scalar_tensor_tensor(
                                out=agg[:], in0=flat(rec_in[:, one(b % RING), 2 * D:3 * D]), scalar=no_edge[:, one(b)],
                                in1=agg[:], op0=ALU.mult, op1=ALU.add)
                        ins.then_inc(s["agg"], 1)

                    def residual(b):
                        step = Steps(dve, s["residual"], b * 2)
                        dve.wait_ge(s["w"], b + 1)
                        step(nc.vector.tensor_tensor(h1[:], flat(rec_in[:, one(b % RING), 3 * D:4 * D]),
                                                     ps_t2_w[:, D:2 * D],
                                                     ALU.add))
                        stats(step, 0, h1[:], s["var1"])

                    def second(b):
                        step = Steps(dve, s["second"], b * (1 if typed else 2))
                        x_in = flat(rec_in[:, one(b % RING), 4 * D:5 * D])
                        to = rec_out[:, one(b % 2), :]
                        if not isinstance(b, int) or b >= 2:
                            scattered.wait()
                            if not typed:
                                stored.wait()
                            settle(dve)
                        nc.vector.tensor_copy(scatter_to[:, one(b % 2)], flat(node_rank[:, one(b), 0:1]))
                        if typed:
                            dve.wait_ge(s["xn1"], b + 1)
                            step(nc.vector.tensor_tensor(xna[:], xna[:], gamma[:], ALU.mult))
                            nc.vector.tensor_tensor(xnb[:], beta[:], x_in, ALU.add).then_inc(s["outx"], 1)
                            dve.wait_ge(s["outx"], b + 1)
                            nc.vector.tensor_tensor(flat(to[:, :, 0:D]), xna[:], xnb[:], ALU.add).then_inc(s["recq"], 1)
                            return
                        dve.wait_ge(s["f2"], b + 1)
                        if l == 0:
                            h = flat(to[:, :, 3 * D:4 * D])
                            step(nc.vector.tensor_tensor(h, h1[:], ps_w[:, D:2 * D], ALU.add))
                            stats(step, 1, h, s["var2"])
                        else:
                            step(nc.vector.tensor_tensor(h1[:], h1[:], ps_w[:, D:2 * D], ALU.add))
                            x1 = flat(to[:, :, 4 * D:5 * D])
                            nc.vector.tensor_tensor(x1, h1[:], x_in, ALU.add).then_inc(s["outx"], 1)
                            dve.wait_ge(s["outx"], b + 1)
                            stats(step, 1, x1, s["var2"])

                    def scales1(b):
                        dve.wait_ge(s["sd1"], b + 1)
                        scales(Steps(dve, s["scale1"], b), 0, s["rs1"])

                    def scales2(b):
                        dve.wait_ge(s["sd2"], b + 1)
                        scales(Steps(dve, s["scale2"], b), 1, s["rs2"])

                    def iteration(b):
                        def second_part():
                            if exists(b - 2):
                                second(b - 2)
                        if exists(b):
                            counts = blocks.next(b)
                            k, chunk0, filled = last_round(counts)
                            start(b)

                            def finish_last():
                                if exists(b - 1):
                                    finish(b - 1, counts[3])

                            def whole(k, chunk0, filled):
                                extra = Steps(dve, s["round"], dve.snap(extras, min_val=0))
                                if typed:
                                    rel_onehots(k, chunk0, filled)
                                scores(b, k, chunk0, filled)
                                maxima(extra, k, chunk0, filled)
                                rescale(extra, b, k)
                                weigh(k, chunk0, filled)
                                dve.reg_add(extras, extras, 4)

                            late = exists(b - 1) and not typed
                            earlier = counts[2]
                            if late:
                                settle(dve)
                                with dve.If(earlier > 0):
                                    finish_last()
                            elif exists(b - 1):
                                finish_last()
                            settle(dve)
                            earlier_rounds(dve, counts, whole)
                            last = Steps(dve, s["last"], b * 4)
                            if typed:
                                rel_onehots(k, chunk0, filled)

                            def finish_late():
                                settle(dve)
                                with dve.If(earlier == 0):
                                    finish_last()
                            scores(b, k, chunk0, filled, finish_late if late else lambda: None)
                            second_part()
                            maxima(last, k, chunk0, filled)
                        else:
                            if exists(b - 1):
                                finish(b - 1, dve.snap(blocks.rounds, min_val=1))
                            second_part()
                        if exists(b - 1):
                            residual(b - 1)
                        if exists(b):
                            rescale(last, b, k)
                        if exists(b - 2) and not typed:
                            scales2(b - 2)
                        if exists(b - 1):
                            scales1(b - 1)
                        if exists(b):
                            weigh(k, chunk0, filled)
                            weight_sums(b, k)

                    sent = [dve.alloc_register(f"l{l}_sent{u}") for u in range(2)]
                    extras = dve.alloc_register(f"l{l}_extras")
                    for reg in (*sent, extras):
                        dve.reg_mov(reg, 0)
                    scattered, stored = Passed(dve, s["scat"], 16), Passed(dve, s["recst"], 16)
                    blocks = Blocks(dve)
                    iterate(dve, iteration, DEPTH + 1)

                @block.scalar
                def _(act):
                    def sum_out(k):
                        act.wait_ge(s["summed"], k + 1)
                        nc.scalar.copy(acc[:], ps_acc[:, 0:D]).then_inc(s["acc"], 1)

                    def turn_sums(b):
                        act.wait_ge(s["aggT"], b + 1)
                        nc.scalar.copy(aggT[:], ps_t).then_inc(s["aggTs"], 1)

                    def exp_round(k):
                        act.wait_ge(s["to_exp"], k + 1)
                        nc.scalar.activation(exw, smw, ACT.Exp, scale=scale).then_inc(s["exped"], 1)

                    def onehots(chunk0, filled):
                        with act.Fori(0, filled) as c:
                            act.wait_ge(s["ohT"], chunk0 + c + 1)
                            nc.scalar.copy(onehotT, ps_oh).then_inc(s["ohTs"], 1)
                        act.nop()

                    def start(b):
                        act.wait_ge(s["rec"], 16 * (b + 1))
                        if not isinstance(b, int) or b:
                            act.wait_ge(s["agg"], b)
                            settle(act)
                        if typed:
                            nc.scalar.copy(acc[:], zeros_b[:]).then_inc(s["acc"], 1)
                        else:
                            nc.scalar.copy(acc[:], flat(rec_in[:, one(b % RING), 2 * D:3 * D])).then_inc(s["acc"], 1)

                    def feed_forward(b):
                        act.wait_ge(s["xT1"], b + 1)
                        for c in range(KD):
                            ins = nc.scalar.activation(xnaT[:, c, :], ps_t[:, c, :], ACT.Identity,
                                                       scale=ln2[:, l, 0, c:c + 1], bias=ln2[:, l, 1, c:c + 1])
                        ins.then_inc(s["xTs1"], 1)

                    def hidden(b):
                        for f in range(KF):
                            act.wait_ge(s["f1"], b * 2 + f // 4 + 1)
                            nc.scalar.activation(gT[:, f, :], ps_big[:, f // 4, (f % 4) * P:(f % 4 + 1) * P], ACT.Gelu,
                                                 bias=b_1[:, l, f:f + 1]).then_inc(s["g"], 1)

                    def normed1(b):
                        act.wait_ge(s["rs1"], b + 1)
                        nc.scalar.activation(xna[:], h1[:], ACT.Identity, scale=rs[:, 0, 0:1],
                                             bias=rs[:, 0, 1:2]).then_inc(s["xn1"], 1)

                    def normed2(b):
                        to = rec_out[:, one(b % 2), :]
                        act.wait_ge(s["rs2"], b + 1)
                        if l == 0:
                            nc.scalar.activation(xnb[:], flat(to[:, :, 3 * D:4 * D]), ACT.Identity,
                                                 scale=rs[:, 1, 0:1], bias=rs[:, 1, 1:2]).then_inc(s["xn2"], 1)
                            nc.scalar.copy(flat(to[:, :, 4 * D:5 * D]), flat(rec_in[:, one(b % RING), 4 * D:5 * D]))
                        else:
                            nc.scalar.activation(xnb[:], flat(to[:, :, 4 * D:5 * D]), ACT.Relu,
                                                 scale=rs[:, 1, 0:1], bias=rs[:, 1, 1:2]).then_inc(s["xn2"], 1)
                            act.wait_ge(s["xn2"], b + 1)
                            nc.scalar.copy(flat(to[:, :, 3 * D:4 * D]), xnb[:])

                    def turn_normed(b):
                        act.wait_ge(s["xT2"], b + 1)
                        for c in range(KD):
                            if l == 0:
                                ins = nc.scalar.activation(xnbT[:, c, :], ps_t2[:, c, :], ACT.Identity,
                                                           scale=ln1[:, 1, 0, c:c + 1], bias=ln1[:, 1, 1, c:c + 1])
                            else:
                                ins = nc.scalar.activation(xnbT[:, c, :], ps_t2[:, c, :], ACT.Identity,
                                                           bias=query[:, c:c + 1])
                        ins.then_inc(s["xTs2"], 1)

                    def record(b):
                        to = rec_out[:, one(b % 2), :]
                        act.wait_ge(s["qkv"], b + 1)
                        nc.scalar.copy(flat(to[:, :, 0:2 * D]), ps_qk)
                        nc.scalar.copy(flat(to[:, :, 2 * D:3 * D]), ps_v[:, 0:D]).then_inc(s["recq"], 1)
                        act.wait_ge(s["recq"], b + 1)
                        if not isinstance(b, int) or b:
                            act.wait_ge(s["recst"], 16 * b)
                            settle(act)
                        act.dma_start(rec_dram[l + 1][one(b)].rearrange("a p n -> p (a n)"),
                                      flat(to)).then_inc(s["recst"], 16)

                    def iteration(b):
                        if exists(b - 2) and not typed:
                            feed_forward(b - 2)
                        if exists(b - 3) and not typed:
                            turn_normed(b - 3)
                        if exists(b - 2) and not typed:
                            hidden(b - 2)
                        if exists(b):
                            counts = blocks.next(b)
                            k, chunk0, filled = last_round(counts)
                            start(b)
                        if exists(b - 1):
                            turn_sums(b - 1)
                        if exists(b):
                            def whole(k, chunk0, filled):
                                if typed:
                                    onehots(chunk0, filled)
                                exp_round(k)
                                sum_out(k)
                            earlier_rounds(act, counts, whole)
                            if typed:
                                onehots(chunk0, filled)
                            exp_round(k)
                        if exists(b - 2) and not typed:
                            act.wait_ge(s["var2"], b - 1)
                            deviation(1, s["sd2"])
                        if exists(b - 1):
                            act.wait_ge(s["var1"], b)
                            deviation(0, s["sd1"])
                        if exists(b - 2) and not typed:
                            normed2(b - 2)
                        if exists(b - 1):
                            normed1(b - 1)
                        if exists(b - 3) and not typed:
                            record(b - 3)
                        if exists(b):
                            sum_out(k)

                    blocks = Blocks(act)
                    iterate(act, iteration)
                    if not typed:
                        act.wait_ge(s["recst"], 16 * NB)
                        settle(act)

                @block.tensor
                def _(pe):
                    def sums(k, chunk0, filled):
                        pe.wait_ge(s["scaled"], k + 1)
                        nc.tensor.matmul(ps_acc[:, 0:D], ident[:], acc_scaled[:], start=True, stop=False,
                                         skip_group_check=True)
                        with pe.Fori(0, filled) as c:
                            pe.wait_ge(s["weighted"], chunk0 + c + 1)
                            at = chunks[:, one((k % 2) * CPS + c), :, D:2 * D]
                            for slot in range(CH):
                                nc.tensor.matmul(ps_acc[:, 0:D], ident[:], at[:, :, slot, :].rearrange(
                                    "p a d -> p (a d)"), start=False, stop=False, skip_group_check=True)
                        nc.tensor.matmul(ps_acc[:, 0:32], ident_b[:], zeros_b[:, 0:32], start=False, stop=True,
                                         skip_group_check=True).then_inc(s["summed"], 1)

                    def relations(chunk0, filled):
                        with pe.Fori(0, filled) as c:
                            n = chunk0 + c
                            pe.wait_ge(s["oh"], n + 1)
                            for pair in range(2):
                                mm = nc.tensor.transpose(ps_oh[:, pair, :],
                                                         flat(onehot[:, one(c), pair * P:(pair + 1) * P]), ident_b[:])
                            mm.then_inc(s["ohT"], 1)
                            pe.wait_ge(s["ohTs"], n + 1)
                            settle(pe)
                            with pe.If(n >= 2):
                                read.wait()
                                settle(pe)
                            for pair in range(2):
                                for part in range(3):
                                    mm = nc.tensor.matmul(
                                        flat(ps_rel[:, one(n % 2), pair * P:(pair + 1) * P]), onehotT[:, pair, :],
                                        rel_part[:, part, :], start=(part == 0), stop=(part == 2))
                            mm.then_inc(s["relp"], 1)
                        pe.nop()

                    def turn_sums(b):
                        pe.wait_ge(s["agg"], b + 1)
                        transposes(ps_t, agg, s["aggT"])

                    def project_sums(b):
                        pe.wait_ge(s["aggTs"], b + 1)
                        project(ps_t2_w[:, D:2 * D], aggT, w_o[l], b_o[:, l, :]).then_inc(s["w"], 1)

                    def turn_hidden(b):
                        pe.wait_ge(s["xn1"], b + 1)
                        transposes(ps_t, xna, s["xT1"])

                    def feed_forward(b):
                        pe.wait_ge(s["xTs1"], b + 1)
                        if l == 1:
                            pe.wait_ge(s["wload"], 32)
                            settle(pe)
                        for f in range(KF):
                            to = ps_big[:, f // 4, (f % 4) * P:(f % 4 + 1) * P]
                            for c in range(KD):
                                mm = nc.tensor.matmul(to, w_1[:, c, f * P:(f + 1) * P], xnaT[:, c, :],
                                                      start=(c == 0), stop=(c == KD - 1))
                            if f % 4 == 3:
                                mm.then_inc(s["f1"], 1)

                    def feed_out(b):
                        to = ps_w[:, D:2 * D]
                        nc.tensor.matmul(to, ones_row[:], b_2[:, l, :], start=True, stop=False)
                        for f in range(KF):
                            pe.wait_ge(s["g"], b * KF + f + 1)
                            mm = nc.tensor.matmul(to, gT[:, f, :], w_2[:, f, :], start=False, stop=(f == KF - 1))
                        mm.then_inc(s["f2"], 1)

                    def turn_normed(b):
                        pe.wait_ge(s["xn2"], b + 1)
                        transposes(ps_t2, xnb, s["xT2"])

                    def next_qkv(b):
                        pe.wait_ge(s["xTs2"], b + 1)
                        if not isinstance(b, int) or b:
                            pe.wait_ge(s["recq"], b)
                            settle(pe)
                        project_qkv(l + 1, xnbT, s["qkv"])

                    def iteration(b):
                        if exists(b - 2) and not typed:
                            turn_hidden(b - 2)
                        if exists(b - 3) and not typed:
                            turn_normed(b - 3)
                        if exists(b - 2) and not typed:
                            feed_forward(b - 2)
                        if exists(b - 1):
                            turn_sums(b - 1)
                        if exists(b - 2) and not typed:
                            feed_out(b - 2)
                        if exists(b - 3) and not typed:
                            pe.wait_ge(s["xTs2"], b - 2)
                            settle(pe)
                        if exists(b - 1):
                            project_sums(b - 1)
                        if exists(b - 3) and not typed:
                            next_qkv(b - 3)
                        if exists(b):
                            counts = blocks.next(b)
                            k, chunk0, filled = last_round(counts)

                            def whole(k, chunk0, filled):
                                if typed:
                                    relations(chunk0, filled)
                                sums(k, chunk0, filled)
                            earlier_rounds(pe, counts, whole)
                            if typed:
                                relations(chunk0, filled)
                            sums(k, chunk0, filled)

                    if typed:
                        read = Passed(pe, s["relk"])
                    blocks = Blocks(pe)
                    iterate(pe, iteration)

        return locals()


_WEIGHTS = [
    "L0_gnn_w_in", "L0_gnn_b_in", "L0_gnn_ln1_g", "L0_gnn_ln1_b", "L0_gnn_ln2_g", "L0_gnn_ln2_b", "L0_gnn_wq",
    "L0_gnn_bq", "L0_gnn_wk", "L0_gnn_bk", "L0_gnn_wv", "L0_gnn_bv", "L0_gnn_wo", "L0_gnn_bo", "L0_gnn_w1",
    "L0_gnn_b1", "L0_gnn_w2", "L0_gnn_b2", "L1_gnn_query_emb", "L1_gnn_Wq", "L1_gnn_bq", "L1_gnn_Wk", "L1_gnn_bk",
    "L1_gnn_Wv", "L1_gnn_bv", "L1_gnn_rel_w", "L1_gnn_Wo", "L1_gnn_bo", "L1_gnn_gamma", "L1_gnn_beta",
]


def kernel(**inputs):
    import concourse.bacc as bacc
    from concourse.bass_utils import run_bass_kernel_spmd

    nc = bacc.Bacc("TRN2", target_bir_lowering=False, num_devices=1)
    arrays, aps = {}, {}

    def give(name, a):
        arrays[f"in_{name}"] = a
        aps[name] = nc.dram_tensor(f"in_{name}", a.shape, mybir.dt.from_np(a.dtype), kind="ExternalInput").ap()

    def padded(a, size, fill):
        out = np.full((size,), fill, a.dtype)
        out[:a.shape[0]] = a
        return out

    give("x", np.ascontiguousarray(inputs["x"]))
    give("src", padded(np.asarray(inputs["src"]), EPAD + W, 0))
    give("dst", padded(np.asarray(inputs["dst"]), EPAD, NPAD))
    give("edge_type_64", padded(np.asarray(inputs["edge_type_64"]), EPAD + W, 0))
    for name in _WEIGHTS:
        give(name, np.ascontiguousarray(inputs[name]))
    out = nc.dram_tensor("out", (N, D), F32, kind="ExternalOutput").ap()
    build(nc, aps["x"], aps["src"], aps["dst"], aps["edge_type_64"], aps, out)
    r = run_bass_kernel_spmd(nc, [arrays], core_ids=[0])
    return r.results[0]["out"]
```

```python
from contextlib import ExitStack, nullcontext

import numpy as np

import concourse.bass as bass
from concourse import mybir

F32 = mybir.dt.float32
I32 = mybir.dt.int32
BF16 = mybir.dt.bfloat16
ALU = mybir.AluOpType
ACT = mybir.ActivationFunctionType
AX_X = mybir.AxisListType.X

P = 128
N = 6250
E = 100000
D = 256
F = 1024
NB = -(-N // P)
NPAD = NB * P
KD = D // P
KF = F // P
EP = -(-E // P)
EPAD = EP * P
CH = 4
CPS = 6
W = CH * CPS
KMAX = NB + E // W
HB = 17
NHB = EP // HB // 2
TYPES = 64
CLASSES = 64
SKIP = 8191
BIG = 3e38
EPS = 1e-5
REC = 5 * D
assert EP == HB * NHB * 2 and NB == 49

HEADS = [8, 8, 4]
RING = 4
SETTLED = []
DEPTH = 3
SCATTER_LAG = 4


def settle(eng):
    eng.sem_inc(SETTLED[0], 1)


class Steps:

    def __init__(self, eng, sem, base=0):
        self.eng, self.sem, self.base, self.n = eng, sem, base, 0

    def __call__(self, ins):
        self.n += 1
        ins.then_inc(self.sem, 1)
        self.eng.wait_ge(self.sem, self.base + self.n)


class Passed:

    def __init__(self, eng, semaphore, by=1):
        self.eng, self.semaphore, self.by = eng, semaphore, by
        self.count = eng.alloc_register()
        eng.reg_mov(self.count, 0)

    def wait(self):
        self.eng.reg_add(self.count, self.count, self.by)
        self.eng.wait_ge(self.semaphore, self.eng.snap(self.count, min_val=1))


def pick(eng, which, do, choices=(0, 1)):
    if isinstance(which, int):
        do(which)
        return
    if len(choices) == 1:
        do(choices[0])
        return
    half = len(choices) // 2
    with eng.If(which < choices[half]):
        pick(eng, which, do, choices[:half])
        eng.nop()
    with eng.Else():
        pick(eng, which, do, choices[half:])
        eng.nop()


def build(nc, x, src, dst, edge_type_64, w, out):
    with ExitStack() as ctx:
        def sb(name, shape, dt=F32):
            return ctx.enter_context(nc.sbuf_tensor(name, shape, dt))

        def pb(name, shape, dt=F32):
            return ctx.enter_context(nc.psum_tensor(name, shape, dt))

        def sem(name):
            return ctx.enter_context(nc.semaphore(name))

        def dram(name, shape, dt=F32):
            return nc.dram_tensor(name, shape, dt).ap()

        SETTLED[:] = [sem("settled")]

        windows = dram("windows", [EPAD, 2 * W], I32)
        node_table = dram("node_table", [NPAD, 4], I32)
        block_table = dram("block_table", [NB, 2], I32)
        slot_index = dram("slot_index", [KMAX, P, W], I32)
        slot_meta = dram("slot_meta", [KMAX, P, 2 * W])
        kv_dram = [dram(f"kv_dram{l}", [N, 2 * D]) for l in range(3)]
        rec_dram = [dram(f"rec_dram{l}", [NB, P, REC]) for l in range(3)]

        kv = sb("kv", [P, 2 * W, 2 * D])
        arena = kv[:].rearrange("p a b -> p (a b)")
        used = [0]

        def carve(n, dt=F32, shape=None):
            words = n if dt != BF16 else -(-n // 2)
            view = arena[:, used[0]:used[0] + words].bitcast(dt)[:, 0:n]
            used[0] += words
            assert used[0] <= 2 * W * 2 * D
            return view

        ident = sb("ident", [P, P])
        ident_b = sb("ident_b", [P, P], BF16)
        iota_f = sb("iota_f", [P, P])
        part_f = sb("part_f", [P, 1])
        ones_rows = sb("ones_rows", [3, P], BF16)
        zeros_b = sb("zeros_b", [P, D], BF16)
        node_rank = sb("node_rank", [P, NB + 1, 4], I32)
        has_edge = sb("has_edge", [P, NB])
        no_edge = sb("no_edge", [P, NB])
        block_row = sb("block_row", [1, NB * 2], I32)

        shared = sb("shared", [P, KF * P])
        w_in = shared[:, 0:KD * D].rearrange("p (c n) -> p c n", c=KD)
        gT = shared[:].rearrange("p (f n) -> p f n", f=KF)
        onehot = shared[:, 0:CPS * CH * TYPES // 2].bitcast(BF16).rearrange("p (c n) -> p c n", c=CPS)
        onehotT = shared[:, CPS * CH * TYPES // 2:CPS * CH * TYPES // 2 + P].bitcast(BF16).rearrange(
            "p (c n) -> p c n", c=2)
        w_qkv = [sb(f"w_qkv{l}", [P, KD, 3 * D]) for l in range(3)]
        w_o = [sb(f"w_o{l}", [P, KD, D]) for l in range(3)]
        w_1 = sb("w_1", [P, KD, F])
        w_2 = sb("w_2", [P, KF, D])
        B_IN, B_QKV, B_O, B_2, B_ALL = 0, D, 10 * D, 13 * D, 15 * D
        bias_parts = sb("bias_parts", [3, B_ALL], BF16)
        b_1 = sb("b_1", [P, 2, KF])
        ln1 = sb("ln1", [P, 2, 2, KD])
        ln2 = sb("ln2", [P, 2, 2, KD])
        query = sb("query", [P, KD])
        gamma = sb("gamma", [P, D])
        beta = sb("beta", [P, D])
        rel = sb("rel", [P, 2 * TYPES])
        rel_rest = sb("rel_rest", [P, 2 * TYPES])
        rel_part = sb("rel_part", [P, 3, 2 * TYPES], BF16)

        rec_in = sb("rec_in", [P, RING, REC])
        rec_out = sb("rec_out", [P, 2, REC])
        scatter_to = sb("scatter_to", [P, RING], I32)
        idx = sb("idx", [P, 2, W], I32)
        meta = sb("meta", [P, 2, 2 * W])
        sc = sb("sc", [P, W * 8])
        sm = sb("sm", [P, (W + 1) * 8])
        ex = sb("ex", [P, (W + 1) * 8])
        mrun = sb("mrun", [P, 8])
        zrun = sb("zrun", [P, 8])
        rz = sb("rz", [P, 8])
        prod = sb("prod", [P, D])
        acc = sb("acc", [P, D])
        acc_scaled = sb("acc_scaled", [P, D])
        agg = sb("agg", [P, D])
        window = sb("window", [P, 2, 2 * W], I32)
        window_at = sb("window_at", [P, 2], I32)
        round_at = sb("round_at", [P, 2, 2])
        valid = sb("valid", [P, W])
        index_f = sb("index_f", [P, W])
        aggT = sb("aggT", [P, KD, P])
        h1 = sb("h1", [P, D])
        xna = sb("xna", [P, D])
        xnaT = sb("xnaT", [P, KD, P])
        xnb = sb("xnb", [P, D])
        xnbT = sb("xnbT", [P, KD, P])
        bns = sb("bns", [P, 2, 6])
        mv = sb("mv", [P, 2, 2])
        sd = sb("sd", [P, 2])
        rs = sb("rs", [P, 2, 2])
        eps_col = sb("eps_col", [P, 1])

        ps_t = pb("ps_t", [P, 512])[:, 0:D].rearrange("p (c n) -> p c n", c=KD)
        ps_t2_w = pb("ps_t2_w", [P, 512])
        ps_t2 = ps_t2_w[:, 0:D].rearrange("p (c n) -> p c n", c=KD)
        ps_w = pb("ps_w", [P, 512])
        ps_acc = pb("ps_acc", [P, 512])
        ps_big = pb("ps_big", [P, 2, 512])
        ps_rel = ps_big[:, :, 0:CH * TYPES]
        ps_qk = pb("ps_qk", [P, 512])[:]
        ps_v = pb("ps_v", [P, 512])
        ps_oh = ps_v[:, 0:P].bitcast(BF16).rearrange("p (c n) -> p c n", c=2)

        dst_i = carve(EP, I32)
        lo_i = carve(EP, I32)
        hi_i = carve(EP, I32)
        lo_b = carve(EP, BF16)
        hi_b = carve(EP, BF16)
        iota_b = carve(P, BF16)
        oh_lo = [carve(HB * P, BF16).rearrange("p (t n) -> p t n", n=P) for _ in range(2)]
        oh_hi = [carve(HB * NB, BF16).rearrange("p (t n) -> p t n", n=NB) for _ in range(2)]
        EW = EP + W
        edge_i = carve(2 * EW, I32)
        window_sb = [carve(HB * 2 * W, I32).rearrange("p (t w) -> p t w", w=2 * W) for _ in range(2)]
        below = carve(P)
        below_b = carve(P, BF16)
        ones_f = carve(P)
        ones_b = carve(P, BF16)
        deg = carve(NB)
        first = carve(NB)
        total = carve(NB)
        total_in = carve(NB)
        running = carve(CLASSES * NB)
        cls = carve(NB)
        cls_iota = carve(CLASSES)
        member = carve(CLASSES * NB, BF16)
        before = carve(CLASSES * NB)
        count = carve(CLASSES * NB)
        rank_f = carve(NB)
        rank_i = carve(NB, I32)
        payload = carve(NB * 4, I32).rearrange("p (b c) -> p b c", c=4)
        iota_i = carve(P, I32)
        part_i = carve(1, I32)
        deg_rank = carve(NB)
        bt = carve(16)
        bt_out = carve(2, I32)
        bias_rest = rec_in[0:3].rearrange("p a n -> p (a n)")[:, 0:B_ALL]
        bias_part = carve(B_ALL, BF16)[0:3]
        part_mask = carve(3)[0:3]
        GR = 7
        GC = CLASSES * NB // GR

        t_ld = sem("t_ld")
        t_ld_edges = sem("t_ld_edges")
        t_iota = sem("t_iota")
        t_step = sem("t_step")
        t_oh = sem("t_oh")
        t_hist = sem("t_hist")
        t_histdone = sem("t_histdone")
        t_deg = sem("t_deg")
        t_pre = sem("t_pre")
        t_member = sem("t_member")
        t_grp = sem("t_grp")
        t_grpcopied = sem("t_grpcopied")
        t_rank = sem("t_rank")
        t_scat = sem("t_scat")
        t_nodes = sem("t_nodes")
        t_degr = sem("t_degr")
        t_degT = sem("t_degT")
        t_bt = sem("t_bt")
        t_btst = sem("t_btst")
        t_win = sem("t_win")
        t_winst = [sem(f"t_winst{u}") for u in range(2)]
        t_row = sem("t_row")
        t_w = sem("t_w")

        windows_v = windows.rearrange("(p c t) w -> p c (t w)", p=P, t=HB)

        def bias_load(at, row):
            return bias_rest[:, at:at + D], row.rearrange("(a n) -> a n", a=1).broadcast_to([3, D])

        loads = [
            (w_in, w["L0_gnn_w_in"].rearrange("(c p) n -> p c n", p=P)),
            (w_1[:], w["L0_gnn_w1"][0].rearrange("(c p) n -> p c n", p=P)),
            (w_2[:], w["L0_gnn_w2"][0].rearrange("(c p) n -> p c n", p=P)),
            bias_load(B_IN, w["L0_gnn_b_in"]),
            (query[:], w["L1_gnn_query_emb"].rearrange("(c p) -> p c", p=P)),
            (gamma[:], w["L1_gnn_gamma"].rearrange("(a n) -> a n", a=1).broadcast_to([P, D])),
            (beta[:], w["L1_gnn_beta"].rearrange("(a n) -> a n", a=1).broadcast_to([P, D])),
            (rel[0:TYPES, 0:TYPES], w["L1_gnn_rel_w"]),
            (rel[TYPES:2 * TYPES, TYPES:2 * TYPES], w["L1_gnn_rel_w"]),
        ]
        for l in range(2):
            for c, k in enumerate("qkv"):
                loads.append((w_qkv[l][:, :, c * D:(c + 1) * D],
                              w[f"L0_gnn_w{k}"][l].rearrange("(c p) n -> p c n", p=P)))
                loads.append(bias_load(B_QKV + (3 * l + c) * D, w[f"L0_gnn_b{k}"][l]))
            loads.append((w_o[l][:], w["L0_gnn_wo"][l].rearrange("(c p) n -> p c n", p=P)))
            loads.append(bias_load(B_O + l * D, w["L0_gnn_bo"][l]))
            loads.append(bias_load(B_2 + l * D, w["L0_gnn_b2"][l]))
            loads.append((b_1[:, l, :], w["L0_gnn_b1"][l].rearrange("(c p) -> p c", p=P)))
            for n, s in enumerate("gb"):
                loads.append((ln1[:, l, n, :], w[f"L0_gnn_ln1_{s}"][l].rearrange("(c p) -> p c", p=P)))
                loads.append((ln2[:, l, n, :], w[f"L0_gnn_ln2_{s}"][l].rearrange("(c p) -> p c", p=P)))
        for c, k in enumerate("qkv"):
            loads.append((w_qkv[2][:, :, c * D:(c + 1) * D],
                          w[f"L1_gnn_W{k}"].rearrange("(c p) n -> p c n", p=P)))
            loads.append(bias_load(B_QKV + (6 + c) * D, w[f"L1_gnn_b{k}"]))
        loads.append((w_o[2][:], w["L1_gnn_Wo"].rearrange("(c p) n -> p c n", p=P)))
        loads.append(bias_load(B_O + 2 * D, w["L1_gnn_bo"]))

        with nc.Block() as block:
            @block.sync
            def _(sp):
                sp.dma_start(dst_i, dst.rearrange("(p t) -> p t", p=P)).then_inc(t_ld, 16)
                for n, a in enumerate((src, edge_type_64)):
                    sp.dma_start(edge_i[:, n * EW:(n + 1) * EW],
                                 bass.AP(tensor=a.tensor, offset=0, ap=[[EP, P], [1, EW]])).then_inc(t_ld_edges, 16)
                sp.wait_ge(t_step, 1)
                for to, of in loads:
                    sp.dma_start(to, of, allow_slow_non_contiguous=True).then_inc(t_w, 16)
                with sp.Fori(0, NHB) as i:
                    for u in range(2):
                        sp.wait_ge(t_win, i * 2 + u + 1)
                        sp.dma_start(windows_v[:, bass.ds(i * 2 + u, 1), :].rearrange("p a b -> p (a b)"),
                                     window_sb[u].rearrange("p t w -> p (t w)")).then_inc(t_winst[u], 16)
                sp.wait_ge(t_scat, 16 * NB)
                sp.dma_start(node_rank[:, 0:NB, :], node_table.rearrange("(b p) c -> p b c", p=P)).then_inc(t_nodes, 16)
                sp.wait_ge(t_bt, 1)
                sp.dma_start(block_table, bt_out[0:NB, :]).then_inc(t_btst, 16)
                sp.wait_ge(t_btst, 16)
                sp.dma_start(block_row[:], block_table.rearrange("(a b) c -> a (b c)", a=1)).then_inc(t_row, 16)
                sp.wait_ge(t_row, 16)
                sp.wait_ge(t_w, 16 * len(loads))
                for u in range(2):
                    sp.wait_ge(t_winst[u], 16 * NHB)
                    settle(sp)

            @block.gpsimd
            def _(pool):
                nc.gpsimd.iota(iota_i, pattern=[[1, P]], base=0, channel_multiplier=0).then_inc(t_iota, 1)
                nc.gpsimd.iota(part_i, pattern=[[1, 1]], base=0, channel_multiplier=1).then_inc(t_iota, 1)
                nc.gpsimd.iota(payload[:, :, 0:1], pattern=[[P, NB], [1, 1]], base=0,
                               channel_multiplier=1).then_inc(t_iota, 1)
                pool.wait_ge(t_rank, 1)
                for b in range(NB):
                    pool.indirect_dma_start(node_table, bass.IndirectOffsetOnAxis(ap=rank_i[:, b:b + 1], axis=0),
                                            payload[:, b, :], None).then_inc(t_scat, 16)

            @block.scalar
            def _(act):
                act.wait_ge(t_ld_edges, 32)
                settle(act)
                with act.Fori(0, NHB) as i:
                    for u in range(2):
                        with act.If(i >= 1):
                            act.wait_ge(t_winst[u], 16 * i)
                            settle(act)
                        for n in range(2):
                            at = edge_i[:, bass.ds(n * EW + (i * 2 + u) * HB, 1)]
                            at = bass.AP(tensor=at.tensor, offset=at.offset, ap=[at.ap[0], [1, HB], [1, W]])
                            ins = nc.scalar.copy(window_sb[u][:, :, n * W:(n + 1) * W], at)
                        ins.then_inc(t_win, 1)

            @block.tensor
            def _(pe):
                pe.wait_ge(t_oh, 1)
                nc.tensor.matmul(ps_w[:, 0:NB], ident_b[:], zeros_b[:, 0:NB], start=True, stop=False,
                                 skip_group_check=True)
                with pe.Fori(0, NHB) as i:
                    for u in range(2):
                        pe.wait_ge(t_oh, i * 2 + u + 2)
                        for t in range(HB):
                            mm = nc.tensor.matmul(ps_w[:, 0:NB], oh_lo[u][:, t, :], oh_hi[u][:, t, :], start=False,
                                                  stop=False, skip_group_check=True)
                        mm.then_inc(t_hist, 1)
                pe.wait_ge(t_deg, 1)
                nc.tensor.matmul(ps_big[:, 0, 0:NB], below, deg, start=True, stop=True).then_inc(t_pre, 1)
                nc.tensor.matmul(ps_big[:, 1, 0:NB], ones_f, deg, start=True, stop=True).then_inc(t_pre, 1)
                pe.wait_ge(t_member, 1)
                for g in range(GR):
                    if g >= 1:
                        pe.wait_ge(t_grpcopied, g)
                        settle(pe)
                    pe.matmul(ps_big[:, 0, 0:GC], below_b, member[:, g * GC:(g + 1) * GC], start=True, stop=True)
                    pe.matmul(ps_big[:, 1, 0:GC], ones_b, member[:, g * GC:(g + 1) * GC], start=True,
                              stop=True).then_inc(t_grp, 1)
                pe.wait_ge(t_degr, 1)
                nc.tensor.transpose(ps_t[0:NB, 0, :], deg_rank, ident[:]).then_inc(t_degT, 1)

            @block.vector
            def _(dve):
                step = Steps(dve, t_step)
                step(nc.vector.memset(rel[:], 0.0))
                dve.wait_ge(t_iota, 3)
                step(nc.vector.tensor_copy(iota_f[:], iota_i))
                step(nc.vector.tensor_copy(part_f[:], part_i))
                nc.vector.tensor_copy(iota_b, iota_f[:])
                nc.vector.memset(zeros_b[:], 0.0)
                nc.vector.memset(eps_col[:], EPS)
                nc.vector.memset(window[:], 0)
                nc.vector.memset(node_rank[:, NB:NB + 1, :], 0)
                nc.vector.memset(ones_rows[:], 1.0)
                nc.vector.memset(ones_f, 1.0)
                nc.vector.memset(ones_b, 1.0)
                nc.vector.memset(running, 0.0)
                nc.vector.tensor_scalar(ident[:], iota_f[:], part_f[:], None, ALU.is_equal)
                nc.vector.tensor_scalar(ident_b[:], iota_f[:], part_f[:], None, ALU.is_equal)
                nc.vector.tensor_scalar(below, iota_f[:], part_f[:], None, ALU.is_gt)
                nc.vector.tensor_scalar(below_b, iota_f[:], part_f[:], None, ALU.is_gt)
                nc.vector.tensor_scalar(cls_iota, iota_f[:, 0:CLASSES], -float(CLASSES - 1), None,
                                        ALU.add).then_inc(t_oh, 1)
                dve.wait_ge(t_ld, 16)
                nc.vector.tensor_scalar(lo_i, dst_i, P - 1, None, ALU.bitwise_and)
                step(nc.vector.tensor_scalar(hi_i, dst_i, 7, None, ALU.arith_shift_right))
                nc.vector.tensor_copy(lo_b, lo_i)
                step(nc.vector.tensor_copy(hi_b, hi_i))
                counted = Passed(dve, t_hist)
                with dve.Fori(0, NHB) as i:
                    for u in range(2):
                        with dve.If(i >= 1):
                            counted.wait()
                            settle(dve)
                        at = bass.ds((i * 2 + u) * HB, HB)
                        nc.vector.tensor_tensor(
                            oh_lo[u], iota_b.unsqueeze(1).broadcast_to([P, HB, P]),
                            lo_b[:, at].unsqueeze(2).broadcast_to([P, HB, P]), ALU.is_equal)
                        nc.vector.tensor_tensor(
                            oh_hi[u], iota_b[:, 0:NB].unsqueeze(1).broadcast_to([P, HB, NB]),
                            hi_b[:, at].unsqueeze(2).broadcast_to([P, HB, NB]), ALU.is_equal).then_inc(t_oh, 1)
                dve.wait_ge(t_hist, NHB * 2)
                nc.vector.tensor_copy(deg, ps_w[:, 0:NB]).then_inc(t_deg, 1)
                dve.wait_ge(t_deg, 1)
                dve.wait_ge(t_pre, 2)
                step(nc.vector.tensor_copy(total, ps_big[:, 1, 0:NB]))
                step(nc.vector.tensor_tensor_scan(total_in, total, running[:, 0:NB], 0.0, ALU.add, ALU.add))
                step(nc.vector.tensor_tensor(first, total_in, total, ALU.subtract))
                step(nc.vector.tensor_tensor(first, first, ps_big[:, 0, 0:NB], ALU.add))
                step(nc.vector.tensor_scalar(cls, deg, float(CLASSES - 1), -1.0, ALU.min, ALU.mult))
                member_v = member.rearrange("p (c b) -> p c b", b=NB)
                nc.vector.tensor_tensor(member_v, cls.unsqueeze(1).broadcast_to([P, CLASSES, NB]),
                                        cls_iota.unsqueeze(2).broadcast_to([P, CLASSES, NB]),
                                        ALU.is_equal).then_inc(t_member, 1)
                dve.wait_ge(t_member, 1)
                for g in range(GR):
                    dve.wait_ge(t_grp, g + 1)
                    nc.vector.tensor_copy(before[:, g * GC:(g + 1) * GC], ps_big[:, 0, 0:GC])
                    nc.vector.tensor_copy(count[:, g * GC:(g + 1) * GC], ps_big[:, 1, 0:GC]).then_inc(t_grpcopied, 1)
                dve.wait_ge(t_grpcopied, GR)
                step(nc.vector.tensor_tensor(before, before, count, ALU.subtract))
                step(nc.vector.tensor_tensor_scan(running, count, running, 0.0, ALU.add, ALU.add))
                step(nc.vector.tensor_tensor(before, before, running, ALU.add))
                step(nc.vector.tensor_tensor(before, before, member, ALU.mult))
                step(nc.vector.tensor_reduce(rank_f, before.rearrange("p (c b) -> p b c", b=NB), AX_X, ALU.add))
                nc.vector.tensor_copy(payload[:, :, 1], first)
                nc.vector.tensor_copy(payload[:, :, 2], deg)
                nc.vector.tensor_copy(payload[:, :, 3], deg)
                nc.vector.tensor_copy(rank_i, rank_f).then_inc(t_rank, 1)
                dve.wait_ge(t_w, 16 * len(loads))
                step(nc.vector.tensor_tensor(part_mask, iota_f[0:3, 0:3], part_f[0:3].broadcast_to([3, 3]),
                                             ALU.is_equal))
                for n in range(3):
                    step(nc.vector.tensor_copy(bias_part, bias_rest))
                    step(nc.vector.tensor_tensor(bias_rest, bias_rest, bias_part, ALU.subtract))
                    if n == 0:
                        step(nc.vector.tensor_scalar(bias_parts[:], bias_part, part_mask[:, 0:1], None, ALU.mult))
                    else:
                        step(nc.vector.scalar_tensor_tensor(out=bias_parts[:], in0=bias_part,
                                                            scalar=part_mask[:, n:n + 1], in1=bias_parts[:],
                                                            op0=ALU.mult, op1=ALU.add))
                nc.vector.memset(rec_in[:], 0.0)
                dve.wait_ge(t_nodes, 16)
                step(nc.vector.tensor_copy(deg_rank, node_rank[:, 0:NB, 2]))
                nc.vector.tensor_scalar(has_edge[:], deg_rank, 1.0, None, ALU.min)
                nc.vector.tensor_scalar(no_edge[:], deg_rank, 0.0, None, ALU.is_equal).then_inc(t_degr, 1)
                dve.wait_ge(t_degT, 1)
                b0 = bt[0:NB]
                step(nc.vector.tensor_reduce(b0[:, 0:1], ps_t[0:NB, 0, :], AX_X, ALU.max))

                def ceil_div(to, of, by):
                    step(nc.vector.tensor_scalar(b0[:, 1:2], of, (by - 1) / 2, 1.0 / by, ALU.add, ALU.mult))
                    step(nc.vector.tensor_scalar(b0[:, 1:2], b0[:, 1:2], 8388608.0, None, ALU.add))
                    step(nc.vector.tensor_scalar(b0[:, 1:2], b0[:, 1:2], 8388608.0, None, ALU.subtract))
                    step(nc.vector.tensor_scalar(to, b0[:, 1:2], 1.0, None, ALU.max))

                ceil_div(b0[:, 2:3], b0[:, 0:1], CH)
                ceil_div(b0[:, 3:4], b0[:, 2:3], CPS)
                step(nc.vector.tensor_scalar(b0[:, 4:5], b0[:, 3:4], -1.0, -float(CPS), ALU.add, ALU.mult))
                step(nc.vector.tensor_tensor(b0[:, 4:5], b0[:, 4:5], b0[:, 2:3], ALU.add))
                nc.vector.tensor_copy(bt_out[0:NB, 0:1], b0[:, 4:5])
                nc.vector.tensor_scalar(bt_out[0:NB, 1:2], b0[:, 3:4], 1.0, None, ALU.subtract).then_inc(t_bt, 1)
                step(nc.vector.tensor_scalar(rel_rest[:], rel[:], 0.2, None, ALU.mult))
                for n in range(3):
                    step(nc.vector.tensor_copy(rel_part[:, n, :], rel_rest[:]))
                    step(nc.vector.tensor_tensor(rel_rest[:], rel_rest[:], rel_part[:, n, :], ALU.subtract))
                nc.vector.tensor_scalar(query[:], query[:], 0.1, None, ALU.mult)
                nc.vector.memset(sc[:], 0.0)


        class Blocks:

            def __init__(self, eng):
                self.eng = eng
                self.chunks = eng.alloc_register()
                self.rounds = eng.alloc_register()
                eng.reg_mov(self.chunks, 0)
                eng.reg_mov(self.rounds, 0)

            def next(self, b):
                def word(c, lo, hi):
                    sl = slice(2 * b + c, 2 * b + c + 1) if isinstance(b, int) else bass.ds(2 * b + c, 1)
                    return self.eng.value_load(block_row[0:1, sl], min_val=lo, max_val=hi)
                last, earlier = word(0, 1, CPS), word(1, 0, KMAX)
                before = [self.eng.snap(reg, min_val=0, max_val=most)
                          for reg, most in ((self.chunks, KMAX * CPS), (self.rounds, KMAX))]
                self.eng.reg_add(self.chunks, self.chunks, earlier * CPS + last)
                self.eng.reg_add(self.rounds, self.rounds, earlier + 1)
                return last, before[0], earlier, before[1]

        def round_number(k):
            return nc.s_assert_within(k, 0, KMAX - 1, skip_runtime_bounds_check_because="a block has a round per W edges of its fullest node at most")

        def one(parity):
            return slice(parity, parity + 1) if isinstance(parity, int) else bass.ds(parity, 1)

        def flat(ap):
            return ap.rearrange("p a n -> p (a n)")

        def stats(step, n, of, done):
            settle(nc.vector)
            step(nc.vector.bn_stats(bns[:, n, :], of))
            settle(nc.vector)
            nc.vector.bn_aggr(mv[:, n, :], bns[:, n, :]).then_inc(done, 1)

        def deviation(n, done):
            nc.scalar.activation(sd[:, n:n + 1], mv[:, n, 1:2], ACT.Sqrt, bias=eps_col[:]).then_inc(done, 1)

        def scales(step, n, done):
            step(nc.vector.reciprocal(rs[:, n, 0:1], sd[:, n:n + 1]))
            nc.vector.tensor_scalar(rs[:, n, 1:2], mv[:, n, 0:1], rs[:, n, 0:1], -1.0, ALU.mult,
                                    ALU.mult).then_inc(done, 1)

        def transposes(to, of, done):
            for c in range(KD):
                mm = nc.tensor.transpose(to[:, c, :], of[:, c * P:(c + 1) * P], ident[:])
            mm.then_inc(done, 1)

        def bias(to, at):
            nc.tensor.matmul(to, ones_rows[:], bias_parts[:, at:at + to.shape[-1]], start=True, stop=False)

        def project(to, ofT, wt, at, cols=(0, D)):
            a, z = cols
            bias(to, at + a)
            for c in range(KD):
                mm = nc.tensor.matmul(to, ofT[:, c, :], wt[:, c, a:z], start=False, stop=(c == KD - 1))
            return mm

        def project_qkv(l, ofT, done):
            project(ps_qk, ofT, w_qkv[l], B_QKV + 3 * l * D, (0, 2 * D))
            project(ps_v[:, 0:D], ofT, w_qkv[l], B_QKV + 3 * l * D, (2 * D, 3 * D)).then_inc(done, 1)

        p_xat = sem("p_xat")
        p_x = [sem(f"p_x{u}") for u in range(2)]
        p_wat = sem("p_wat")
        p_win = sem("p_win")
        p_slot = sem("p_slot")
        p_slotst = sem("p_slotst")
        p_round = sem("p_round")
        p_stepa = sem("p_stepa")
        p_stepb = sem("p_stepb")
        p_cur = sem("p_cur")
        p_vara, p_sda, p_rsa, p_xna, p_ta, p_taT = (sem("p_a" + s) for s in ("var", "sd", "rs", "xn", "tp", "ts"))
        p_h = sem("p_h")
        p_varb, p_sdb, p_rsb, p_xnb, p_tb, p_tbT = (sem("p_b" + s) for s in ("var", "sd", "rs", "xn", "tp", "ts"))
        p_qkv = sem("p_qkv")
        p_rec = sem("p_rec")
        p_recst = sem("p_recst")
        p_kvst = [sem(f"p_kvst{u}") for u in range(2)]

        def part(b, a, z):
            return flat(rec_in[:, one(b % RING), a * D:z * D])

        def exists(b):
            return not isinstance(b, int) or 0 <= b < NB

        with nc.Block() as block:
            @block.sync
            def _(sp):
                blocks = Blocks(sp)
                with sp.Fori(0, NB) as b:
                    _, _, earlier, before_b = blocks.next(b)
                    with sp.Fori(0, earlier + 1) as j:
                        k = round_number(before_b + j)
                        sp.wait_ge(p_slot, k + 1)
                        sp.dma_start(slot_index[bass.ds(k, 1)].rearrange("a p w -> p (a w)"),
                                     flat(idx[:, one(k % 2), :])).then_inc(p_slotst, 16)
                        sp.dma_start(slot_meta[bass.ds(k, 1)].rearrange("a p w -> p (a w)"),
                                     flat(meta[:, one(k % 2), :])).then_inc(p_slotst, 16)
                        sp.wait_ge(p_slotst, 32 * (k + 1))
                        settle(sp)

            @block.gpsimd
            def _(pool):
                def gather_x(b):
                    def do(u):
                        pool.indirect_dma_start(
                            rec_in[:, u, 4 * D:5 * D], None, x,
                            bass.IndirectOffsetOnAxis(ap=scatter_to[:, u:u + 1], axis=0),
                            bounds_check=N - 1, oob_is_err=False).then_inc(p_x[u % 2], 16)
                    pool.wait_ge(p_xat, b + 1)
                    settle(pool)
                    pick(pool, b % RING, do, range(RING))

                def scatter_kv(b):
                    def do(u):
                        pool.indirect_dma_start(
                            kv_dram[0], bass.IndirectOffsetOnAxis(ap=scatter_to[:, u:u + 1], axis=0),
                            rec_in[:, u, D:3 * D], None, bounds_check=N - 1,
                            oob_is_err=False).then_inc(p_kvst[u % 2], 16)
                    pool.wait_ge(p_rec, b + 1)
                    settle(pool)
                    pick(pool, b % RING, do, range(RING))

                def gather_windows(k):
                    def do(u):
                        pool.indirect_dma_start(
                            window[:, u, :], None, windows, bass.IndirectOffsetOnAxis(ap=window_at[:, u:u + 1], axis=0),
                            bounds_check=EPAD - 1, oob_is_err=False).then_inc(p_win, 16)
                    pool.wait_ge(p_wat, k + 1)
                    settle(pool)
                    pick(pool, k % 2, do)

                def iteration(b):
                    _, _, earlier, before_b = blocks.next(b)
                    if exists(b + 1):
                        gather_x(b + 1)
                    if exists(b - 2):
                        scatter_kv(b - 2)
                    with pool.Fori(0, earlier + 1) as j:
                        gather_windows(before_b + j + 1)
                    pool.nop()

                blocks = Blocks(pool)
                gather_x(0)
                gather_windows(0)
                iteration(0)
                iteration(1)
                with pool.Fori(2, NB - 1) as b:
                    iteration(b)
                iteration(NB - 1)
                scatter_kv(NB - 2)
                scatter_kv(NB - 1)
                for u in range(2):
                    pool.wait_ge(p_kvst[u], 16 * ((NB + 1 - u) // 2))
                    settle(pool)
                pool.wait_ge(p_win, pool.snap(blocks.rounds, min_val=1) * 16 + 16)
                settle(pool)

            @block.vector
            def _(dve):
                def number_nodes(b):
                    if not isinstance(b, int) or b >= RING:
                        gone = b - RING
                        dve.wait_ge(p_kvst[0], 16 * (gone // 2 + 1))
                        settle(dve)
                        dve.wait_ge(p_kvst[1], 16 * ((gone + 1) // 2))
                        settle(dve)
                        dve.wait_ge(p_recst, 16 * (gone + 1))
                        settle(dve)
                    nc.vector.tensor_copy(scatter_to[:, one(b % RING)],
                                          flat(node_rank[:, one(b), 0:1])).then_inc(p_xat, 1)

                def start_round(k):
                    dve.wait_ge(p_cur, k + 1)
                    nc.vector.tensor_copy(window_at[:, one(k % 2)], flat(round_at[:, one(k % 2), 0:1])).then_inc(p_wat, 1)

                def stats_x(b):
                    dve.wait_ge(p_x[0], 16 * (b // 2 + 1))
                    settle(dve)
                    dve.wait_ge(p_x[1], 16 * ((b + 1) // 2))
                    settle(dve)
                    step = Steps(dve, p_stepa, b * 2)
                    stats(step, 0, part(b, 4, 5), p_vara)
                    return step

                def stats_h(b):
                    step = Steps(dve, p_stepb, b * 3)
                    dve.wait_ge(p_h, b + 1)
                    step(nc.vector.tensor_copy(part(b, 3, 4), ps_w[:, 0:D]))
                    stats(step, 1, part(b, 3, 4), p_varb)
                    return step

                def slots(b, earlier, before_b):
                    with dve.Fori(0, earlier + 1) as j:
                        k = round_number(before_b + j)
                        dve.wait_ge(p_win, 16 * (k + 1))
                        settle(dve)
                        now, then = round_at[:, one(k % 2), :], round_at[:, one((k + 1) % 2), :]
                        with dve.If(j < earlier):
                            nc.vector.tensor_scalar(flat(then[:, :, 0:1]), flat(now[:, :, 0:1]), float(W), None, ALU.add)
                            nc.vector.tensor_scalar(flat(then[:, :, 1:2]), flat(now[:, :, 1:2]), -float(W), None,
                                                    ALU.add).then_inc(p_cur, 1)
                        with dve.Else():
                            nc.vector.tensor_copy(then, node_rank[:, one(b + 1), 1:3]).then_inc(p_cur, 1)
                        start_round(k + 1)
                        settle(dve)
                        with dve.If(k >= 2):
                            stored.wait()
                            settle(dve)
                        m = flat(meta[:, one(k % 2), :])
                        source = flat(window[:, one(k % 2), :])
                        chain = Steps(dve, p_round, k * 3)
                        chain(nc.vector.tensor_scalar(valid[:], iota_f[:, 0:W], flat(now[:, :, 1:2]), None, ALU.is_lt))
                        nc.vector.tensor_copy(m[:, W:2 * W], source[:, W:2 * W])
                        chain(nc.vector.scalar_tensor_tensor(out=index_f[:], in0=source[:, 0:W], scalar=-float(SKIP),
                                                             in1=valid[:], op0=ALU.add, op1=ALU.mult))
                        chain(nc.vector.tensor_scalar(m[:, 0:W], valid[:], 0.5, BIG, ALU.subtract, ALU.mult))
                        nc.vector.tensor_scalar(flat(idx[:, one(k % 2), :]), index_f[:], float(SKIP), None,
                                                ALU.add).then_inc(p_slot, 1)
                        dve.wait_ge(p_slot, k + 1)
                        settle(dve)
                    dve.nop()

                def iteration(b):
                    if exists(b):
                        _, _, earlier, before_b = blocks.next(b)
                        if exists(b + 1):
                            number_nodes(b + 1)
                        step_x = stats_x(b)
                    if exists(b - 1):
                        step_h = stats_h(b - 1)
                    if exists(b):
                        dve.wait_ge(p_sda, b + 1)
                        scales(step_x, 0, p_rsa)
                    if exists(b - 1):
                        dve.wait_ge(p_sdb, b)
                        scales(step_h, 1, p_rsb)
                    if exists(b):
                        slots(b, earlier, before_b)
                        if not isinstance(b, int) or b < 2 * W:
                            nc.vector.tensor_copy(kv[:, one(b), :].rearrange("p a (z d) -> p (a z) d", d=D),
                                                  zeros_b[:].unsqueeze(1).broadcast_to([P, 2, D]))

                stored = Passed(dve, p_slotst, 32)
                blocks = Blocks(dve)
                number_nodes(0)
                nc.vector.tensor_copy(round_at[:, 0:1, :], node_rank[:, 0:1, 1:3]).then_inc(p_cur, 1)
                start_round(0)
                for b in range(RING - 1):
                    iteration(b)
                with dve.Fori(RING - 1, NB - 1) as b:
                    iteration(b)
                iteration(NB - 1)
                iteration(NB)

            @block.scalar
            def _(act):
                def record(b):
                    act.wait_ge(p_qkv, b + 1)
                    nc.scalar.copy(part(b, 0, 2), ps_qk)
                    nc.scalar.copy(part(b, 2, 3), ps_v[:, 0:D]).then_inc(p_rec, 1)
                    act.wait_ge(p_rec, b + 1)
                    if not isinstance(b, int) or b:
                        act.wait_ge(p_recst, 16 * b)
                        settle(act)
                    act.dma_start(rec_dram[0][one(b)].rearrange("a p n -> p (a n)"), part(b, 0, 5)).then_inc(p_recst, 16)

                def iteration(b):
                    if exists(b):
                        act.wait_ge(p_vara, b + 1)
                        deviation(0, p_sda)
                    if exists(b - 1):
                        act.wait_ge(p_varb, b)
                        deviation(1, p_sdb)
                    if exists(b):
                        act.wait_ge(p_rsa, b + 1)
                        nc.scalar.activation(xna[:], part(b, 4, 5), ACT.Relu, scale=rs[:, 0, 0:1],
                                             bias=rs[:, 0, 1:2]).then_inc(p_xna, 1)
                    if exists(b - 1):
                        act.wait_ge(p_rsb, b)
                        nc.scalar.activation(xnb[:], part(b - 1, 3, 4), ACT.Identity, scale=rs[:, 1, 0:1],
                                             bias=rs[:, 1, 1:2]).then_inc(p_xnb, 1)
                    if exists(b):
                        act.wait_ge(p_ta, b + 1)
                        nc.scalar.copy(xnaT[:], ps_t).then_inc(p_taT, 1)
                    if exists(b - 1):
                        act.wait_ge(p_tb, b)
                        for c in range(KD):
                            ins = nc.scalar.activation(xnbT[:, c, :], ps_t2[:, c, :], ACT.Identity,
                                                       scale=ln1[:, 0, 0, c:c + 1], bias=ln1[:, 0, 1, c:c + 1])
                        ins.then_inc(p_tbT, 1)
                        record(b - 1)

                iteration(0)
                iteration(1)
                with act.Fori(2, NB) as b:
                    iteration(b)
                iteration(NB)
                act.wait_ge(p_recst, 16 * NB)
                settle(act)

            @block.tensor
            def _(pe):
                def iteration(b):
                    if exists(b):
                        pe.wait_ge(p_xna, b + 1)
                        transposes(ps_t, xna, p_ta)
                    if exists(b - 1):
                        pe.wait_ge(p_xnb, b)
                        transposes(ps_t2, xnb, p_tb)
                    if exists(b):
                        pe.wait_ge(p_taT, b + 1)
                        project(ps_w[:, 0:D], xnaT, w_in, B_IN).then_inc(p_h, 1)
                    if exists(b - 1):
                        pe.wait_ge(p_tbT, b)
                        if not isinstance(b, int) or b >= 2:
                            pe.wait_ge(p_rec, b - 1)
                            settle(pe)
                        project_qkv(0, xnbT, p_qkv)

                iteration(0)
                iteration(1)
                with pe.Fori(2, NB) as b:
                    iteration(b)
                iteration(NB)


        moved_by_dma = ("idx", "meta", "kv0", "kv1", "rec", "recst", "scat", "wload")
        between = {name: sem(name) for name in (
            "mul", "score", "relk", "to_exp", "exped", "scaled", "weighted", "summed", "acc", "agg", "round", "start",
            "norm", "residual", "second", "scale1", "scale2", "aggT", "aggTs", "w", "var1", "sd1", "var2", "sd2", "rs1", "xn1", "xT1", "xTs1", "f1", "g", "f2", "rs2", "xn2", "xT2", "xTs2", "qkv", "recq", "oh", "ohT", "ohTs", "relp", "outx", "mixed", "last",
            "arrived")}
        numbers = sorted(handle.num for handle in between.values())
        assert numbers[-1] - numbers[0] == len(numbers) - 1
        for l in range(3):
            H = HEADS[l]
            DH = D // H
            scale = 1.0 / float(np.sqrt(DH))
            typed = l == 2
            s = dict(between, **{name: sem(f"l{l}_{name}") for name in moved_by_dma})
            if l:
                with nc.Block() as block:
                    @block.gpsimd
                    def _(pool):
                        pool.sem_clear(range(numbers[0], numbers[-1] + 1))
            kv_sem = [s["kv0"], s["kv1"]]
            scw = sc[:, 0:W * H]
            smw = sm[:, 0:(W + 1) * H]
            exw = ex[:, 0:(W + 1) * H]
            chunks = kv[:].rearrange("p (r s) d -> p r s d", s=CH)

            def last_round(counts):
                last, chunks_before, earlier, rounds_before = counts
                return (round_number(rounds_before + earlier), chunks_before + earlier * CPS, last)

            def iterate(eng, iteration, peeled=DEPTH):
                for b in range(peeled):
                    iteration(b)
                with eng.Fori(peeled, NB) as b:
                    iteration(b)
                for b in range(NB, NB + DEPTH):
                    iteration(b)

            def earlier_rounds(eng, counts, do):
                _, chunks_before, earlier, rounds_before = counts
                with eng.If(earlier > 0):
                    with eng.Fori(0, earlier) as j:
                        do(round_number(rounds_before + j), chunks_before + j * CPS, CPS)
                    eng.nop()

            with nc.Block() as block:
                @block.sync
                def _(sp):
                    if l == 1:
                        sp.dma_start(w_1[:], w["L0_gnn_w1"][1].rearrange("(c p) n -> p c n", p=P)).then_inc(s["wload"], 16)
                        sp.dma_start(w_2[:], w["L0_gnn_w2"][1].rearrange("(c p) n -> p c n", p=P)).then_inc(s["wload"], 16)
                    arrived, scored, done = (Passed(sp, s[name]) for name in ("arrived", "scaled", "recq"))
                    blocks = Blocks(sp)
                    with sp.Fori(0, NB) as b:
                        _, _, earlier, rounds_before = blocks.next(b)
                        with sp.Fori(0, earlier + 1) as j:
                            k = round_number(rounds_before + j)
                            with sp.If(k >= 2):
                                arrived.wait()
                                settle(sp)
                            with sp.If(k >= 1):
                                sp.wait_ge(s["idx"], 16 * k)
                                settle(sp)
                            sp.dma_start(flat(idx[:, one(k % 2), :]),
                                         slot_index[bass.ds(k, 1)].rearrange("a p w -> p (a w)")).then_inc(s["idx"], 16)
                            with sp.If(k >= 2):
                                scored.wait()
                                settle(sp)
                            with sp.If(k >= 1):
                                sp.wait_ge(s["meta"], 16 * k)
                                settle(sp)
                            sp.dma_start(flat(meta[:, one(k % 2), :]),
                                         slot_meta[bass.ds(k, 1)].rearrange("a p w -> p (a w)")).then_inc(s["meta"], 16)
                        with sp.If(b >= RING):
                            done.wait()
                            settle(sp)
                        with sp.If(b >= 1):
                            sp.wait_ge(s["rec"], 16 * b)
                            settle(sp)
                        sp.dma_start(flat(rec_in[:, one(b % RING), :]),
                                     rec_dram[l][bass.ds(b, 1)].rearrange("a p n -> p (a n)")).then_inc(s["rec"], 16)

                @block.gpsimd
                def _(pool):
                    summed, recorded = Passed(pool, s["summed"]), Passed(pool, s["recq"])
                    scattered = Passed(pool, s["scat"], 16)

                    def scatter(par):
                        def do(u):
                            if typed:
                                to, of = out, rec_out[:, u, 0:D]
                            else:
                                to, of = kv_dram[l + 1], rec_out[:, u, D:3 * D]
                            pool.indirect_dma_start(
                                to, bass.IndirectOffsetOnAxis(ap=scatter_to[:, u:u + 1], axis=0), of, None,
                                bounds_check=N - 1, oob_is_err=False).then_inc(s["scat"], 16)
                        recorded.wait()
                        settle(pool)
                        pick(pool, par, do)
                        scattered.wait()
                        settle(pool)

                    def gather_round(u, k, filled):
                        def gather(c):
                            for slot in range(c * CH, (c + 1) * CH):
                                pool.indirect_dma_start(
                                    kv[:, u * W + slot, :], None, kv_dram[l],
                                    bass.IndirectOffsetOnAxis(ap=idx[:, u, slot:slot + 1], axis=0),
                                    bounds_check=N - 1, oob_is_err=False).then_inc(kv_sem[u], 16)
                        gather(0)
                        for c in range(1, CPS):
                            if isinstance(filled, int):
                                gather(c)
                                continue
                            with pool.If(filled > c):
                                gather(c)
                            pool.nop()

                    blocks = Blocks(pool)
                    with pool.Fori(0, NB) as b:
                        counts = blocks.next(b)

                        def gathers(k, _, filled):
                            pool.wait_ge(s["idx"], 16 * (k + 1))
                            settle(pool)
                            with pool.If(k >= 2):
                                summed.wait()
                                settle(pool)
                            pick(pool, k % 2, lambda u: gather_round(u, k, filled))
                        earlier_rounds(pool, counts, gathers)
                        gathers(*last_round(counts))
                        with pool.If(b >= SCATTER_LAG):
                            scatter(b % 2)
                    for b in range(NB - SCATTER_LAG, NB):
                        scatter(b % 2)

                @block.vector
                def _(dve):
                    def rel_onehots(k, chunk0, filled):
                        types = flat(meta[:, one(k % 2), W:2 * W])
                        dve.wait_ge(s["meta"], 16 * (k + 1))
                        settle(dve)
                        with dve.Fori(0, filled) as c:
                            at = types_slice(types, c)
                            nc.vector.tensor_tensor(
                                onehot[:, one(c), :].rearrange("p a (s n) -> p (a s) n", n=TYPES),
                                iota_f[:, 0:TYPES].unsqueeze(1).broadcast_to([P, CH, TYPES]),
                                at.unsqueeze(2).broadcast_to([P, CH, TYPES]), ALU.is_equal).then_inc(s["oh"], 1)
                        dve.nop()

                    def types_slice(types, c):
                        return types[:, bass.ds(c * CH, CH)]

                    def chunk_of(k, c, z):
                        return chunks[:, one((k % 2) * CPS + c), :, z * D:(z + 1) * D].rearrange("p a s d -> p (a s) d")

                    def scores(b, k, chunk0, filled, meanwhile=lambda: None):
                        q = flat(rec_in[:, one(b % RING), 0:D]).unsqueeze(1).broadcast_to([P, CH, D])

                        for u in range(2):
                            dve.reg_add(sent[u], sent[u], ((k + 1 + u) % 2) * (filled * (16 * CH)))
                        for u in range(2):
                            dve.wait_ge(kv_sem[u], dve.snap(sent[u], min_val=0))
                            settle(dve)
                        nc.vector.memset(prod[:, 0:1], 0.0).then_inc(s["arrived"], 1)
                        if not typed:
                            dve.wait_ge(s["meta"], 16 * (k + 1))

                        def add_relation(c):
                            dve.wait_ge(s["relp"], chunk0 + c + 1)
                            at = chunk_of(k, c, 0).rearrange("p s (h d) -> p s h d", h=H)
                            nc.vector.tensor_tensor(
                                at, at, rel_of(chunk0 + c).unsqueeze(2).broadcast_to([P, CH, H, DH]),
                                ALU.add).then_inc(s["relk"], 1)

                        def products(c):
                            if typed:
                                dve.wait_ge(s["relk"], chunk0 + c + 1)
                            at = chunk_of(k, c, 0)
                            nc.vector.tensor_tensor(at, at, q, ALU.mult).then_inc(s["mul"], 1)

                        def head_sums(c):
                            dve.wait_ge(s["mul"], chunk0 + c + 1)
                            if typed:
                                settle(dve)
                            nc.vector.tensor_reduce(
                                scw[:, slice(c * CH * H, (c + 1) * CH * H) if isinstance(c, int) else
                                    bass.ds(c * (CH * H), CH * H)].rearrange("p (s h) -> p s h", h=H),
                                chunk_of(k, c, 0).rearrange("p s (h d) -> p s h d", h=H), AX_X,
                                ALU.add).then_inc(s["score"], 1)

                        if typed:
                            add_relation(0)
                        else:
                            products(0)
                        meanwhile()
                        settle(dve)
                        with dve.If(filled > 1) if not isinstance(filled, int) else nullcontext():
                            with dve.Fori(1, filled) as c:
                                if typed:
                                    products(c - 1)
                                    add_relation(c)
                                else:
                                    products(c)
                                head_sums(c - 1)
                            dve.nop()
                        if typed:
                            products(filled - 1)
                        head_sums(filled - 1)

                    def rel_of(chunk):
                        return ps_rel[:, one(chunk % 2), :].rearrange("p a (s d) -> p (a s) d", d=TYPES)

                    def maxima(step, k, chunk0, filled):
                        dve.wait_ge(s["score"], chunk0 + filled)
                        cap = flat(meta[:, one(k % 2), 0:W]).unsqueeze(2).broadcast_to([P, W, H])
                        nc.vector.tensor_copy(smw[:, W * H:], mrun[:, 0:H])
                        step(nc.vector.tensor_tensor(smw[:, 0:W * H].rearrange("p (s h) -> p s h", h=H),
                                                     scw.rearrange("p (s h) -> p s h", h=H), cap, ALU.min))
                        step(nc.vector.tensor_reduce(mrun[:, 0:H], smw.rearrange("p (s h) -> p h s", h=H), AX_X,
                                                     ALU.max))
                        view = smw.rearrange("p (s h) -> p s h", h=H)
                        nc.vector.tensor_tensor(view, view, mrun[:, 0:H].unsqueeze(1).broadcast_to([P, W + 1, H]),
                                                ALU.subtract).then_inc(s["to_exp"], 1)

                    def rescale(step, b, k):
                        dve.wait_ge(s["exped"], k + 1)
                        dve.wait_ge(s["acc"], k + b + 1)
                        alpha = exw[:, W * H:]
                        step(nc.vector.tensor_tensor(
                            acc_scaled[:].rearrange("p (h d) -> p h d", h=H), acc[:].rearrange("p (h d) -> p h d", h=H),
                            alpha.unsqueeze(2).broadcast_to([P, H, DH]), ALU.mult))
                        step(nc.vector.tensor_tensor(alpha, alpha, zrun[:, 0:H], ALU.mult))
                        nc.vector.tensor_reduce(zrun[:, 0:H], exw.rearrange("p (s h) -> p h s", h=H), AX_X,
                                                ALU.add).then_inc(s["scaled"], 1)

                    def weigh(k, chunk0, filled):
                        with dve.Fori(0, filled) as c:
                            at = chunk_of(k, c, 1).rearrange("p s (h d) -> p s h d", h=H)
                            wt = exw[:, bass.ds(c * (CH * H), CH * H)].rearrange("p (s h) -> p s h", h=H)
                            nc.vector.tensor_tensor(at, at, wt.unsqueeze(3).broadcast_to([P, CH, H, DH]),
                                                    ALU.mult).then_inc(s["weighted"], 1)
                        dve.nop()

                    def start(b):
                        dve.wait_ge(s["rec"], 16 * (b + 1))
                        r = rec_in[:, one(b % RING), :]
                        step = Steps(dve, s["start"], b * (1 if typed else 2))
                        if typed:
                            nc.vector.memset(mrun[:], -1e37)
                            step(nc.vector.memset(zrun[:], 0.0))
                        else:
                            nc.vector.memset(zrun[:], 1.0)
                            step(nc.vector.tensor_tensor(prod[:], flat(r[:, :, 0:D]), flat(r[:, :, D:2 * D]), ALU.mult))
                            step(nc.vector.tensor_reduce(mrun[:, 0:H], prod[:].rearrange("p (h d) -> p h d", h=H),
                                                         AX_X, ALU.add))

                    def weight_sums(b, k):
                        step = Steps(dve, s["norm"], b * 2)
                        dve.wait_ge(s["scaled"], k + 1)
                        if typed:
                            step(nc.vector.tensor_scalar(rz[:, 0:H], zrun[:, 0:H], 1e-30, None, ALU.max))
                            step(nc.vector.reciprocal(rz[:, 0:H], rz[:, 0:H]))
                        else:
                            step(nc.vector.reciprocal(rz[:, 0:H], zrun[:, 0:H]))
                            step(nc.vector.tensor_scalar(rz[:, 0:H], rz[:, 0:H], has_edge[:, one(b)], None, ALU.mult))

                    def finish(b, rounds):
                        dve.wait_ge(s["acc"], rounds + b + 1)
                        ins = nc.vector.tensor_tensor(
                            agg[:].rearrange("p (h d) -> p h d", h=H), acc[:].rearrange("p (h d) -> p h d", h=H),
                            rz[:, 0:H].unsqueeze(2).broadcast_to([P, H, DH]), ALU.mult)
                        if typed:
                            ins.then_inc(s["mixed"], 1)
                            dve.wait_ge(s["mixed"], b + 1)
                            ins = nc.vector.scalar_tensor_tensor(
                                out=agg[:], in0=flat(rec_in[:, one(b % RING), 2 * D:3 * D]), scalar=no_edge[:, one(b)],
                                in1=agg[:], op0=ALU.mult, op1=ALU.add)
                        ins.then_inc(s["agg"], 1)

                    def residual(b):
                        step = Steps(dve, s["residual"], b * 2)
                        dve.wait_ge(s["w"], b + 1)
                        step(nc.vector.tensor_tensor(h1[:], flat(rec_in[:, one(b % RING), 3 * D:4 * D]),
                                                     ps_t2_w[:, D:2 * D],
                                                     ALU.add))
                        stats(step, 0, h1[:], s["var1"])

                    def second(b):
                        step = Steps(dve, s["second"], b * (1 if typed else 2))
                        x_in = flat(rec_in[:, one(b % RING), 4 * D:5 * D])
                        to = rec_out[:, one(b % 2), :]
                        if not isinstance(b, int) or b >= 2:
                            scattered.wait()
                            if not typed:
                                stored.wait()
                            settle(dve)
                        nc.vector.tensor_copy(scatter_to[:, one(b % 2)], flat(node_rank[:, one(b), 0:1]))
                        if typed:
                            dve.wait_ge(s["xn1"], b + 1)
                            step(nc.vector.tensor_tensor(xna[:], xna[:], gamma[:], ALU.mult))
                            nc.vector.tensor_tensor(xnb[:], beta[:], x_in, ALU.add).then_inc(s["outx"], 1)
                            dve.wait_ge(s["outx"], b + 1)
                            nc.vector.tensor_tensor(flat(to[:, :, 0:D]), xna[:], xnb[:], ALU.add).then_inc(s["recq"], 1)
                            return
                        dve.wait_ge(s["f2"], b + 1)
                        if l == 0:
                            h = flat(to[:, :, 3 * D:4 * D])
                            step(nc.vector.tensor_tensor(h, h1[:], ps_w[:, D:2 * D], ALU.add))
                            stats(step, 1, h, s["var2"])
                        else:
                            step(nc.vector.tensor_tensor(h1[:], h1[:], ps_w[:, D:2 * D], ALU.add))
                            x1 = flat(to[:, :, 4 * D:5 * D])
                            nc.vector.tensor_tensor(x1, h1[:], x_in, ALU.add).then_inc(s["outx"], 1)
                            dve.wait_ge(s["outx"], b + 1)
                            stats(step, 1, x1, s["var2"])

                    def scales1(b):
                        dve.wait_ge(s["sd1"], b + 1)
                        scales(Steps(dve, s["scale1"], b), 0, s["rs1"])

                    def scales2(b):
                        dve.wait_ge(s["sd2"], b + 1)
                        scales(Steps(dve, s["scale2"], b), 1, s["rs2"])

                    def iteration(b):
                        def second_part():
                            if exists(b - 2):
                                second(b - 2)
                        if exists(b):
                            counts = blocks.next(b)
                            k, chunk0, filled = last_round(counts)
                            start(b)

                            def finish_last():
                                if exists(b - 1):
                                    finish(b - 1, counts[3])

                            def whole(k, chunk0, filled):
                                extra = Steps(dve, s["round"], dve.snap(extras, min_val=0))
                                if typed:
                                    rel_onehots(k, chunk0, filled)
                                scores(b, k, chunk0, filled)
                                maxima(extra, k, chunk0, filled)
                                rescale(extra, b, k)
                                weigh(k, chunk0, filled)
                                dve.reg_add(extras, extras, 4)

                            late = exists(b - 1) and not typed
                            earlier = counts[2]
                            if late:
                                settle(dve)
                                with dve.If(earlier > 0):
                                    finish_last()
                            elif exists(b - 1):
                                finish_last()
                            settle(dve)
                            earlier_rounds(dve, counts, whole)
                            last = Steps(dve, s["last"], b * 4)
                            if typed:
                                rel_onehots(k, chunk0, filled)

                            def finish_late():
                                settle(dve)
                                with dve.If(earlier == 0):
                                    finish_last()
                            scores(b, k, chunk0, filled, finish_late if late else lambda: None)
                            second_part()
                            maxima(last, k, chunk0, filled)
                        else:
                            if exists(b - 1):
                                finish(b - 1, dve.snap(blocks.rounds, min_val=1))
                            second_part()
                        if exists(b - 1):
                            residual(b - 1)
                        if exists(b):
                            rescale(last, b, k)
                        if exists(b - 2) and not typed:
                            scales2(b - 2)
                        if exists(b - 1):
                            scales1(b - 1)
                        if exists(b):
                            weigh(k, chunk0, filled)
                            weight_sums(b, k)

                    sent = [dve.alloc_register(f"l{l}_sent{u}") for u in range(2)]
                    extras = dve.alloc_register(f"l{l}_extras")
                    for reg in (*sent, extras):
                        dve.reg_mov(reg, 0)
                    scattered, stored = Passed(dve, s["scat"], 16), Passed(dve, s["recst"], 16)
                    blocks = Blocks(dve)
                    iterate(dve, iteration, DEPTH + 1)

                @block.scalar
                def _(act):
                    def sum_out(k):
                        act.wait_ge(s["summed"], k + 1)
                        nc.scalar.copy(acc[:], ps_acc[:, 0:D]).then_inc(s["acc"], 1)

                    def turn_sums(b):
                        act.wait_ge(s["aggT"], b + 1)
                        nc.scalar.copy(aggT[:], ps_t).then_inc(s["aggTs"], 1)

                    def exp_round(k):
                        act.wait_ge(s["to_exp"], k + 1)
                        nc.scalar.activation(exw, smw, ACT.Exp, scale=scale).then_inc(s["exped"], 1)

                    def onehots(chunk0, filled):
                        with act.Fori(0, filled) as c:
                            act.wait_ge(s["ohT"], chunk0 + c + 1)
                            nc.scalar.copy(onehotT, ps_oh).then_inc(s["ohTs"], 1)
                        act.nop()

                    def start(b):
                        act.wait_ge(s["rec"], 16 * (b + 1))
                        if not isinstance(b, int) or b:
                            act.wait_ge(s["agg"], b)
                            settle(act)
                        if typed:
                            nc.scalar.copy(acc[:], zeros_b[:]).then_inc(s["acc"], 1)
                        else:
                            nc.scalar.copy(acc[:], flat(rec_in[:, one(b % RING), 2 * D:3 * D])).then_inc(s["acc"], 1)

                    def feed_forward(b):
                        act.wait_ge(s["xT1"], b + 1)
                        for c in range(KD):
                            ins = nc.scalar.activation(xnaT[:, c, :], ps_t[:, c, :], ACT.Identity,
                                                       scale=ln2[:, l, 0, c:c + 1], bias=ln2[:, l, 1, c:c + 1])
                        ins.then_inc(s["xTs1"], 1)

                    def hidden(b):
                        for f in range(KF):
                            act.wait_ge(s["f1"], b * 2 + f // 4 + 1)
                            nc.scalar.activation(gT[:, f, :], ps_big[:, f // 4, (f % 4) * P:(f % 4 + 1) * P], ACT.Gelu,
                                                 bias=b_1[:, l, f:f + 1]).then_inc(s["g"], 1)

                    def normed1(b):
                        act.wait_ge(s["rs1"], b + 1)
                        nc.scalar.activation(xna[:], h1[:], ACT.Identity, scale=rs[:, 0, 0:1],
                                             bias=rs[:, 0, 1:2]).then_inc(s["xn1"], 1)

                    def normed2(b):
                        to = rec_out[:, one(b % 2), :]
                        act.wait_ge(s["rs2"], b + 1)
                        if l == 0:
                            nc.scalar.activation(xnb[:], flat(to[:, :, 3 * D:4 * D]), ACT.Identity,
                                                 scale=rs[:, 1, 0:1], bias=rs[:, 1, 1:2]).then_inc(s["xn2"], 1)
                            nc.scalar.copy(flat(to[:, :, 4 * D:5 * D]), flat(rec_in[:, one(b % RING), 4 * D:5 * D]))
                        else:
                            nc.scalar.activation(xnb[:], flat(to[:, :, 4 * D:5 * D]), ACT.Relu,
                                                 scale=rs[:, 1, 0:1], bias=rs[:, 1, 1:2]).then_inc(s["xn2"], 1)
                            act.wait_ge(s["xn2"], b + 1)
                            nc.scalar.copy(flat(to[:, :, 3 * D:4 * D]), xnb[:])

                    def turn_normed(b):
                        act.wait_ge(s["xT2"], b + 1)
                        for c in range(KD):
                            if l == 0:
                                ins = nc.scalar.activation(xnbT[:, c, :], ps_t2[:, c, :], ACT.Identity,
                                                           scale=ln1[:, 1, 0, c:c + 1], bias=ln1[:, 1, 1, c:c + 1])
                            else:
                                ins = nc.scalar.activation(xnbT[:, c, :], ps_t2[:, c, :], ACT.Identity,
                                                           bias=query[:, c:c + 1])
                        ins.then_inc(s["xTs2"], 1)

                    def record(b):
                        to = rec_out[:, one(b % 2), :]
                        act.wait_ge(s["qkv"], b + 1)
                        nc.scalar.copy(flat(to[:, :, 0:2 * D]), ps_qk)
                        nc.scalar.copy(flat(to[:, :, 2 * D:3 * D]), ps_v[:, 0:D]).then_inc(s["recq"], 1)
                        act.wait_ge(s["recq"], b + 1)
                        if not isinstance(b, int) or b:
                            act.wait_ge(s["recst"], 16 * b)
                            settle(act)
                        act.dma_start(rec_dram[l + 1][one(b)].rearrange("a p n -> p (a n)"),
                                      flat(to)).then_inc(s["recst"], 16)

                    def iteration(b):
                        if exists(b - 2) and not typed:
                            feed_forward(b - 2)
                        if exists(b - 3) and not typed:
                            turn_normed(b - 3)
                        if exists(b - 2) and not typed:
                            hidden(b - 2)
                        if exists(b):
                            counts = blocks.next(b)
                            k, chunk0, filled = last_round(counts)
                            start(b)
                        if exists(b - 1):
                            turn_sums(b - 1)
                        if exists(b):
                            def whole(k, chunk0, filled):
                                if typed:
                                    onehots(chunk0, filled)
                                exp_round(k)
                                sum_out(k)
                            earlier_rounds(act, counts, whole)
                            if typed:
                                onehots(chunk0, filled)
                            exp_round(k)
                        if exists(b - 2) and not typed:
                            act.wait_ge(s["var2"], b - 1)
                            deviation(1, s["sd2"])
                        if exists(b - 1):
                            act.wait_ge(s["var1"], b)
                            deviation(0, s["sd1"])
                        if exists(b - 2) and not typed:
                            normed2(b - 2)
                        if exists(b - 1):
                            normed1(b - 1)
                        if exists(b - 3) and not typed:
                            record(b - 3)
                        if exists(b):
                            sum_out(k)

                    blocks = Blocks(act)
                    iterate(act, iteration)
                    if not typed:
                        act.wait_ge(s["recst"], 16 * NB)
                        settle(act)

                @block.tensor
                def _(pe):
                    def sums(k, chunk0, filled):
                        pe.wait_ge(s["scaled"], k + 1)
                        nc.tensor.matmul(ps_acc[:, 0:D], ident[:], acc_scaled[:], start=True, stop=False,
                                         skip_group_check=True)
                        with pe.Fori(0, filled) as c:
                            pe.wait_ge(s["weighted"], chunk0 + c + 1)
                            at = chunks[:, one((k % 2) * CPS + c), :, D:2 * D]
                            for slot in range(CH):
                                nc.tensor.matmul(ps_acc[:, 0:D], ident[:], at[:, :, slot, :].rearrange(
                                    "p a d -> p (a d)"), start=False, stop=False, skip_group_check=True)
                        nc.tensor.matmul(ps_acc[:, 0:32], ident_b[:], zeros_b[:, 0:32], start=False, stop=True,
                                         skip_group_check=True).then_inc(s["summed"], 1)

                    def relations(chunk0, filled):
                        with pe.Fori(0, filled) as c:
                            n = chunk0 + c
                            pe.wait_ge(s["oh"], n + 1)
                            for pair in range(2):
                                mm = nc.tensor.transpose(ps_oh[:, pair, :],
                                                         flat(onehot[:, one(c), pair * P:(pair + 1) * P]), ident_b[:])
                            mm.then_inc(s["ohT"], 1)
                            pe.wait_ge(s["ohTs"], n + 1)
                            settle(pe)
                            with pe.If(n >= 2):
                                read.wait()
                                settle(pe)
                            for pair in range(2):
                                for part in range(3):
                                    mm = nc.tensor.matmul(
                                        flat(ps_rel[:, one(n % 2), pair * P:(pair + 1) * P]), onehotT[:, pair, :],
                                        rel_part[:, part, :], start=(part == 0), stop=(part == 2))
                            mm.then_inc(s["relp"], 1)
                        pe.nop()

                    def turn_sums(b):
                        pe.wait_ge(s["agg"], b + 1)
                        transposes(ps_t, agg, s["aggT"])

                    def project_sums(b):
                        pe.wait_ge(s["aggTs"], b + 1)
                        project(ps_t2_w[:, D:2 * D], aggT, w_o[l], B_O + l * D).then_inc(s["w"], 1)

                    def turn_hidden(b):
                        pe.wait_ge(s["xn1"], b + 1)
                        transposes(ps_t, xna, s["xT1"])

                    def feed_forward(b):
                        pe.wait_ge(s["xTs1"], b + 1)
                        if l == 1:
                            pe.wait_ge(s["wload"], 32)
                            settle(pe)
                        for f in range(KF):
                            to = ps_big[:, f // 4, (f % 4) * P:(f % 4 + 1) * P]
                            for c in range(KD):
                                mm = nc.tensor.matmul(to, w_1[:, c, f * P:(f + 1) * P], xnaT[:, c, :],
                                                      start=(c == 0), stop=(c == KD - 1))
                            if f % 4 == 3:
                                mm.then_inc(s["f1"], 1)

                    def feed_out(b):
                        to = ps_w[:, D:2 * D]
                        bias(to, B_2 + l * D)
                        for f in range(KF):
                            pe.wait_ge(s["g"], b * KF + f + 1)
                            mm = nc.tensor.matmul(to, gT[:, f, :], w_2[:, f, :], start=False, stop=(f == KF - 1))
                        mm.then_inc(s["f2"], 1)

                    def turn_normed(b):
                        pe.wait_ge(s["xn2"], b + 1)
                        transposes(ps_t2, xnb, s["xT2"])

                    def next_qkv(b):
                        pe.wait_ge(s["xTs2"], b + 1)
                        if not isinstance(b, int) or b:
                            pe.wait_ge(s["recq"], b)
                            settle(pe)
                        project_qkv(l + 1, xnbT, s["qkv"])

                    def iteration(b):
                        if exists(b - 2) and not typed:
                            turn_hidden(b - 2)
                        if exists(b - 3) and not typed:
                            turn_normed(b - 3)
                        if exists(b - 2) and not typed:
                            feed_forward(b - 2)
                        if exists(b - 1):
                            turn_sums(b - 1)
                        if exists(b - 2) and not typed:
                            feed_out(b - 2)
                        if exists(b - 3) and not typed:
                            pe.wait_ge(s["xTs2"], b - 2)
                            settle(pe)
                        if exists(b - 1):
                            project_sums(b - 1)
                        if exists(b - 3) and not typed:
                            next_qkv(b - 3)
                        if exists(b):
                            counts = blocks.next(b)
                            k, chunk0, filled = last_round(counts)

                            def whole(k, chunk0, filled):
                                if typed:
                                    relations(chunk0, filled)
                                sums(k, chunk0, filled)
                            earlier_rounds(pe, counts, whole)
                            if typed:
                                relations(chunk0, filled)
                            sums(k, chunk0, filled)

                    if typed:
                        read = Passed(pe, s["relk"])
                    blocks = Blocks(pe)
                    iterate(pe, iteration)

        return locals()


_WEIGHTS = [
    "L0_gnn_w_in", "L0_gnn_b_in", "L0_gnn_ln1_g", "L0_gnn_ln1_b", "L0_gnn_ln2_g", "L0_gnn_ln2_b", "L0_gnn_wq",
    "L0_gnn_bq", "L0_gnn_wk", "L0_gnn_bk", "L0_gnn_wv", "L0_gnn_bv", "L0_gnn_wo", "L0_gnn_bo", "L0_gnn_w1",
    "L0_gnn_b1", "L0_gnn_w2", "L0_gnn_b2", "L1_gnn_query_emb", "L1_gnn_Wq", "L1_gnn_bq", "L1_gnn_Wk", "L1_gnn_bk",
    "L1_gnn_Wv", "L1_gnn_bv", "L1_gnn_rel_w", "L1_gnn_Wo", "L1_gnn_bo", "L1_gnn_gamma", "L1_gnn_beta",
]


def kernel(**inputs):
    import concourse.bacc as bacc
    from concourse.bass_utils import run_bass_kernel_spmd

    nc = bacc.Bacc("TRN2", target_bir_lowering=False, num_devices=1)
    arrays, aps = {}, {}

    def give(name, a):
        arrays[f"in_{name}"] = a
        aps[name] = nc.dram_tensor(f"in_{name}", a.shape, mybir.dt.from_np(a.dtype), kind="ExternalInput").ap()

    def padded(a, size, fill):
        out = np.full((size,), fill, a.dtype)
        out[:a.shape[0]] = a
        return out

    give("x", np.ascontiguousarray(inputs["x"]))
    give("src", padded(np.asarray(inputs["src"]), EPAD + W, 0))
    give("dst", padded(np.asarray(inputs["dst"]), EPAD, NPAD))
    give("edge_type_64", padded(np.asarray(inputs["edge_type_64"]), EPAD + W, 0))
    for name in _WEIGHTS:
        give(name, np.ascontiguousarray(inputs[name]))
    out = nc.dram_tensor("out", (N, D), F32, kind="ExternalOutput").ap()
    build(nc, aps["x"], aps["src"], aps["dst"], aps["edge_type_64"], aps, out)
    r = run_bass_kernel_spmd(nc, [arrays], core_ids=[0])
    return r.results[0]["out"]
```
